# Optimizing a Trainium2 kernel written in Bass

```python
import numpy as np
import jax
import jax.numpy as jnp

def _softmax(x, axis=-1):
    return jax.nn.softmax(x, axis=axis)

def _gelu(x):
    return jax.nn.gelu(x, approximate=True)

def _silu(x):
    return jax.nn.silu(x)

def _sigmoid(x):
    return jax.nn.sigmoid(x)

def _layernorm(x, axis=-1, eps=1e-05):
    m = jnp.mean(x, axis=axis, keepdims=True)
    v = jnp.var(x, axis=axis, keepdims=True)
    return (x - m) / jnp.sqrt(v + eps)

def _scatter_add(tgt, idx, src, axis=0):
    return tgt.at[idx].add(src)

def _segment_sum(src, seg, n):
    return jax.ops.segment_sum(src, seg, n)
kernel_name = 'mk_gnn_resnorm_d2_gnn_r8_37206a'

def setup_inputs(seed: int=0):
    np.random.seed(seed)
    _w = jnp.asarray

    def _rec_inputs():
        import jax
        import jax.numpy as jnp
        _gk = jax.random.key(seed)
        x = -0.000202 + 1 * jax.random.normal(jax.random.fold_in(_gk, 1), (12500, 128), jnp.float32)
        _s = jax.random.randint(jax.random.fold_in(_gk, 2), (200000,), 0, 12500, jnp.int32)
        _d = jax.random.randint(jax.random.fold_in(_gk, 3), (200000,), 0, 12500, jnp.int32)
        _loop = jnp.arange(12500, dtype=jnp.int32)
        src = jnp.concatenate([_s, _d, _loop])
        dst = jnp.concatenate([_d, _s, _loop])
        _o = jnp.argsort(dst, stable=True)
        src = src[_o]
        dst = dst[_o]
        edge_attr_50 = 0.000152336 + 1.00009 * jax.random.normal(jax.random.fold_in(_gk, 11), (412500, 50), jnp.float32)
        edge_weight = jax.random.uniform(jax.random.fold_in(_gk, 14), (412500,), jnp.float32, 0.0, 9.99998)
        return (x, src, dst, edge_attr_50, edge_weight)
    x, src, dst, edge_attr_50, edge_weight = _rec_inputs()

    def _L0_gnn_setup():
        import jax, jax.numpy as jnp
        import numpy as np
        N_NODES = 6250
        N_EDGES = 100000
        D_FEAT = 128
        UNITS = 128
        key = jax.random.key(seed)
        k1, k2, k3, k4, k5 = jax.random.split(key, 5)
        node_states = jax.random.normal(k1, (N_NODES, D_FEAT), dtype=jnp.float32)
        src = jnp.sort(jax.random.randint(k2, (N_EDGES,), 0, N_NODES))
        dst = jax.random.randint(k3, (N_EDGES,), 0, N_NODES)
        edges = jnp.stack([src, dst], axis=1).astype(jnp.int64)
        kernel = jax.random.normal(k4, (D_FEAT, UNITS), dtype=jnp.float32) * (1.0 / np.sqrt(D_FEAT))
        kernel_attention = jax.random.normal(k5, (2 * UNITS, 1), dtype=jnp.float32) * (1.0 / np.sqrt(2 * UNITS))
        return {'node_states': node_states, 'edges': edges, 'kernel': kernel, 'kernel_attention': kernel_attention}
    _L0_gnn_all = _L0_gnn_setup()
    _L0_gnn_in = {k: v for k, v in _L0_gnn_all.items() if k in ('kernel', 'kernel_attention')}
    del _L0_gnn_all

    def _L1_gnn_setup():
        import jax, jax.numpy as jnp
        import numpy as np
        N_NODES = 5000
        N_EDGES = 80000
        HIDDEN = 128
        NUM_RBF = 50
        CUTOFF = 10.0
        key = jax.random.key(seed)
        ks = jax.random.split(key, 8)
        s = 1.0 / np.sqrt(HIDDEN)
        sf = 1.0 / np.sqrt(NUM_RBF)
        return {'x': jax.random.normal(ks[0], (N_NODES, HIDDEN), dtype=jnp.float32), 'edge_index': jax.random.randint(ks[1], (2, N_EDGES), 0, N_NODES, dtype=jnp.int64), 'edge_weight': jax.random.uniform(ks[2], (N_EDGES,), dtype=jnp.float32) * CUTOFF, 'edge_attr': jax.random.normal(ks[3], (N_EDGES, NUM_RBF), dtype=jnp.float32), 'W_f1': jax.random.normal(ks[4], (NUM_RBF, HIDDEN), dtype=jnp.float32) * sf, 'b_f1': jnp.zeros((HIDDEN,), dtype=jnp.float32), 'W_f2': jax.random.normal(ks[5], (HIDDEN, HIDDEN), dtype=jnp.float32) * s, 'b_f2': jnp.zeros((HIDDEN,), dtype=jnp.float32), 'W_in': jax.random.normal(ks[6], (HIDDEN, HIDDEN), dtype=jnp.float32) * s, 'W_out': jax.random.normal(ks[7], (HIDDEN, HIDDEN), dtype=jnp.float32) * s, 'b_out': jnp.zeros((HIDDEN,), dtype=jnp.float32), 'W_lin': jax.random.normal(jax.random.fold_in(key, 7), (HIDDEN, HIDDEN), dtype=jnp.float32) * s, 'b_lin': jnp.zeros((HIDDEN,), dtype=jnp.float32)}
    _L1_gnn_all = _L1_gnn_setup()
    _L1_gnn_in = {k: v for k, v in _L1_gnn_all.items() if k in ('W_f1', 'b_f1', 'W_f2', 'b_f2', 'W_in', 'W_out', 'b_out', 'W_lin', 'b_lin')}
    del _L1_gnn_all
    return {'x': x, 'src': src, 'dst': dst, 'edge_attr_50': edge_attr_50, 'edge_weight': edge_weight, 'L0_gnn_kernel': _L0_gnn_in['kernel'], 'L0_gnn_kernel_attention': _L0_gnn_in['kernel_attention'], 'L1_gnn_W_f1': _L1_gnn_in['W_f1'], 'L1_gnn_b_f1': _L1_gnn_in['b_f1'], 'L1_gnn_W_f2': _L1_gnn_in['W_f2'], 'L1_gnn_b_f2': _L1_gnn_in['b_f2'], 'L1_gnn_W_in': _L1_gnn_in['W_in'], 'L1_gnn_W_out': _L1_gnn_in['W_out'], 'L1_gnn_b_out': _L1_gnn_in['b_out'], 'L1_gnn_W_lin': _L1_gnn_in['W_lin'], 'L1_gnn_b_lin': _L1_gnn_in['b_lin']}

def reference(x, src, dst, edge_attr_50, edge_weight, L0_gnn_kernel, L0_gnn_kernel_attention, L1_gnn_W_f1, L1_gnn_b_f1, L1_gnn_W_f2, L1_gnn_b_f2, L1_gnn_W_in, L1_gnn_W_out, L1_gnn_b_out, L1_gnn_W_lin, L1_gnn_b_lin):
    import jax
    import jax.numpy as jnp

    def _L0_gnn_ref(node_states, edges, kernel, kernel_attention):
        import jax, jax.numpy as jnp
        import numpy as np
        N_NODES = 6250
        N_EDGES = 100000
        D_FEAT = 128
        UNITS = 128
        n_nodes = node_states.shape[0]
        src, dst = (edges[:, 0], edges[:, 1])
        h = node_states @ kernel
        e_feat = jnp.concatenate([h[src], h[dst]], axis=-1)
        logits = jax.nn.leaky_relu((e_feat @ kernel_attention)[:, 0], negative_slope=0.2)
        scores = jnp.exp(jnp.clip(logits, -2.0, 2.0))
        denom = jax.ops.segment_sum(scores, src, num_segments=n_nodes)
        alpha = scores / denom[src]
        out = jax.ops.segment_sum(h[dst] * alpha[:, None], src, num_segments=n_nodes)
        return out

    def _L1_gnn_ref(x, edge_index, edge_weight, edge_attr, W_f1, b_f1, W_f2, b_f2, W_in, W_out, b_out, W_lin, b_lin):
        import jax, jax.numpy as jnp
        import numpy as np
        N_NODES = 5000
        N_EDGES = 80000
        HIDDEN = 128
        NUM_RBF = 50
        CUTOFF = 10.0
        src = edge_index[0]
        dst = edge_index[1]
        n_nodes = x.shape[0]
        C = 0.5 * (jnp.cos(edge_weight * (jnp.pi / CUTOFF)) + 1.0)
        Wf = jnp.tanh(edge_attr @ W_f1 + b_f1) @ W_f2 + b_f2
        Wf = Wf * C[:, None]
        h = x @ W_in
        msg = h[src] * Wf
        agg = jax.ops.segment_sum(msg, dst, num_segments=n_nodes)
        out = agg @ W_out + b_out
        out = jnp.tanh(out)
        return out @ W_lin + b_lin
    edge_index = jnp.stack([src, dst])
    edge_index_t = jnp.stack([src, dst], axis=1)
    x = _layernorm(x + _L0_gnn_ref(x, edge_index_t, L0_gnn_kernel, L0_gnn_kernel_attention), axis=-1)
    x = _layernorm(x + _L1_gnn_ref(x, edge_index, edge_weight, edge_attr_50, L1_gnn_W_f1, L1_gnn_b_f1, L1_gnn_W_f2, L1_gnn_b_f2, L1_gnn_W_in, L1_gnn_W_out, L1_gnn_b_out, L1_gnn_W_lin, L1_gnn_b_lin), axis=-1)
    return x

_drawn_inputs = setup_inputs


def setup_inputs(seed=0):
    import zlib

    import numpy as np

    out = dict(_drawn_inputs(seed))
    spreads = {'L1_gnn_b_f1': (0.0, 0.1),
     'L1_gnn_b_f2': (0.0, 0.1),
     'L1_gnn_b_out': (0.0, 0.1),
     'L1_gnn_b_lin': (0.0, 0.1)}
    factors = {}
    for name, (base, spread) in spreads.items():
        noise = np.random.default_rng([zlib.crc32(name.encode()), seed]).standard_normal(out[name].shape)
        drawn = base * np.exp(spread * noise) if base else spread * noise
        out[name] = jnp.asarray(drawn.astype(out[name].dtype))
    for name, factor in factors.items():
        out[name] = (out[name] * factor).astype(out[name].dtype)
    return out
```

```python
import concourse.bass as bass
from concourse import mybir
from contextlib import ExitStack

FP32 = mybir.dt.float32
BF16 = mybir.dt.bfloat16
I32 = mybir.dt.int32
ALU = mybir.AluOpType
ACT = mybir.ActivationFunctionType

P = 128
D = 128
N_NODES = 12500
N_EDGES = 412500
RBF = 50
RBF_ROWS = 64
TS = 8
NODE_BLOCKS = -(-N_NODES // P)
NB = 7
NODE_STEPS = NODE_BLOCKS // NB
NODES_P = NODE_BLOCKS * P
STEPS = -(-N_EDGES // (P * TS))
STEPS += STEPS % 2
TILES = STEPS * TS
EDGES_P = TILES * P
HW = 132
U_COL, V_COL, ONE_COL = 128, 129, 130
COPIES = 4
ROWS = NODES_P + P
EPS = 1e-5
CUTOFF = 10.0
PI = 3.141592653589793
ROUND = 12582912.0


class Tally:

    def __init__(self, sem, per):
        self.sem, self.per, self.n, self.it = sem, per, 0, 0

    def start(self, it):
        self.it, self.n = it, 0

    def inc(self, instruction):
        self.n += 1
        instruction.then_inc(self.sem, 1)

    def wait(self, engine):
        engine.wait_ge(self.sem, self.it * self.per + self.n)

    def end(self):
        assert self.n == self.per, (self.n, self.per)


def gate(pool, c, sem, value):
    pool.wait_ge(sem, value)
    pool.sem_inc(c["gates_passed"], 1)


def constants(nc, ctx):
    c = {"gates_passed": ctx.enter_context(nc.semaphore("gates_passed"))}
    for name, shape, dt in (("ident", [P, P], FP32), ("ident_lo", [P, P], BF16), ("ident_hi", [P, P], BF16),
                            ("later", [P, P], FP32), ("spare_row", [P, 1], FP32), ("eps", [P, 1], FP32),
                            ("half_pi", [P, 1], FP32)):
        c[name] = ctx.enter_context(nc.sbuf_tensor(name, shape, dt))
    with nc.semaphore("const_filled") as filled, nc.Block() as block:
        @block.gpsimd
        def _(pool):
            pool.memset(c["ident"][:], 0.0)
            pool.memset(c["ident_lo"][:], 0.0)
            pool.memset(c["ident_hi"][:], 0.0)
            pool.memset(c["later"][:], 1.0)
            pool.memset(c["eps"][:], EPS)
            pool.memset(c["half_pi"][:], PI / 2)
            pool.iota(c["spare_row"][:], [[0, 1]], base=NODES_P, channel_multiplier=1,
                      allow_small_or_imprecise_dtypes=True).then_inc(filled, 1)
            pool.wait_ge(filled, 1)
            for name, one in (("ident", 1.0), ("ident_lo", 1.0), ("ident_hi", 128.0)):
                pool.affine_select(out=c[name][:], in_=c[name][:], pattern=[[-1, P]],
                                   compare_op=ALU.not_equal, fill=one, base=0, channel_multiplier=1)
            pool.affine_select(out=c["later"][:], in_=c["later"][:], pattern=[[1, P]],
                               compare_op=ALU.is_ge, fill=0.0, base=0, channel_multiplier=-1).then_inc(filled, 1)
    return c


def zero_tables(nc, tables, width, landed):
    rows = ROWS // P
    with nc.sbuf_tensor(f"zeros{width}", [P, width], FP32) as zeros, nc.semaphore(f"zeros{width}_set") as zeros_set, \
            nc.Block() as block:
        @block.vector
        def _(dve):
            nc.vector.memset(zeros[:], 0.0).then_inc(zeros_set, 1)

        @block.gpsimd
        def _(pool):
            pool.wait_ge(zeros_set, 1)
            for k, table in enumerate(tables):
                pool.dma_start(table[:, :].rearrange("(p r) c -> p r c", p=P),
                               zeros[:].unsqueeze(1).to_broadcast([P, rows, width])).then_inc(landed[k], 16)
            for k in range(len(tables)):
                pool.wait_ge(landed[k], 16)


def node_rows(table, step, width):
    return table[bass.ds(step * (NB * P), NB * P), :].rearrange("(b p) c -> p b c", p=P)


def project_nodes(nc, c, xT, kernel, kernelT, att, hv):
    with ExitStack() as ctx:
        sb = lambda n, s, d=FP32: ctx.enter_context(nc.sbuf_tensor("pr_" + n, s, d))
        sem = lambda n: ctx.enter_context(nc.semaphore("pr_" + n))
        kw = sb("kw", [P, D + 2])
        kT = sb("kT", [P, D])
        att_sb = sb("att_sb", [P, 2])
        xt = [sb(f"xt{q}", [P, NB * P]) for q in range(2)]
        rows = [sb(f"hv_rows{q}", [P, NB, HW]) for q in range(2)]
        ps_a = ctx.enter_context(nc.psum_tensor("pr_ps_a", [P, 512], FP32))
        ps = [ctx.enter_context(nc.psum_tensor(f"pr_ps_h{q}", [P, 3, 512], FP32)) for q in range(2)]
        weights_in, ka_ready, kw_ready = sem("weights_in"), sem("ka_ready"), sem("kw_ready")
        xt_in = [sem(f"xt_in{q}") for q in range(2)]
        h_ready = [sem(f"h_ready{q}") for q in range(2)]
        rows_ready = [sem(f"rows_ready{q}") for q in range(2)]
        stored = [sem(f"hv_stored{q}") for q in range(2)]
        block = ctx.enter_context(nc.Block())

        @block.sync
        def _(sp):
            sp.dma_start(kw[:, 0:D], kernel).then_inc(weights_in, 16)
            sp.dma_start(kT[:], kernelT).then_inc(weights_in, 16)
            sp.dma_start(att_sb[:], att).then_inc(weights_in, 16)
            with sp.Fori(0, NODE_STEPS // 2) as it:
                for q in range(2):
                    sp.wait_ge(h_ready[q], it)
                    sp.dma_start(xt[q][:], xT[:, bass.ds((it * 2 + q) * (NB * P), NB * P)]).then_inc(xt_in[q], 16)

        @block.tensor
        def _(pe):
            pe.wait_ge(weights_in, 48)
            nc.tensor.matmul(ps_a[:, 0:2], kT[:], att_sb[:], start=True, stop=True).then_inc(ka_ready, 1)
            pe.wait_ge(kw_ready, 1)
            with pe.Fori(0, NODE_STEPS // 2) as it:
                for q in range(2):
                    pe.wait_ge(xt_in[q], it * 16 + 16)
                    pe.wait_ge(rows_ready[q], it)
                    for b in range(NB):
                        last = nc.tensor.matmul(ps[q][:, b // 3, (b % 3) * (D + 2):(b % 3 + 1) * (D + 2)],
                                                xt[q][:, b * P:(b + 1) * P], kw[:], start=True, stop=True)
                    last.then_inc(h_ready[q], 1)

        @block.vector
        def _(dve):
            nc.vector.memset(rows[0][:], 1.0)
            nc.vector.memset(rows[1][:], 1.0)
            dve.wait_ge(ka_ready, 1)
            nc.vector.tensor_copy(kw[:, D:D + 2], ps_a[:, 0:2]).then_inc(kw_ready, 1)
            dve.wait_ge(kw_ready, 1)
            with dve.Fori(0, NODE_STEPS // 2) as it:
                for q in range(2):
                    dve.wait_ge(h_ready[q], it + 1)
                    dve.wait_ge(stored[q], it * 16)
                    for k in range(3):
                        b0, b1 = 3 * k, min(3 * k + 3, NB)
                        n = b1 - b0
                        last = nc.vector.tensor_copy(
                            rows[q][:, b0:b1, 0:D + 2],
                            ps[q][:, k, 0:n * (D + 2)].rearrange("p (b c) -> p b c", b=n))
                    last.then_inc(rows_ready[q], 1)

        @block.scalar
        def _(act):
            with act.Fori(0, NODE_STEPS // 2) as it:
                for q in range(2):
                    act.wait_ge(rows_ready[q], it + 1)
                    act.dma_start(node_rows(hv, it * 2 + q, HW), rows[q][:]).then_inc(stored[q], 16)
            for q in range(2):
                act.wait_ge(stored[q], 16 * (NODE_STEPS // 2))


def attend_any(nc, c, src, dst, hv, tables, landed):
    with ExitStack() as ctx:
        sb = lambda n, s, d=FP32: [ctx.enter_context(nc.sbuf_tensor(f"l0_{n}{q}", s, d)) for q in range(2)]
        sem = lambda n: ctx.enter_context(nc.semaphore("l0_" + n))
        sems = lambda n: [sem(f"{n}{q}") for q in range(2)]
        src_all = ctx.enter_context(nc.sbuf_tensor("l0_src_all", [P, TILES], I32))
        dst_all = ctx.enter_context(nc.sbuf_tensor("l0_dst_all", [P, TILES], I32))
        src_i, dst_i, hi_i, lo_i, to_i = (sb(n, [P, TS], I32) for n in ("src_i", "dst_i", "hi_i", "lo_i", "to_i"))
        src_f, cnt, away, z, zl, zc, w = (sb(n, [P, TS]) for n in ("src_f", "cnt", "away", "z", "zl", "zc", "w"))
        hl = sb("hl", [P, 2, TS], BF16)
        equal = sb("equal", [P, TS, P])
        h_dst, h_src, hw, sums = (sb(n, [P, TS, HW]) for n in ("h_dst", "h_src", "hw", "sums"))
        ps_key = ctx.enter_context(nc.psum_tensor("l0_ps_key", [P, TS, P], FP32))
        ps_sum = ctx.enter_context(nc.psum_tensor("l0_ps_sum", [P, 3, 512], FP32))
        ids_in = sem("ids_in")
        ids_ready, halves_ready, keys_ready, equal_ready = (sems(n) for n in ("ids_ready", "halves_ready", "keys_ready", "equal_ready"))
        gathered, clipped, scored, weighted, summed, sums_ready = (
            sems(n) for n in ("gathered", "clipped", "scored", "weighted", "summed", "sums_ready"))
        chain = sem("dve_chain")
        scattered = landed
        block = ctx.enter_context(nc.Block())
        HALF = STEPS // 2
        PER_COPY = 2 * TS // COPIES

        @block.sync
        def _(sp):
            sp.dma_start(src_all[:], src).then_inc(ids_in, 16)
            sp.dma_start(dst_all[:], dst).then_inc(ids_in, 16)
            sp.wait_ge(ids_in, 32)

        @block.gpsimd
        def _(pool):
            with pool.Fori(0, HALF) as it:
                for q in range(2):
                    gate(pool, c, ids_ready[q], it + 1)
                    gate(pool, c, weighted[q], it)
                    for u in range(TS):
                        pool.indirect_dma_start(h_dst[q][:, u, :], None, hv[:, :],
                                                bass.IndirectOffsetOnAxis(dst_i[q][:, u:u + 1], 0)).then_inc(gathered[q], 16)
                        pool.indirect_dma_start(h_src[q][:, u, :], None, hv[:, :],
                                                bass.IndirectOffsetOnAxis(src_i[q][:, u:u + 1], 0)).then_inc(gathered[q], 16)
                for q in range(2):
                    gate(pool, c, sums_ready[q], it + 1)
                    for u in range(TS):
                        k = u % COPIES
                        gate(pool, c, scattered[k], it * (16 * PER_COPY) + 16 * (1 + q * (TS // COPIES) + u // COPIES))
                        pool.indirect_dma_start(tables[k][:, :], bass.IndirectOffsetOnAxis(to_i[q][:, u:u + 1], 0),
                                                sums[q][:, u, :], None, compute_op=ALU.add).then_inc(scattered[k], 16)
            for k in range(COPIES):
                pool.wait_ge(scattered[k], 16 * (1 + HALF * PER_COPY))

        @block.vector
        def _(dve):
            dve.wait_ge(ids_in, 32)
            own = Tally(chain, 2 * 6)
            with dve.Fori(0, HALF) as it:
                own.start(it)
                for q in range(2):
                    cols = bass.ds((it * 2 + q) * TS, TS)
                    dve.wait_ge(gathered[q], it * (32 * TS))
                    nc.vector.tensor_copy(dst_i[q][:], dst_all[:, cols])
                    nc.vector.tensor_copy(src_i[q][:], src_all[:, cols]).then_inc(ids_ready[q], 1)
                    nc.vector.tensor_copy(src_f[q][:], src_all[:, cols])
                    nc.vector.tensor_single_scalar(hi_i[q][:], src_all[:, cols], 7, ALU.arith_shift_right)
                    own.inc(nc.vector.tensor_single_scalar(lo_i[q][:], src_all[:, cols], 127, ALU.bitwise_and))
                    own.wait(dve)
                    nc.vector.tensor_copy(hl[q][:, 0, :], hi_i[q][:])
                    nc.vector.tensor_copy(hl[q][:, 1, :], lo_i[q][:]).then_inc(halves_ready[q], 1)
                for q in range(2):
                    dve.wait_ge(keys_ready[q], it + 1)
                    dve.wait_ge(summed[q], it)
                    for u in range(TS):
                        last = nc.vector.scalar_tensor_tensor(
                            out=equal[q][:, u, :], in0=ps_key[:, u, :], scalar=src_f[q][:, u:u + 1], in1=c["later"][:],
                            op0=ALU.is_equal, op1=ALU.mult, accum_out=cnt[q][:, u:u + 1])
                    last.then_inc(equal_ready[q], 1)
                    own.inc(nc.vector.tensor_scalar(away[q][:], src_f[q][:], c["spare_row"][:, 0:1], None, ALU.subtract))
                    own.wait(dve)
                    dve.wait_ge(equal_ready[q], it + 1)
                    own.inc(nc.vector.scalar_tensor_tensor(out=z[q][:], in0=cnt[q][:], scalar=1.0, in1=away[q][:],
                                                           op0=ALU.is_equal, op1=ALU.mult))
                    own.wait(dve)
                    for k in range(COPIES):
                        dve.wait_ge(scattered[k], it * (16 * PER_COPY) + 16)
                    own.inc(nc.vector.tensor_scalar(to_i[q][:], z[q][:], c["spare_row"][:, 0:1], None, ALU.add))
                    own.wait(dve)
                    dve.wait_ge(gathered[q], it * (32 * TS) + 32 * TS)
                    own.inc(nc.vector.tensor_tensor(z[q][:], h_src[q][:, :, U_COL], h_dst[q][:, :, V_COL], ALU.add))
                    own.wait(dve)
                    own.inc(nc.vector.scalar_tensor_tensor(out=zl[q][:], in0=z[q][:], scalar=0.2, in1=z[q][:],
                                                           op0=ALU.mult, op1=ALU.max))
                    own.wait(dve)
                    nc.vector.tensor_scalar(zc[q][:], zl[q][:], 2.0, -2.0, ALU.min, ALU.max).then_inc(clipped[q], 1)
                own.end()

        @block.tensor
        def _(pe):
            with pe.Fori(0, HALF) as it:
                for q in range(2):
                    pe.wait_ge(halves_ready[q], it + 1)
                    pe.wait_ge(equal_ready[1 - q], it + q)
                    for u in range(TS):
                        nc.tensor.matmul(ps_key[:, u, :], hl[q][:, 0, u:u + 1].to_broadcast([P, P]), c["ident_hi"][:],
                                         start=True, stop=False)
                        last = nc.tensor.matmul(ps_key[:, u, :], hl[q][:, 1, u:u + 1].to_broadcast([P, P]), c["ident_lo"][:],
                                                start=False, stop=True)
                    last.then_inc(keys_ready[q], 1)
                    pe.wait_ge(equal_ready[q], it + 1)
                    pe.wait_ge(weighted[q], it + 1)
                    pe.wait_ge(sums_ready[1 - q], it + q)
                    for u in range(TS):
                        last = nc.tensor.matmul(ps_sum[:, u // 3, (u % 3) * HW:(u % 3 + 1) * HW], equal[q][:, u, :],
                                                hw[q][:, u, :], start=True, stop=True)
                    last.then_inc(summed[q], 1)

        @block.scalar
        def _(act):
            with act.Fori(0, HALF) as it:
                for q in range(2):
                    act.wait_ge(clipped[q], it + 1)
                    nc.scalar.activation(w[q][:], zc[q][:], ACT.Exp).then_inc(scored[q], 1)
                    act.wait_ge(scored[q], it + 1)
                    act.wait_ge(summed[q], it)
                    for u in range(TS):
                        last = nc.scalar.activation(hw[q][:, u, :], h_dst[q][:, u, :], ACT.Copy, scale=w[q][:, u:u + 1])
                    last.then_inc(weighted[q], 1)
                    act.wait_ge(summed[q], it + 1)
                    for k in range(COPIES):
                        act.wait_ge(scattered[k], it * (16 * PER_COPY) + 16)
                    for k in range(3):
                        u0, u1 = 3 * k, min(3 * k + 3, TS)
                        last = nc.scalar.activation(sums[q][:, u0:u1, :],
                                                    ps_sum[:, k, 0:(u1 - u0) * HW].rearrange("p (u c) -> p u c", u=u1 - u0),
                                                    ACT.Copy)
                    last.then_inc(sums_ready[q], 1)


def update_nodes(nc, c, x, tables, w_in, x1, h1):
    with ExitStack() as ctx:
        sb = lambda n, s, d=FP32: [ctx.enter_context(nc.sbuf_tensor(f"n0_{n}{q}", s, d)) for q in range(2)]
        sem = lambda n: ctx.enter_context(nc.semaphore("n0_" + n))
        sems = lambda n: [sem(f"{n}{q}") for q in range(2)]
        w_sb = ctx.enter_context(nc.sbuf_tensor("n0_w_in_sb", [P, D], FP32))
        part = sb("part", [P, COPIES, NB, HW])
        xs, y, x1s, xT, h1s = (sb(n, [P, NB, D]) for n in ("xs", "y", "x1s", "xT", "h1s"))
        den, rden, std, rstd = (sb(n, [P, NB]) for n in ("den", "rden", "std", "rstd"))
        stats = sb("stats", [P, NB, 6])
        mv = sb("mv", [P, NB, 2])
        ps_t = ctx.enter_context(nc.psum_tensor("n0_ps_t", [P, 8, P], FP32))
        ps_h = ctx.enter_context(nc.psum_tensor("n0_ps_h", [P, 8, P], FP32))
        w_ready = sem("w_ready")
        loaded, stored = sems("loaded"), sems("stored")
        var_ready, std_ready, x1_ready, xT_done, xT_ready, h1_done, h1_ready = (
            sems(n) for n in ("var_ready", "std_ready", "x1_ready", "xT_done", "xT_ready", "h1_done", "h1_ready"))
        chain = sem("dve_chain")
        block = ctx.enter_context(nc.Block())
        HALF = NODE_STEPS // 2

        @block.sync
        def _(sp):
            sp.dma_start(w_sb[:], w_in).then_inc(w_ready, 16)
            with sp.Fori(0, HALF) as it:
                for q in range(2):
                    sp.wait_ge(x1_ready[q], it)
                    for k in range(COPIES):
                        sp.dma_start(part[q][:, k], node_rows(tables[k], it * 2 + q, HW)).then_inc(loaded[q], 16)
                    sp.dma_start(xs[q][:], node_rows(x, it * 2 + q, D)).then_inc(loaded[q], 16)

        @block.vector
        def _(dve):
            own = Tally(chain, 2 * 7)
            with dve.Fori(0, HALF) as it:
                own.start(it)
                for q in range(2):
                    dve.wait_ge(loaded[q], it * (16 * (COPIES + 1)) + 16 * (COPIES + 1))
                    nc.vector.tensor_tensor(part[q][:, 0], part[q][:, 0], part[q][:, 1], ALU.add)
                    own.inc(nc.vector.tensor_tensor(part[q][:, 2], part[q][:, 2], part[q][:, 3], ALU.add))
                    own.wait(dve)
                    own.inc(nc.vector.tensor_tensor(part[q][:, 0], part[q][:, 0], part[q][:, 2], ALU.add))
                    own.wait(dve)
                    own.inc(nc.vector.tensor_scalar(den[q][:], part[q][:, 0, :, ONE_COL], 1e-30, None, ALU.max))
                    own.wait(dve)
                    own.inc(nc.vector.reciprocal(rden[q][:], den[q][:]))
                    own.wait(dve)
                    for b in range(NB):
                        last = nc.vector.scalar_tensor_tensor(out=y[q][:, b], in0=part[q][:, 0, b, 0:D],
                                                              scalar=rden[q][:, b:b + 1], in1=xs[q][:, b],
                                                              op0=ALU.mult, op1=ALU.add)
                    own.inc(last)
                    own.wait(dve)
                    for b in range(NB):
                        last = nc.vector.bn_stats(stats[q][:, b], y[q][:, b])
                    own.inc(last)
                    own.wait(dve)
                    dve.sem_inc(c["gates_passed"], 1)
                    for b in range(NB):
                        last = nc.vector.bn_aggr(mv[q][:, b], stats[q][:, b])
                    last.then_inc(var_ready[q], 1)
                    dve.wait_ge(std_ready[q], it + 1)
                    own.inc(nc.vector.reciprocal(rstd[q][:], std[q][:]))
                    own.wait(dve)
                    dve.wait_ge(stored[q], it * 32)
                    for b in range(NB):
                        last = nc.vector.tensor_scalar(x1s[q][:, b], y[q][:, b], mv[q][:, b, 0:1], rstd[q][:, b:b + 1],
                                                       ALU.subtract, ALU.mult)
                    last.then_inc(x1_ready[q], 1)
                own.end()

        @block.tensor
        def _(pe):
            pe.wait_ge(w_ready, 16)
            with pe.Fori(0, HALF) as it:
                for q in range(2):
                    pe.wait_ge(x1_ready[q], it + 1)
                    pe.wait_ge(xT_ready[1 - q], it + q)
                    for b in range(NB):
                        last = nc.tensor.transpose(ps_t[:, b, :], x1s[q][:, b], c["ident"][:])
                    last.then_inc(xT_done[q], 1)
                    pe.wait_ge(xT_ready[q], it + 1)
                    pe.wait_ge(h1_ready[1 - q], it + q)
                    for b in range(NB):
                        last = nc.tensor.matmul(ps_h[:, b, :], xT[q][:, b], w_sb[:], start=True, stop=True)
                    last.then_inc(h1_done[q], 1)

        @block.scalar
        def _(act):
            with act.Fori(0, HALF) as it:
                for q in range(2):
                    act.wait_ge(var_ready[q], it + 1)
                    nc.scalar.activation(std[q][:], mv[q][:, :, 1], ACT.Sqrt, bias=c["eps"][:, 0:1]).then_inc(std_ready[q], 1)
                    act.wait_ge(xT_done[q], it + 1)
                    nc.scalar.activation(xT[q][:, 0:4], ps_t[:, 0:4], ACT.Copy)
                    nc.scalar.activation(xT[q][:, 4:NB], ps_t[:, 4:NB], ACT.Copy).then_inc(xT_ready[q], 1)
                    act.wait_ge(h1_done[q], it + 1)
                    act.wait_ge(stored[q], it * 32)
                    nc.scalar.activation(h1s[q][:, 0:4], ps_h[:, 0:4], ACT.Copy)
                    nc.scalar.activation(h1s[q][:, 4:NB], ps_h[:, 4:NB], ACT.Copy).then_inc(h1_ready[q], 1)

        @block.gpsimd
        def _(pool):
            with pool.Fori(0, HALF) as it:
                for q in range(2):
                    gate(pool, c, x1_ready[q], it + 1)
                    pool.dma_start(node_rows(x1, it * 2 + q, D), x1s[q][:]).then_inc(stored[q], 16)
                    gate(pool, c, h1_ready[q], it + 1)
                    pool.dma_start(node_rows(h1, it * 2 + q, D), h1s[q][:]).then_inc(stored[q], 16)
            for q in range(2):
                pool.wait_ge(stored[q], 32 * HALF)


def convolve_any(nc, c, src, dst, weight, attr, w1, b1, w2, b2, h1, tables, landed):
    with ExitStack() as ctx:
        sb = lambda n, s, d=FP32: [ctx.enter_context(nc.sbuf_tensor(f"l1_{n}{q}", s, d)) for q in range(2)]
        one = lambda n, s, d=FP32: ctx.enter_context(nc.sbuf_tensor("l1_" + n, s, d))
        sem = lambda n: ctx.enter_context(nc.semaphore("l1_" + n))
        sems = lambda n: [sem(f"{n}{q}") for q in range(2)]
        src_all, dst_all = one("src_all", [P, TILES], I32), one("dst_all", [P, TILES], I32)
        cut = one("cut", [P, TILES])
        turns = one("turns", [P, TILES])
        w1_sb, w2_sb, b1_sb = one("w1_sb", [P, D]), one("w2_sb", [P, D]), one("b1_sb", [P, 1])
        b2_row, ones = one("b2_row", [1, D]), one("ones", [1, P])
        src_i, dst_i, hi_i, lo_i, to_i = (sb(n, [P, TS], I32) for n in ("src_i", "dst_i", "hi_i", "lo_i", "to_i"))
        dst_f, cnt, away, z, cut_s = (sb(n, [P, TS]) for n in ("dst_f", "cnt", "away", "z", "cut_s"))
        hl = sb("hl", [P, 2, TS], BF16)
        equal, h_src, msg, sums = (sb(n, [P, TS, P]) for n in ("equal", "h_src", "msg", "sums"))
        at, hid = sb("at", [P, TS * P // 2]), sb("hid", [P, TS, P])
        ps_key = ctx.enter_context(nc.psum_tensor("l1_ps_key", [P, TS, P], FP32))
        ps_hid = ctx.enter_context(nc.psum_tensor("l1_ps_hid", [P, TS, P], FP32))
        ps_f = ctx.enter_context(nc.psum_tensor("l1_ps_f", [P, TS, P], FP32))
        ps_sum = ctx.enter_context(nc.psum_tensor("l1_ps_sum", [P, TS, P], FP32))
        ids_in, weights_in, cut_ready, ones_ready = sem("ids_in"), sem("weights_in"), sem("cut_ready"), sem("ones_ready")
        ids_ready, halves_ready, keys_ready, equal_ready, attr_in = (
            sems(n) for n in ("ids_ready", "halves_ready", "keys_ready", "equal_ready", "attr_in"))
        gathered, hid_done, hid_ready, filtered, msg_ready, summed, sums_ready = (
            sems(n) for n in ("gathered", "hid_done", "hid_ready", "filtered", "msg_ready", "summed", "sums_ready"))
        pre, chain = sem("dve_pre"), sem("dve_chain")
        scattered = landed
        block = ctx.enter_context(nc.Block())
        HALF = STEPS // 2
        PER_COPY = 2 * TS // COPIES

        @block.sync
        def _(sp):
            sp.dma_start(src_all[:], src).then_inc(ids_in, 16)
            sp.dma_start(dst_all[:], dst).then_inc(ids_in, 16)
            sp.dma_start(cut[:], weight).then_inc(ids_in, 16)
            for tile, array in ((w1_sb[:], w1), (w2_sb[:], w2), (b1_sb[:], b1), (b2_row[:], b2)):
                sp.dma_start(tile, array).then_inc(weights_in, 16)
            sp.wait_ge(weights_in, 64)
            with sp.Fori(0, HALF) as it:
                for q in range(2):
                    sp.wait_ge(hid_done[q], it)
                    sp.dma_start(at[q][:], attr[bass.ds((it * 2 + q) * P, P), :]).then_inc(attr_in[q], 16)

        @block.gpsimd
        def _(pool):
            with pool.Fori(0, HALF) as it:
                for q in range(2):
                    gate(pool, c, ids_ready[q], it + 1)
                    gate(pool, c, msg_ready[q], it)
                    for u in range(TS):
                        pool.indirect_dma_start(h_src[q][:, u, :], None, h1[:, :],
                                                bass.IndirectOffsetOnAxis(src_i[q][:, u:u + 1], 0)).then_inc(gathered[q], 16)
                for q in range(2):
                    gate(pool, c, sums_ready[q], it + 1)
                    for u in range(TS):
                        k = u % COPIES
                        gate(pool, c, scattered[k], it * (16 * PER_COPY) + 16 * (1 + q * (TS // COPIES) + u // COPIES))
                        pool.indirect_dma_start(tables[k][:, :], bass.IndirectOffsetOnAxis(to_i[q][:, u:u + 1], 0),
                                                sums[q][:, u, :], None, compute_op=ALU.add).then_inc(scattered[k], 16)
            for k in range(COPIES):
                pool.wait_ge(scattered[k], 16 * (1 + HALF * PER_COPY))

        @block.vector
        def _(dve):
            dve.wait_ge(ids_in, 48)
            nc.vector.tensor_scalar(turns[:], cut[:], 1 / (2 * CUTOFF), ROUND, ALU.mult, ALU.add).then_inc(pre, 1)
            dve.wait_ge(pre, 1)
            nc.vector.tensor_scalar(turns[:], turns[:], ROUND, -2 * CUTOFF, ALU.subtract, ALU.mult).then_inc(pre, 1)
            dve.wait_ge(pre, 2)
            nc.vector.tensor_tensor(turns[:], turns[:], cut[:], ALU.add).then_inc(pre, 1)
            dve.wait_ge(pre, 3)
            nc.vector.scalar_tensor_tensor(out=turns[:], in0=turns[:], scalar=-1.0, in1=turns[:],
                                           op0=ALU.mult, op1=ALU.max).then_inc(pre, 1)
            dve.wait_ge(cut_ready, 1)
            nc.vector.tensor_scalar(cut[:], turns[:], 0.5, 0.5, ALU.mult, ALU.add).then_inc(pre, 1)
            nc.vector.memset(ones[:], 1.0).then_inc(ones_ready, 1)
            dve.wait_ge(pre, 5)
            own = Tally(chain, 2 * 4)
            with dve.Fori(0, HALF) as it:
                own.start(it)
                for q in range(2):
                    cols = bass.ds((it * 2 + q) * TS, TS)
                    dve.wait_ge(gathered[q], it * (16 * TS))
                    nc.vector.tensor_copy(src_i[q][:], src_all[:, cols]).then_inc(ids_ready[q], 1)
                    nc.vector.tensor_copy(dst_f[q][:], dst_all[:, cols])
                    nc.vector.tensor_copy(cut_s[q][:], cut[:, cols])
                    nc.vector.tensor_single_scalar(hi_i[q][:], dst_all[:, cols], 7, ALU.arith_shift_right)
                    own.inc(nc.vector.tensor_single_scalar(lo_i[q][:], dst_all[:, cols], 127, ALU.bitwise_and))
                    own.wait(dve)
                    nc.vector.tensor_copy(hl[q][:, 0, :], hi_i[q][:])
                    nc.vector.tensor_copy(hl[q][:, 1, :], lo_i[q][:]).then_inc(halves_ready[q], 1)
                for q in range(2):
                    dve.wait_ge(keys_ready[q], it + 1)
                    dve.wait_ge(summed[q], it)
                    for u in range(TS):
                        last = nc.vector.scalar_tensor_tensor(
                            out=equal[q][:, u, :], in0=ps_key[:, u, :], scalar=dst_f[q][:, u:u + 1], in1=c["later"][:],
                            op0=ALU.is_equal, op1=ALU.mult, accum_out=cnt[q][:, u:u + 1])
                    last.then_inc(equal_ready[q], 1)
                    own.inc(nc.vector.tensor_scalar(away[q][:], dst_f[q][:], c["spare_row"][:, 0:1], None, ALU.subtract))
                    own.wait(dve)
                    dve.wait_ge(equal_ready[q], it + 1)
                    own.inc(nc.vector.scalar_tensor_tensor(out=z[q][:], in0=cnt[q][:], scalar=1.0, in1=away[q][:],
                                                           op0=ALU.is_equal, op1=ALU.mult))
                    own.wait(dve)
                    for k in range(COPIES):
                        dve.wait_ge(scattered[k], it * (16 * PER_COPY) + 16)
                    own.inc(nc.vector.tensor_scalar(to_i[q][:], z[q][:], c["spare_row"][:, 0:1], None, ALU.add))
                    own.wait(dve)
                    dve.wait_ge(gathered[q], it * (16 * TS) + 16 * TS)
                    dve.wait_ge(filtered[q], it + 1)
                    for u in range(TS):
                        last = nc.vector.scalar_tensor_tensor(out=msg[q][:, u], in0=ps_f[:, u], scalar=cut_s[q][:, u:u + 1],
                                                              in1=h_src[q][:, u], op0=ALU.mult, op1=ALU.mult)
                    last.then_inc(msg_ready[q], 1)
                own.end()

        @block.tensor
        def _(pe):
            pe.wait_ge(weights_in, 64)
            pe.wait_ge(ones_ready, 1)
            with pe.Fori(0, HALF) as it:
                for q in range(2):
                    pe.wait_ge(halves_ready[q], it + 1)
                    pe.wait_ge(equal_ready[1 - q], it + q)
                    for u in range(TS):
                        nc.tensor.matmul(ps_key[:, u, :], hl[q][:, 0, u:u + 1].to_broadcast([P, P]), c["ident_hi"][:],
                                         start=True, stop=False)
                        last = nc.tensor.matmul(ps_key[:, u, :], hl[q][:, 1, u:u + 1].to_broadcast([P, P]), c["ident_lo"][:],
                                                start=False, stop=True)
                    last.then_inc(keys_ready[q], 1)
                    pe.wait_ge(attr_in[q], it * 16 + 16)
                    pe.wait_ge(hid_ready[1 - q], it + q)
                    for half in range(2):
                        rows = slice(half * RBF_ROWS, half * RBF_ROWS + RBF_ROWS)
                        last = nc.tensor.matmul(ps_hid[:, half * 4:half * 4 + 4, :].rearrange("p u c -> p (u c)"),
                                                w1_sb[rows, :], at[q][rows, :], start=True, stop=True)
                    last.then_inc(hid_done[q], 1)
                    pe.wait_ge(hid_ready[q], it + 1)
                    pe.wait_ge(msg_ready[1 - q], it + q)
                    for u in range(TS):
                        nc.tensor.matmul(ps_f[:, u, :], ones[:], b2_row[:], start=True, stop=False)
                        last = nc.tensor.matmul(ps_f[:, u, :], hid[q][:, u, :], w2_sb[:], start=False, stop=True)
                    last.then_inc(filtered[q], 1)
                    pe.wait_ge(equal_ready[q], it + 1)
                    pe.wait_ge(msg_ready[q], it + 1)
                    pe.wait_ge(sums_ready[1 - q], it + q)
                    for u in range(TS):
                        last = nc.tensor.matmul(ps_sum[:, u, :], equal[q][:, u, :], msg[q][:, u, :], start=True, stop=True)
                    last.then_inc(summed[q], 1)

        @block.scalar
        def _(act):
            act.wait_ge(weights_in, 64)
            act.wait_ge(pre, 4)
            nc.scalar.activation(turns[:], turns[:], ACT.Sin, bias=c["half_pi"][:, 0:1], scale=-PI / CUTOFF).then_inc(cut_ready, 1)
            with act.Fori(0, HALF) as it:
                for q in range(2):
                    act.wait_ge(hid_done[q], it + 1)
                    act.wait_ge(filtered[q], it)
                    for half in range(2):
                        last = nc.scalar.activation(hid[q][:, half * 4:half * 4 + 4], ps_hid[:, half * 4:half * 4 + 4],
                                                    ACT.Tanh, bias=b1_sb[:, 0:1])
                    last.then_inc(hid_ready[q], 1)
                    act.wait_ge(summed[q], it + 1)
                    for k in range(COPIES):
                        act.wait_ge(scattered[k], it * (16 * PER_COPY) + 16)
                    for half in range(2):
                        last = nc.scalar.activation(sums[q][:, half * 4:half * 4 + 4], ps_sum[:, half * 4:half * 4 + 4],
                                                    ACT.Copy)
                    last.then_inc(sums_ready[q], 1)


def finish_nodes(nc, c, tables, x1, w_out, b_out, w_lin, b_lin, out):
    with ExitStack() as ctx:
        sb = lambda n, s, d=FP32: [ctx.enter_context(nc.sbuf_tensor(f"n1_{n}{q}", s, d)) for q in range(2)]
        one = lambda n, s, d=FP32: ctx.enter_context(nc.sbuf_tensor("n1_" + n, s, d))
        sem = lambda n: ctx.enter_context(nc.semaphore("n1_" + n))
        sems = lambda n: [sem(f"{n}{q}") for q in range(2)]
        wo, wl, bo, bl = one("wo", [P, D]), one("wl", [P, D]), one("bo", [P, 1]), one("bl", [P, D])
        part = sb("part", [P, COPIES, NB, D])
        xs, y, outs, aggT, hidT = (sb(n, [P, NB, D]) for n in ("xs", "y", "outs", "aggT", "hidT"))
        std, rstd = (sb(n, [P, NB]) for n in ("std", "rstd"))
        stats = sb("stats", [P, NB, 6])
        mv = sb("mv", [P, NB, 2])
        ps_t = ctx.enter_context(nc.psum_tensor("n1_ps_t", [P, 8, P], FP32))
        ps_h = ctx.enter_context(nc.psum_tensor("n1_ps_h", [P, 8, P], FP32))
        ps_o = ctx.enter_context(nc.psum_tensor("n1_ps_o", [P, 8, P], FP32))
        w_ready = sem("w_ready")
        loaded, stored = sems("loaded"), sems("stored")
        added, aggT_done, aggT_ready, h_done, h_ready, o_done, var_ready, std_ready, out_ready, y_ready = (
            sems(n) for n in ("added", "aggT_done", "aggT_ready", "h_done", "h_ready", "o_done", "var_ready",
                              "std_ready", "out_ready", "y_ready"))
        chain = sem("dve_chain")
        block = ctx.enter_context(nc.Block())
        HALF = NODE_STEPS // 2

        @block.sync
        def _(sp):
            for tile, array in ((wo[:], w_out), (wl[:], w_lin), (bo[:], b_out), (bl[:], b_lin.to_broadcast([P, D]))):
                sp.dma_start(tile, array).then_inc(w_ready, 16)
            with sp.Fori(0, HALF) as it:
                for q in range(2):
                    sp.wait_ge(y_ready[q], it)
                    for k in range(COPIES):
                        sp.dma_start(part[q][:, k], node_rows(tables[k], it * 2 + q, D)).then_inc(loaded[q], 16)
                    sp.dma_start(xs[q][:], node_rows(x1, it * 2 + q, D)).then_inc(loaded[q], 16)

        @block.vector
        def _(dve):
            dve.wait_ge(w_ready, 64)
            own = Tally(chain, 2 * 4)
            with dve.Fori(0, HALF) as it:
                own.start(it)
                for q in range(2):
                    dve.wait_ge(loaded[q], it * (16 * (COPIES + 1)) + 16 * (COPIES + 1))
                    nc.vector.tensor_tensor(part[q][:, 0], part[q][:, 0], part[q][:, 1], ALU.add)
                    own.inc(nc.vector.tensor_tensor(part[q][:, 2], part[q][:, 2], part[q][:, 3], ALU.add))
                    own.wait(dve)
                    nc.vector.tensor_tensor(part[q][:, 0], part[q][:, 0], part[q][:, 2], ALU.add).then_inc(added[q], 1)
                    own.inc(nc.vector.tensor_tensor(xs[q][:], xs[q][:], bl[:].unsqueeze(1).to_broadcast([P, NB, D]), ALU.add))
                    own.wait(dve)
                    dve.wait_ge(o_done[q], it + 1)
                    nc.vector.tensor_tensor(y[q][:, 0:4], ps_o[:, 0:4], xs[q][:, 0:4], ALU.add)
                    nc.vector.tensor_tensor(y[q][:, 4:NB], ps_o[:, 4:NB], xs[q][:, 4:NB], ALU.add).then_inc(y_ready[q], 1)
                    dve.wait_ge(y_ready[q], it + 1)
                    for b in range(NB):
                        last = nc.vector.bn_stats(stats[q][:, b], y[q][:, b])
                    own.inc(last)
                    own.wait(dve)
                    dve.sem_inc(c["gates_passed"], 1)
                    for b in range(NB):
                        last = nc.vector.bn_aggr(mv[q][:, b], stats[q][:, b])
                    last.then_inc(var_ready[q], 1)
                    dve.wait_ge(std_ready[q], it + 1)
                    own.inc(nc.vector.reciprocal(rstd[q][:], std[q][:]))
                    own.wait(dve)
                    dve.wait_ge(stored[q], it * 16)
                    for b in range(NB):
                        last = nc.vector.tensor_scalar(outs[q][:, b], y[q][:, b], mv[q][:, b, 0:1], rstd[q][:, b:b + 1],
                                                       ALU.subtract, ALU.mult)
                    last.then_inc(out_ready[q], 1)
                own.end()

        @block.tensor
        def _(pe):
            pe.wait_ge(w_ready, 64)
            with pe.Fori(0, HALF) as it:
                for q in range(2):
                    pe.wait_ge(added[q], it + 1)
                    pe.wait_ge(aggT_ready[1 - q], it + q)
                    for b in range(NB):
                        last = nc.tensor.transpose(ps_t[:, b, :], part[q][:, 0, b], c["ident"][:])
                    last.then_inc(aggT_done[q], 1)
                    pe.wait_ge(aggT_ready[q], it + 1)
                    pe.wait_ge(h_ready[1 - q], it + q)
                    for b0, b1 in ((0, 4), (4, NB)):
                        last = nc.tensor.matmul(ps_h[:, b0:b1, :].rearrange("p b c -> p (b c)"), wo[:],
                                                aggT[q][:, b0:b1].rearrange("p b c -> p (b c)"), start=True, stop=True)
                    last.then_inc(h_done[q], 1)
                    pe.wait_ge(h_ready[q], it + 1)
                    pe.wait_ge(y_ready[1 - q], it + q)
                    for b in range(NB):
                        last = nc.tensor.matmul(ps_o[:, b, :], hidT[q][:, b], wl[:], start=True, stop=True)
                    last.then_inc(o_done[q], 1)

        @block.scalar
        def _(act):
            act.wait_ge(w_ready, 64)
            with act.Fori(0, HALF) as it:
                for q in range(2):
                    act.wait_ge(aggT_done[q], it + 1)
                    nc.scalar.activation(aggT[q][:, 0:4], ps_t[:, 0:4], ACT.Copy)
                    nc.scalar.activation(aggT[q][:, 4:NB], ps_t[:, 4:NB], ACT.Copy).then_inc(aggT_ready[q], 1)
                    act.wait_ge(h_done[q], it + 1)
                    nc.scalar.activation(hidT[q][:, 0:4], ps_h[:, 0:4], ACT.Tanh, bias=bo[:, 0:1])
                    nc.scalar.activation(hidT[q][:, 4:NB], ps_h[:, 4:NB], ACT.Tanh, bias=bo[:, 0:1]).then_inc(h_ready[q], 1)
                    act.wait_ge(var_ready[q], it + 1)
                    nc.scalar.activation(std[q][:], mv[q][:, :, 1], ACT.Sqrt, bias=c["eps"][:, 0:1]).then_inc(std_ready[q], 1)

        @block.gpsimd
        def _(pool):
            with pool.Fori(0, HALF) as it:
                for q in range(2):
                    gate(pool, c, out_ready[q], it + 1)
                    pool.dma_start(node_rows(out, it * 2 + q, D), outs[q][:]).then_inc(stored[q], 16)
            for q in range(2):
                pool.wait_ge(stored[q], 16 * HALF)


def network(nc, x, xT, src, dst, weight, attr, kernel, kernelT, att, w1, b1, w2, b2, w_in, w_out, b_out, w_lin, b_lin, out):
    dram = lambda n, rows, cols: nc.dram_tensor(n, [rows, cols], FP32, kind="Internal")
    hv = dram("hv", NODES_P, HW)
    x1, h1 = dram("x1", NODES_P, D), dram("h1", NODES_P, D)
    sums0 = [dram(f"sums0_{k}", ROWS, HW) for k in range(COPIES)]
    sums1 = [dram(f"sums1_{k}", ROWS, D) for k in range(COPIES)]
    with ExitStack() as ctx:
        c = constants(nc, ctx)
        landed0 = [ctx.enter_context(nc.semaphore(f"landed0_{k}")) for k in range(COPIES)]
        landed1 = [ctx.enter_context(nc.semaphore(f"landed1_{k}")) for k in range(COPIES)]
        project_nodes(nc, c, xT, kernel, kernelT, att, hv)
        zero_tables(nc, sums0, HW, landed0)
        attend_any(nc, c, src, dst, hv, sums0, landed0)
        zero_tables(nc, sums1, D, landed1)
        update_nodes(nc, c, x, sums0, w_in, x1, h1)
        convolve_any(nc, c, src, dst, weight, attr, w1, b1, w2, b2, h1, sums1, landed1)
        finish_nodes(nc, c, sums1, x1, w_out, b_out, w_lin, b_lin, out)


def kernel(x, src, dst, edge_attr_50, edge_weight, L0_gnn_kernel, L0_gnn_kernel_attention, L1_gnn_W_f1, L1_gnn_b_f1,
           L1_gnn_W_f2, L1_gnn_b_f2, L1_gnn_W_in, L1_gnn_W_out, L1_gnn_b_out, L1_gnn_W_lin, L1_gnn_b_lin):
    import numpy as np
    import concourse.bacc as bacc
    from concourse.bass_utils import run_bass_kernel_spmd as run

    def padded(a, n, value=0):
        a = np.asarray(a)
        return np.concatenate([a, np.full((n - a.shape[0],) + a.shape[1:], value, a.dtype)])

    def by_tile(a, value):
        return np.ascontiguousarray(padded(a, EDGES_P, value).reshape(TILES, P).T)

    xp = padded(x, NODES_P)
    attr = padded(edge_attr_50, EDGES_P).reshape(STEPS, 2, TS * P // 2, RBF).transpose(0, 1, 3, 2)
    attr = np.concatenate([attr, np.zeros((STEPS, 2, RBF_ROWS - RBF, TS * P // 2), attr.dtype)], axis=2)
    w1 = padded(L1_gnn_W_f1, RBF_ROWS)
    arrays = {
        "x": xp, "xT": xp.T,
        "src": by_tile(src, N_NODES), "dst": by_tile(dst, N_NODES), "weight": by_tile(edge_weight, 0),
        "attr": attr.reshape(STEPS * P, TS * P // 2),
        "kernel": L0_gnn_kernel, "kernelT": np.asarray(L0_gnn_kernel).T,
        "att": np.asarray(L0_gnn_kernel_attention).reshape(2, D).T,
        "w1": np.concatenate([w1, w1]), "b1": np.asarray(L1_gnn_b_f1).reshape(D, 1),
        "w2": L1_gnn_W_f2, "b2": np.asarray(L1_gnn_b_f2).reshape(1, D), "w_in": L1_gnn_W_in,
        "w_out": L1_gnn_W_out, "b_out": np.asarray(L1_gnn_b_out).reshape(D, 1),
        "w_lin": L1_gnn_W_lin, "b_lin": np.asarray(L1_gnn_b_lin).reshape(1, D),
    }
    arrays = {k: np.ascontiguousarray(v) for k, v in arrays.items()}
    nc = bacc.Bacc("TRN2", target_bir_lowering=False, num_devices=1)
    aps = {k: nc.dram_tensor(f"in_{k}", v.shape, mybir.dt.from_np(v.dtype), kind="ExternalInput").ap() for k, v in arrays.items()}
    out = nc.dram_tensor("out", (NODES_P, D), FP32, kind="ExternalOutput").ap()
    network(nc, out=out, **aps)
    return run(nc, [{f"in_{k}": v for k, v in arrays.items()}], core_ids=[0]).results[0]["out"][:N_NODES]
```

```python
import concourse.bass as bass
from concourse import mybir
from contextlib import ExitStack

FP32 = mybir.dt.float32
BF16 = mybir.dt.bfloat16
I32 = mybir.dt.int32
ALU = mybir.AluOpType
ACT = mybir.ActivationFunctionType

P = 128
D = 128
N_NODES = 12500
N_EDGES = 412500
RBF = 50
RBF_ROWS = 64
TS = 8
NODE_BLOCKS = -(-N_NODES // P)
NB = 7
NODE_STEPS = NODE_BLOCKS // NB
NODES_P = NODE_BLOCKS * P
STEPS = -(-N_EDGES // (P * TS))
STEPS += STEPS % 2
TILES = STEPS * TS
EDGES_P = TILES * P
HW = 132
U_COL, V_COL, ONE_COL = 128, 129, 130
WIN = 64
UNIT = 4
COPIES = 4
ROWS = NODES_P + P
EPS = 1e-5
CUTOFF = 10.0
PI = 3.141592653589793
ROUND = 12582912.0


class Tally:

    def __init__(self, sem, per):
        self.sem, self.per, self.n, self.it = sem, per, 0, 0

    def start(self, it):
        self.it, self.n = it, 0

    def inc(self, instruction):
        self.n += 1
        instruction.then_inc(self.sem, 1)

    def wait(self, engine):
        engine.wait_ge(self.sem, self.it * self.per + self.n)

    def end(self):
        assert self.n == self.per, (self.n, self.per)


def gate(pool, c, sem, value):
    pool.wait_ge(sem, value)
    pool.sem_inc(c["gates_passed"], 1)


def constants(nc, ctx):
    c = {"gates_passed": ctx.enter_context(nc.semaphore("gates_passed"))}
    for name, shape, dt in (("ident", [P, P], FP32), ("ident_lo", [P, P], BF16), ("ident_hi", [P, P], BF16),
                            ("later", [P, P], FP32), ("spare_row", [P, 1], FP32), ("eps", [P, 1], FP32),
                            ("half_pi", [P, 1], FP32), ("partition", [P, 1], FP32), ("block_no", [P, NODE_BLOCKS], FP32),
                            ("win_no", [P, WIN], FP32)):
        c[name] = ctx.enter_context(nc.sbuf_tensor(name, shape, dt))
    with nc.semaphore("const_filled") as filled, nc.Block() as block:
        @block.gpsimd
        def _(pool):
            pool.memset(c["ident"][:], 0.0)
            pool.memset(c["ident_lo"][:], 0.0)
            pool.memset(c["ident_hi"][:], 0.0)
            pool.memset(c["later"][:], 1.0)
            pool.memset(c["eps"][:], EPS)
            pool.memset(c["half_pi"][:], PI / 2)
            pool.iota(c["partition"][:], [[0, 1]], base=0, channel_multiplier=1, allow_small_or_imprecise_dtypes=True)
            pool.iota(c["block_no"][:], [[1, NODE_BLOCKS]], base=0, channel_multiplier=0,
                      allow_small_or_imprecise_dtypes=True)
            pool.iota(c["win_no"][:], [[1, WIN]], base=0, channel_multiplier=0, allow_small_or_imprecise_dtypes=True)
            pool.iota(c["spare_row"][:], [[0, 1]], base=NODES_P, channel_multiplier=1,
                      allow_small_or_imprecise_dtypes=True).then_inc(filled, 1)
            pool.wait_ge(filled, 1)
            for name, one in (("ident", 1.0), ("ident_lo", 1.0), ("ident_hi", 128.0)):
                pool.affine_select(out=c[name][:], in_=c[name][:], pattern=[[-1, P]],
                                   compare_op=ALU.not_equal, fill=one, base=0, channel_multiplier=1)
            pool.affine_select(out=c["later"][:], in_=c["later"][:], pattern=[[1, P]],
                               compare_op=ALU.is_ge, fill=0.0, base=0, channel_multiplier=-1).then_inc(filled, 1)
    return c


def zero_tables(nc, tables, width, landed):
    rows = ROWS // P
    with nc.sbuf_tensor(f"zeros{width}", [P, width], FP32) as zeros, nc.semaphore(f"zeros{width}_set") as zeros_set, \
            nc.Block() as block:
        @block.vector
        def _(dve):
            nc.vector.memset(zeros[:], 0.0).then_inc(zeros_set, 1)

        @block.gpsimd
        def _(pool):
            pool.wait_ge(zeros_set, 1)
            for k, table in enumerate(tables):
                pool.dma_start(table[:, :].rearrange("(p r) c -> p r c", p=P),
                               zeros[:].unsqueeze(1).to_broadcast([P, rows, width])).then_inc(landed[k], 16)
            for k in range(len(tables)):
                pool.wait_ge(landed[k], 16)


def node_rows(table, step, width):
    return table[bass.ds(step * (NB * P), NB * P), :].rearrange("(b p) c -> p b c", p=P)


def project_nodes(nc, c, xT, kernel, kernelT, att, hv, uv):
    with ExitStack() as ctx:
        sb = lambda n, s, d=FP32: ctx.enter_context(nc.sbuf_tensor("pr_" + n, s, d))
        sem = lambda n: ctx.enter_context(nc.semaphore("pr_" + n))
        kw = sb("kw", [P, D + 2])
        kT = sb("kT", [P, D])
        att_sb = sb("att_sb", [P, 2])
        xt = [sb(f"xt{q}", [P, NB * P]) for q in range(2)]
        rows = [sb(f"hv_rows{q}", [P, NB, HW]) for q in range(2)]
        ps_a = ctx.enter_context(nc.psum_tensor("pr_ps_a", [P, 512], FP32))
        ps = [ctx.enter_context(nc.psum_tensor(f"pr_ps_h{q}", [P, 3, 512], FP32)) for q in range(2)]
        weights_in, ka_ready, kw_ready = sem("weights_in"), sem("ka_ready"), sem("kw_ready")
        xt_in = [sem(f"xt_in{q}") for q in range(2)]
        h_ready = [sem(f"h_ready{q}") for q in range(2)]
        rows_ready = [sem(f"rows_ready{q}") for q in range(2)]
        stored = [sem(f"hv_stored{q}") for q in range(2)]
        block = ctx.enter_context(nc.Block())

        @block.sync
        def _(sp):
            sp.dma_start(kw[:, 0:D], kernel).then_inc(weights_in, 16)
            sp.dma_start(kT[:], kernelT).then_inc(weights_in, 16)
            sp.dma_start(att_sb[:], att).then_inc(weights_in, 16)
            with sp.Fori(0, NODE_STEPS // 2) as it:
                for q in range(2):
                    sp.wait_ge(h_ready[q], it)
                    sp.dma_start(xt[q][:], xT[:, bass.ds((it * 2 + q) * (NB * P), NB * P)]).then_inc(xt_in[q], 16)

        @block.tensor
        def _(pe):
            pe.wait_ge(weights_in, 48)
            nc.tensor.matmul(ps_a[:, 0:2], kT[:], att_sb[:], start=True, stop=True).then_inc(ka_ready, 1)
            pe.wait_ge(kw_ready, 1)
            with pe.Fori(0, NODE_STEPS // 2) as it:
                for q in range(2):
                    pe.wait_ge(xt_in[q], it * 16 + 16)
                    pe.wait_ge(rows_ready[q], it)
                    for b in range(NB):
                        last = nc.tensor.matmul(ps[q][:, b // 3, (b % 3) * (D + 2):(b % 3 + 1) * (D + 2)],
                                                xt[q][:, b * P:(b + 1) * P], kw[:], start=True, stop=True)
                    last.then_inc(h_ready[q], 1)

        @block.vector
        def _(dve):
            nc.vector.memset(rows[0][:], 1.0)
            nc.vector.memset(rows[1][:], 1.0)
            dve.wait_ge(ka_ready, 1)
            nc.vector.tensor_copy(kw[:, D:D + 2], ps_a[:, 0:2]).then_inc(kw_ready, 1)
            dve.wait_ge(kw_ready, 1)
            with dve.Fori(0, NODE_STEPS // 2) as it:
                for q in range(2):
                    dve.wait_ge(h_ready[q], it + 1)
                    dve.wait_ge(stored[q], it * 16)
                    for k in range(3):
                        b0, b1 = 3 * k, min(3 * k + 3, NB)
                        n = b1 - b0
                        last = nc.vector.tensor_copy(
                            rows[q][:, b0:b1, 0:D + 2],
                            ps[q][:, k, 0:n * (D + 2)].rearrange("p (b c) -> p b c", b=n))
                    last.then_inc(rows_ready[q], 1)
                    dve.wait_ge(rows_ready[q], it + 1)
                    nc.vector.tensor_copy(uv[:, :, bass.ds((it * 2 + q) * NB, NB)],
                                          rows[q][:, :, D:D + 2].rearrange("p b k -> p k b"))

        @block.scalar
        def _(act):
            with act.Fori(0, NODE_STEPS // 2) as it:
                for q in range(2):
                    act.wait_ge(rows_ready[q], it + 1)
                    act.dma_start(node_rows(hv, it * 2 + q, HW), rows[q][:]).then_inc(stored[q], 16)
            for q in range(2):
                act.wait_ge(stored[q], 16 * (NODE_STEPS // 2))


def attend_any(nc, c, src, dst, hv, tables, landed):
    with ExitStack() as ctx:
        sb = lambda n, s, d=FP32: [ctx.enter_context(nc.sbuf_tensor(f"l0_{n}{q}", s, d)) for q in range(2)]
        sem = lambda n: ctx.enter_context(nc.semaphore("l0_" + n))
        sems = lambda n: [sem(f"{n}{q}") for q in range(2)]
        src_all = ctx.enter_context(nc.sbuf_tensor("l0_src_all", [P, TILES], I32))
        dst_all = ctx.enter_context(nc.sbuf_tensor("l0_dst_all", [P, TILES], I32))
        src_i, dst_i, hi_i, lo_i, to_i = (sb(n, [P, TS], I32) for n in ("src_i", "dst_i", "hi_i", "lo_i", "to_i"))
        src_f, cnt, away, z, zl, zc, w = (sb(n, [P, TS]) for n in ("src_f", "cnt", "away", "z", "zl", "zc", "w"))
        hl = sb("hl", [P, 2, TS], BF16)
        equal = sb("equal", [P, TS, P])
        h_dst, h_src, hw, sums = (sb(n, [P, TS, HW]) for n in ("h_dst", "h_src", "hw", "sums"))
        ps_key = ctx.enter_context(nc.psum_tensor("l0_ps_key", [P, TS, P], FP32))
        ps_sum = ctx.enter_context(nc.psum_tensor("l0_ps_sum", [P, 3, 512], FP32))
        ids_in = sem("ids_in")
        ids_ready, halves_ready, keys_ready, equal_ready = (sems(n) for n in ("ids_ready", "halves_ready", "keys_ready", "equal_ready"))
        gathered, clipped, scored, weighted, summed, sums_ready = (
            sems(n) for n in ("gathered", "clipped", "scored", "weighted", "summed", "sums_ready"))
        chain = sem("dve_chain")
        scattered = landed
        block = ctx.enter_context(nc.Block())
        HALF = STEPS // 2
        PER_COPY = 2 * TS // COPIES

        @block.sync
        def _(sp):
            sp.dma_start(src_all[:], src).then_inc(ids_in, 16)
            sp.dma_start(dst_all[:], dst).then_inc(ids_in, 16)
            sp.wait_ge(ids_in, 32)

        @block.gpsimd
        def _(pool):
            with pool.Fori(0, HALF) as it:
                for q in range(2):
                    gate(pool, c, ids_ready[q], it + 1)
                    gate(pool, c, weighted[q], it)
                    for u in range(TS):
                        pool.indirect_dma_start(h_dst[q][:, u, :], None, hv[:, :],
                                                bass.IndirectOffsetOnAxis(dst_i[q][:, u:u + 1], 0)).then_inc(gathered[q], 16)
                        pool.indirect_dma_start(h_src[q][:, u, :], None, hv[:, :],
                                                bass.IndirectOffsetOnAxis(src_i[q][:, u:u + 1], 0)).then_inc(gathered[q], 16)
                for q in range(2):
                    gate(pool, c, sums_ready[q], it + 1)
                    for u in range(TS):
                        k = u % COPIES
                        gate(pool, c, scattered[k], it * (16 * PER_COPY) + 16 * (1 + q * (TS // COPIES) + u // COPIES))
                        pool.indirect_dma_start(tables[k][:, :], bass.IndirectOffsetOnAxis(to_i[q][:, u:u + 1], 0),
                                                sums[q][:, u, :], None, compute_op=ALU.add).then_inc(scattered[k], 16)
            for k in range(COPIES):
                pool.wait_ge(scattered[k], 16 * (1 + HALF * PER_COPY))

        @block.vector
        def _(dve):
            dve.wait_ge(ids_in, 32)
            own = Tally(chain, 2 * 6)
            with dve.Fori(0, HALF) as it:
                own.start(it)
                for q in range(2):
                    cols = bass.ds((it * 2 + q) * TS, TS)
                    dve.wait_ge(gathered[q], it * (32 * TS))
                    nc.vector.tensor_copy(dst_i[q][:], dst_all[:, cols])
                    nc.vector.tensor_copy(src_i[q][:], src_all[:, cols]).then_inc(ids_ready[q], 1)
                    nc.vector.tensor_copy(src_f[q][:], src_all[:, cols])
                    nc.vector.tensor_single_scalar(hi_i[q][:], src_all[:, cols], 7, ALU.arith_shift_right)
                    own.inc(nc.vector.tensor_single_scalar(lo_i[q][:], src_all[:, cols], 127, ALU.bitwise_and))
                    own.wait(dve)
                    nc.vector.tensor_copy(hl[q][:, 0, :], hi_i[q][:])
                    nc.vector.tensor_copy(hl[q][:, 1, :], lo_i[q][:]).then_inc(halves_ready[q], 1)
                for q in range(2):
                    dve.wait_ge(keys_ready[q], it + 1)
                    dve.wait_ge(summed[q], it)
                    for u in range(TS):
                        last = nc.vector.scalar_tensor_tensor(
                            out=equal[q][:, u, :], in0=ps_key[:, u, :], scalar=src_f[q][:, u:u + 1], in1=c["later"][:],
                            op0=ALU.is_equal, op1=ALU.mult, accum_out=cnt[q][:, u:u + 1])
                    last.then_inc(equal_ready[q], 1)
                    own.inc(nc.vector.tensor_scalar(away[q][:], src_f[q][:], c["spare_row"][:, 0:1], None, ALU.subtract))
                    own.wait(dve)
                    dve.wait_ge(equal_ready[q], it + 1)
                    own.inc(nc.vector.scalar_tensor_tensor(out=z[q][:], in0=cnt[q][:], scalar=1.0, in1=away[q][:],
                                                           op0=ALU.is_equal, op1=ALU.mult))
                    own.wait(dve)
                    for k in range(COPIES):
                        dve.wait_ge(scattered[k], it * (16 * PER_COPY) + 16)
                    own.inc(nc.vector.tensor_scalar(to_i[q][:], z[q][:], c["spare_row"][:, 0:1], None, ALU.add))
                    own.wait(dve)
                    dve.wait_ge(gathered[q], it * (32 * TS) + 32 * TS)
                    own.inc(nc.vector.tensor_tensor(z[q][:], h_src[q][:, :, U_COL], h_dst[q][:, :, V_COL], ALU.add))
                    own.wait(dve)
                    own.inc(nc.vector.scalar_tensor_tensor(out=zl[q][:], in0=z[q][:], scalar=0.2, in1=z[q][:],
                                                           op0=ALU.mult, op1=ALU.max))
                    own.wait(dve)
                    nc.vector.tensor_scalar(zc[q][:], zl[q][:], 2.0, -2.0, ALU.min, ALU.max).then_inc(clipped[q], 1)
                own.end()

        @block.tensor
        def _(pe):
            with pe.Fori(0, HALF) as it:
                for q in range(2):
                    pe.wait_ge(halves_ready[q], it + 1)
                    pe.wait_ge(equal_ready[1 - q], it + q)
                    for u in range(TS):
                        nc.tensor.matmul(ps_key[:, u, :], hl[q][:, 0, u:u + 1].to_broadcast([P, P]), c["ident_hi"][:],
                                         start=True, stop=False)
                        last = nc.tensor.matmul(ps_key[:, u, :], hl[q][:, 1, u:u + 1].to_broadcast([P, P]), c["ident_lo"][:],
                                                start=False, stop=True)
                    last.then_inc(keys_ready[q], 1)
                    pe.wait_ge(equal_ready[q], it + 1)
                    pe.wait_ge(weighted[q], it + 1)
                    pe.wait_ge(sums_ready[1 - q], it + q)
                    for u in range(TS):
                        last = nc.tensor.matmul(ps_sum[:, u // 3, (u % 3) * HW:(u % 3 + 1) * HW], equal[q][:, u, :],
                                                hw[q][:, u, :], start=True, stop=True)
                    last.then_inc(summed[q], 1)

        @block.scalar
        def _(act):
            with act.Fori(0, HALF) as it:
                for q in range(2):
                    act.wait_ge(clipped[q], it + 1)
                    nc.scalar.activation(w[q][:], zc[q][:], ACT.Exp).then_inc(scored[q], 1)
                    act.wait_ge(scored[q], it + 1)
                    act.wait_ge(summed[q], it)
                    for u in range(TS):
                        last = nc.scalar.activation(hw[q][:, u, :], h_dst[q][:, u, :], ACT.Copy, scale=w[q][:, u:u + 1])
                    last.then_inc(weighted[q], 1)
                    act.wait_ge(summed[q], it + 1)
                    for k in range(COPIES):
                        act.wait_ge(scattered[k], it * (16 * PER_COPY) + 16)
                    for k in range(3):
                        u0, u1 = 3 * k, min(3 * k + 3, TS)
                        last = nc.scalar.activation(sums[q][:, u0:u1, :],
                                                    ps_sum[:, k, 0:(u1 - u0) * HW].rearrange("p (u c) -> p u c", u=u1 - u0),
                                                    ACT.Copy)
                    last.then_inc(sums_ready[q], 1)


def update_nodes(nc, c, x, tables, w_in, x1, h1):
    with ExitStack() as ctx:
        sb = lambda n, s, d=FP32: [ctx.enter_context(nc.sbuf_tensor(f"n0_{n}{q}", s, d)) for q in range(2)]
        sem = lambda n: ctx.enter_context(nc.semaphore("n0_" + n))
        sems = lambda n: [sem(f"{n}{q}") for q in range(2)]
        w_sb = ctx.enter_context(nc.sbuf_tensor("n0_w_in_sb", [P, D], FP32))
        part = sb("part", [P, COPIES, NB, HW])
        xs, y, x1s, xT, h1s = (sb(n, [P, NB, D]) for n in ("xs", "y", "x1s", "xT", "h1s"))
        den, rden, std, rstd = (sb(n, [P, NB]) for n in ("den", "rden", "std", "rstd"))
        stats = sb("stats", [P, NB, 6])
        mv = sb("mv", [P, NB, 2])
        ps_t = ctx.enter_context(nc.psum_tensor("n0_ps_t", [P, 8, P], FP32))
        ps_h = ctx.enter_context(nc.psum_tensor("n0_ps_h", [P, 8, P], FP32))
        w_ready = sem("w_ready")
        loaded, stored = sems("loaded"), sems("stored")
        var_ready, std_ready, x1_ready, xT_done, xT_ready, h1_done, h1_ready = (
            sems(n) for n in ("var_ready", "std_ready", "x1_ready", "xT_done", "xT_ready", "h1_done", "h1_ready"))
        chain = sem("dve_chain")
        block = ctx.enter_context(nc.Block())
        HALF = NODE_STEPS // 2

        @block.sync
        def _(sp):
            sp.dma_start(w_sb[:], w_in).then_inc(w_ready, 16)
            with sp.Fori(0, HALF) as it:
                for q in range(2):
                    sp.wait_ge(x1_ready[q], it)
                    for k in range(COPIES):
                        sp.dma_start(part[q][:, k], node_rows(tables[k], it * 2 + q, HW)).then_inc(loaded[q], 16)
                    sp.dma_start(xs[q][:], node_rows(x, it * 2 + q, D)).then_inc(loaded[q], 16)

        @block.vector
        def _(dve):
            own = Tally(chain, 2 * 7)
            with dve.Fori(0, HALF) as it:
                own.start(it)
                for q in range(2):
                    dve.wait_ge(loaded[q], it * (16 * (COPIES + 1)) + 16 * (COPIES + 1))
                    nc.vector.tensor_tensor(part[q][:, 0], part[q][:, 0], part[q][:, 1], ALU.add)
                    own.inc(nc.vector.tensor_tensor(part[q][:, 2], part[q][:, 2], part[q][:, 3], ALU.add))
                    own.wait(dve)
                    own.inc(nc.vector.tensor_tensor(part[q][:, 0], part[q][:, 0], part[q][:, 2], ALU.add))
                    own.wait(dve)
                    own.inc(nc.vector.tensor_scalar(den[q][:], part[q][:, 0, :, ONE_COL], 1e-30, None, ALU.max))
                    own.wait(dve)
                    own.inc(nc.vector.reciprocal(rden[q][:], den[q][:]))
                    own.wait(dve)
                    for b in range(NB):
                        last = nc.vector.scalar_tensor_tensor(out=y[q][:, b], in0=part[q][:, 0, b, 0:D],
                                                              scalar=rden[q][:, b:b + 1], in1=xs[q][:, b],
                                                              op0=ALU.mult, op1=ALU.add)
                    own.inc(last)
                    own.wait(dve)
                    for b in range(NB):
                        last = nc.vector.bn_stats(stats[q][:, b], y[q][:, b])
                    own.inc(last)
                    own.wait(dve)
                    dve.sem_inc(c["gates_passed"], 1)
                    for b in range(NB):
                        last = nc.vector.bn_aggr(mv[q][:, b], stats[q][:, b])
                    last.then_inc(var_ready[q], 1)
                    dve.wait_ge(std_ready[q], it + 1)
                    own.inc(nc.vector.reciprocal(rstd[q][:], std[q][:]))
                    own.wait(dve)
                    dve.wait_ge(stored[q], it * 32)
                    for b in range(NB):
                        last = nc.vector.tensor_scalar(x1s[q][:, b], y[q][:, b], mv[q][:, b, 0:1], rstd[q][:, b:b + 1],
                                                       ALU.subtract, ALU.mult)
                    last.then_inc(x1_ready[q], 1)
                own.end()

        @block.tensor
        def _(pe):
            pe.wait_ge(w_ready, 16)
            with pe.Fori(0, HALF) as it:
                for q in range(2):
                    pe.wait_ge(x1_ready[q], it + 1)
                    pe.wait_ge(xT_ready[1 - q], it + q)
                    for b in range(NB):
                        last = nc.tensor.transpose(ps_t[:, b, :], x1s[q][:, b], c["ident"][:])
                    last.then_inc(xT_done[q], 1)
                    pe.wait_ge(xT_ready[q], it + 1)
                    pe.wait_ge(h1_ready[1 - q], it + q)
                    for b in range(NB):
                        last = nc.tensor.matmul(ps_h[:, b, :], xT[q][:, b], w_sb[:], start=True, stop=True)
                    last.then_inc(h1_done[q], 1)

        @block.scalar
        def _(act):
            with act.Fori(0, HALF) as it:
                for q in range(2):
                    act.wait_ge(var_ready[q], it + 1)
                    nc.scalar.activation(std[q][:], mv[q][:, :, 1], ACT.Sqrt, bias=c["eps"][:, 0:1]).then_inc(std_ready[q], 1)
                    act.wait_ge(xT_done[q], it + 1)
                    nc.scalar.activation(xT[q][:, 0:4], ps_t[:, 0:4], ACT.Copy)
                    nc.scalar.activation(xT[q][:, 4:NB], ps_t[:, 4:NB], ACT.Copy).then_inc(xT_ready[q], 1)
                    act.wait_ge(h1_done[q], it + 1)
                    act.wait_ge(stored[q], it * 32)
                    nc.scalar.activation(h1s[q][:, 0:4], ps_h[:, 0:4], ACT.Copy)
                    nc.scalar.activation(h1s[q][:, 4:NB], ps_h[:, 4:NB], ACT.Copy).then_inc(h1_ready[q], 1)

        @block.gpsimd
        def _(pool):
            with pool.Fori(0, HALF) as it:
                for q in range(2):
                    gate(pool, c, x1_ready[q], it + 1)
                    pool.dma_start(node_rows(x1, it * 2 + q, D), x1s[q][:]).then_inc(stored[q], 16)
                    gate(pool, c, h1_ready[q], it + 1)
                    pool.dma_start(node_rows(h1, it * 2 + q, D), h1s[q][:]).then_inc(stored[q], 16)
            for q in range(2):
                pool.wait_ge(stored[q], 32 * HALF)


def convolve_any(nc, c, src_all, dst, weight, attr, w1, b1, w2, b2, h1, tables, landed):
    with ExitStack() as ctx:
        sb = lambda n, s, d=FP32: [ctx.enter_context(nc.sbuf_tensor(f"l1_{n}{q}", s, d)) for q in range(2)]
        one = lambda n, s, d=FP32: ctx.enter_context(nc.sbuf_tensor("l1_" + n, s, d))
        sem = lambda n: ctx.enter_context(nc.semaphore("l1_" + n))
        sems = lambda n: [sem(f"{n}{q}") for q in range(2)]
        dst_all = one("dst_all", [P, TILES], I32)
        cut = one("cut", [P, TILES])
        turns = one("turns", [P, TILES])
        w1_sb, w2_sb, b1_sb = one("w1_sb", [P, D]), one("w2_sb", [P, D]), one("b1_sb", [P, 1])
        b2_row, ones = one("b2_row", [1, D]), one("ones", [1, P])
        src_i, dst_i, hi_i, lo_i, to_i = (sb(n, [P, TS], I32) for n in ("src_i", "dst_i", "hi_i", "lo_i", "to_i"))
        dst_f, cnt, away, z, cut_s = (sb(n, [P, TS]) for n in ("dst_f", "cnt", "away", "z", "cut_s"))
        hl = sb("hl", [P, 2, TS], BF16)
        equal, h_src, msg, sums = (sb(n, [P, TS, P]) for n in ("equal", "h_src", "msg", "sums"))
        at, hid = sb("at", [P, TS * P // 2]), sb("hid", [P, TS, P])
        ps_key = ctx.enter_context(nc.psum_tensor("l1_ps_key", [P, TS, P], FP32))
        ps_hid = ctx.enter_context(nc.psum_tensor("l1_ps_hid", [P, TS, P], FP32))
        ps_f = ctx.enter_context(nc.psum_tensor("l1_ps_f", [P, TS, P], FP32))
        ps_sum = ctx.enter_context(nc.psum_tensor("l1_ps_sum", [P, TS, P], FP32))
        ids_in, weights_in, cut_ready, ones_ready = sem("ids_in"), sem("weights_in"), sem("cut_ready"), sem("ones_ready")
        ids_ready, halves_ready, keys_ready, equal_ready, attr_in = (
            sems(n) for n in ("ids_ready", "halves_ready", "keys_ready", "equal_ready", "attr_in"))
        gathered, hid_done, hid_ready, filtered, msg_ready, summed, sums_ready = (
            sems(n) for n in ("gathered", "hid_done", "hid_ready", "filtered", "msg_ready", "summed", "sums_ready"))
        pre, chain = sem("dve_pre"), sem("dve_chain")
        scattered = landed
        block = ctx.enter_context(nc.Block())
        HALF = STEPS // 2
        PER_COPY = 2 * TS // COPIES

        @block.sync
        def _(sp):
            sp.dma_start(dst_all[:], dst).then_inc(ids_in, 16)
            sp.dma_start(cut[:], weight).then_inc(ids_in, 16)
            for tile, array in ((w1_sb[:], w1), (w2_sb[:], w2), (b1_sb[:], b1), (b2_row[:], b2)):
                sp.dma_start(tile, array).then_inc(weights_in, 16)
            sp.wait_ge(weights_in, 64)
            with sp.Fori(0, HALF) as it:
                for q in range(2):
                    sp.wait_ge(hid_done[q], it)
                    sp.dma_start(at[q][:], attr[bass.ds((it * 2 + q) * P, P), :]).then_inc(attr_in[q], 16)

        @block.gpsimd
        def _(pool):
            with pool.Fori(0, HALF) as it:
                for q in range(2):
                    gate(pool, c, ids_ready[q], it + 1)
                    gate(pool, c, msg_ready[q], it)
                    for u in range(TS):
                        pool.indirect_dma_start(h_src[q][:, u, :], None, h1[:, :],
                                                bass.IndirectOffsetOnAxis(src_i[q][:, u:u + 1], 0)).then_inc(gathered[q], 16)
                for q in range(2):
                    gate(pool, c, sums_ready[q], it + 1)
                    for u in range(TS):
                        k = u % COPIES
                        gate(pool, c, scattered[k], it * (16 * PER_COPY) + 16 * (1 + q * (TS // COPIES) + u // COPIES))
                        pool.indirect_dma_start(tables[k][:, :], bass.IndirectOffsetOnAxis(to_i[q][:, u:u + 1], 0),
                                                sums[q][:, u, :], None, compute_op=ALU.add).then_inc(scattered[k], 16)
            for k in range(COPIES):
                pool.wait_ge(scattered[k], 16 * (1 + HALF * PER_COPY))

        @block.vector
        def _(dve):
            dve.wait_ge(ids_in, 32)
            nc.vector.tensor_scalar(turns[:], cut[:], 1 / (2 * CUTOFF), ROUND, ALU.mult, ALU.add).then_inc(pre, 1)
            dve.wait_ge(pre, 1)
            nc.vector.tensor_scalar(turns[:], turns[:], ROUND, -2 * CUTOFF, ALU.subtract, ALU.mult).then_inc(pre, 1)
            dve.wait_ge(pre, 2)
            nc.vector.tensor_tensor(turns[:], turns[:], cut[:], ALU.add).then_inc(pre, 1)
            dve.wait_ge(pre, 3)
            nc.vector.scalar_tensor_tensor(out=turns[:], in0=turns[:], scalar=-1.0, in1=turns[:],
                                           op0=ALU.mult, op1=ALU.max).then_inc(pre, 1)
            dve.wait_ge(cut_ready, 1)
            nc.vector.tensor_scalar(cut[:], turns[:], 0.5, 0.5, ALU.mult, ALU.add).then_inc(pre, 1)
            nc.vector.memset(ones[:], 1.0).then_inc(ones_ready, 1)
            dve.wait_ge(pre, 5)
            own = Tally(chain, 2 * 4)
            with dve.Fori(0, HALF) as it:
                own.start(it)
                for q in range(2):
                    cols = bass.ds((it * 2 + q) * TS, TS)
                    dve.wait_ge(gathered[q], it * (16 * TS))
                    nc.vector.tensor_copy(src_i[q][:], src_all[:, cols]).then_inc(ids_ready[q], 1)
                    nc.vector.tensor_copy(dst_f[q][:], dst_all[:, cols])
                    nc.vector.tensor_copy(cut_s[q][:], cut[:, cols])
                    nc.vector.tensor_single_scalar(hi_i[q][:], dst_all[:, cols], 7, ALU.arith_shift_right)
                    own.inc(nc.vector.tensor_single_scalar(lo_i[q][:], dst_all[:, cols], 127, ALU.bitwise_and))
                    own.wait(dve)
                    nc.vector.tensor_copy(hl[q][:, 0, :], hi_i[q][:])
                    nc.vector.tensor_copy(hl[q][:, 1, :], lo_i[q][:]).then_inc(halves_ready[q], 1)
                for q in range(2):
                    dve.wait_ge(keys_ready[q], it + 1)
                    dve.wait_ge(summed[q], it)
                    for u in range(TS):
                        last = nc.vector.scalar_tensor_tensor(
                            out=equal[q][:, u, :], in0=ps_key[:, u, :], scalar=dst_f[q][:, u:u + 1], in1=c["later"][:],
                            op0=ALU.is_equal, op1=ALU.mult, accum_out=cnt[q][:, u:u + 1])
                    last.then_inc(equal_ready[q], 1)
                    own.inc(nc.vector.tensor_scalar(away[q][:], dst_f[q][:], c["spare_row"][:, 0:1], None, ALU.subtract))
                    own.wait(dve)
                    dve.wait_ge(equal_ready[q], it + 1)
                    own.inc(nc.vector.scalar_tensor_tensor(out=z[q][:], in0=cnt[q][:], scalar=1.0, in1=away[q][:],
                                                           op0=ALU.is_equal, op1=ALU.mult))
                    own.wait(dve)
                    for k in range(COPIES):
                        dve.wait_ge(scattered[k], it * (16 * PER_COPY) + 16)
                    own.inc(nc.vector.tensor_scalar(to_i[q][:], z[q][:], c["spare_row"][:, 0:1], None, ALU.add))
                    own.wait(dve)
                    dve.wait_ge(gathered[q], it * (16 * TS) + 16 * TS)
                    dve.wait_ge(filtered[q], it + 1)
                    for u in range(TS):
                        last = nc.vector.scalar_tensor_tensor(out=msg[q][:, u], in0=ps_f[:, u], scalar=cut_s[q][:, u:u + 1],
                                                              in1=h_src[q][:, u], op0=ALU.mult, op1=ALU.mult)
                    last.then_inc(msg_ready[q], 1)
                own.end()

        @block.tensor
        def _(pe):
            pe.wait_ge(weights_in, 64)
            pe.wait_ge(ones_ready, 1)
            with pe.Fori(0, HALF) as it:
                for q in range(2):
                    pe.wait_ge(halves_ready[q], it + 1)
                    pe.wait_ge(equal_ready[1 - q], it + q)
                    for u in range(TS):
                        nc.tensor.matmul(ps_key[:, u, :], hl[q][:, 0, u:u + 1].to_broadcast([P, P]), c["ident_hi"][:],
                                         start=True, stop=False)
                        last = nc.tensor.matmul(ps_key[:, u, :], hl[q][:, 1, u:u + 1].to_broadcast([P, P]), c["ident_lo"][:],
                                                start=False, stop=True)
                    last.then_inc(keys_ready[q], 1)
                    pe.wait_ge(attr_in[q], it * 16 + 16)
                    pe.wait_ge(hid_ready[1 - q], it + q)
                    for half in range(2):
                        rows = slice(half * RBF_ROWS, half * RBF_ROWS + RBF_ROWS)
                        last = nc.tensor.matmul(ps_hid[:, half * 4:half * 4 + 4, :].rearrange("p u c -> p (u c)"),
                                                w1_sb[rows, :], at[q][rows, :], start=True, stop=True)
                    last.then_inc(hid_done[q], 1)
                    pe.wait_ge(hid_ready[q], it + 1)
                    pe.wait_ge(msg_ready[1 - q], it + q)
                    for u in range(TS):
                        nc.tensor.matmul(ps_f[:, u, :], ones[:], b2_row[:], start=True, stop=False)
                        last = nc.tensor.matmul(ps_f[:, u, :], hid[q][:, u, :], w2_sb[:], start=False, stop=True)
                    last.then_inc(filtered[q], 1)
                    pe.wait_ge(equal_ready[q], it + 1)
                    pe.wait_ge(msg_ready[q], it + 1)
                    pe.wait_ge(sums_ready[1 - q], it + q)
                    for u in range(TS):
                        last = nc.tensor.matmul(ps_sum[:, u, :], equal[q][:, u, :], msg[q][:, u, :], start=True, stop=True)
                    last.then_inc(summed[q], 1)

        @block.scalar
        def _(act):
            act.wait_ge(weights_in, 64)
            act.wait_ge(pre, 4)
            nc.scalar.activation(turns[:], turns[:], ACT.Sin, bias=c["half_pi"][:, 0:1], scale=-PI / CUTOFF).then_inc(cut_ready, 1)
            with act.Fori(0, HALF) as it:
                for q in range(2):
                    act.wait_ge(hid_done[q], it + 1)
                    act.wait_ge(filtered[q], it)
                    for half in range(2):
                        last = nc.scalar.activation(hid[q][:, half * 4:half * 4 + 4], ps_hid[:, half * 4:half * 4 + 4],
                                                    ACT.Tanh, bias=b1_sb[:, 0:1])
                    last.then_inc(hid_ready[q], 1)
                    act.wait_ge(summed[q], it + 1)
                    for k in range(COPIES):
                        act.wait_ge(scattered[k], it * (16 * PER_COPY) + 16)
                    for half in range(2):
                        last = nc.scalar.activation(sums[q][:, half * 4:half * 4 + 4], ps_sum[:, half * 4:half * 4 + 4],
                                                    ACT.Copy)
                    last.then_inc(sums_ready[q], 1)


def number_edges(nc, c, src, dst, dst_steps, weight, e):
    SP_ = STEPS // 4
    with ExitStack() as ctx:
        one = lambda n, s, d=FP32: ctx.enter_context(nc.sbuf_tensor("ne_" + n, s, d))
        sem = lambda n: ctx.enter_context(nc.semaphore("ne_" + n))
        dst_i, half_i = one("dst_i", [P, TILES], I32), one("half_i", [P, TILES], I32)
        steps_i = one("steps_i", [SP_, 4, TS * P], I32)
        low, high, span = one("low", [SP_, 4]), one("high", [SP_, 4]), one("span", [SP_, 4])
        base_i = one("base_i", [SP_, 4], I32)
        base_all = one("base_all", [P, STEPS], I32)
        span_row, widest = one("span_row", [1, STEPS]), one("widest", [1, 1])
        turns, cut = one("turns", [P, TILES]), one("cut", [P, TILES])
        span_d = nc.dram_tensor("span_d", [STEPS], FP32, kind="Internal")
        ids_in, steps_in, weight_in = sem("ids_in"), sem("steps_in"), sem("weight_in")
        based, base_stored, base_back = sem("based"), sem("base_stored"), sem("base_back")
        turned, cosine, done = sem("turned"), sem("cosine"), sem("dve_done")
        block = ctx.enter_context(nc.Block())

        @block.sync
        def _(sp):
            sp.dma_start(steps_i[:], dst_steps).then_inc(steps_in, 16)
            sp.dma_start(e["src_i"][:], src).then_inc(ids_in, 16)
            sp.dma_start(dst_i[:], dst).then_inc(ids_in, 16)
            sp.dma_start(cut[:], weight).then_inc(weight_in, 16)
            sp.wait_ge(based, 1)
            sp.dma_start(e["base_d"][:].rearrange("(p c) -> p c", c=4), base_i[:]).then_inc(base_stored, 16)
            sp.dma_start(span_d[:].rearrange("(p c) -> p c", c=4), span[:]).then_inc(base_stored, 16)
            sp.wait_ge(base_stored, 32)
            sp.dma_start(e["base_row"][:], e["base_d"][:].unsqueeze(0)).then_inc(base_back, 16)
            sp.dma_start(base_all[:], e["base_d"][:].unsqueeze(0).to_broadcast([P, STEPS])).then_inc(base_back, 16)
            sp.dma_start(span_row[:], span_d[:].unsqueeze(0)).then_inc(base_back, 16)

        @block.vector
        def _(dve):
            n = 0

            def then(instruction, wait=True):
                nonlocal n
                n += 1
                instruction.then_inc(done, 1)
                if wait:
                    dve.wait_ge(done, n)

            dve.wait_ge(steps_in, 16)
            then(nc.vector.tensor_reduce(low[:], steps_i[:], mybir.AxisListType.X, ALU.min), False)
            then(nc.vector.tensor_reduce(high[:], steps_i[:], mybir.AxisListType.X, ALU.max))
            then(nc.vector.tensor_scalar(low[:], low[:], float(NODES_P - WIN), None, ALU.min))
            then(nc.vector.tensor_tensor(span[:], high[:], low[:], ALU.subtract), False)
            nc.vector.tensor_copy(base_i[:], low[:]).then_inc(based, 1)
            dve.wait_ge(ids_in, 32)
            nc.vector.tensor_copy(e["key_f"][:, :, 0], e["src_i"][:])
            then(nc.vector.tensor_single_scalar(half_i[:], e["src_i"][:], 7, ALU.arith_shift_right))
            nc.vector.tensor_copy(e["key_f"][:, :, 1], half_i[:])
            then(nc.vector.tensor_copy(e["key_b"][:, :, 0], half_i[:]))
            then(nc.vector.tensor_single_scalar(half_i[:], e["src_i"][:], P - 1, ALU.bitwise_and))
            then(nc.vector.tensor_copy(e["key_b"][:, :, 1], half_i[:]))
            dve.wait_ge(weight_in, 16)
            then(nc.vector.tensor_scalar(turns[:], cut[:], 1 / (2 * CUTOFF), ROUND, ALU.mult, ALU.add))
            then(nc.vector.tensor_scalar(turns[:], turns[:], ROUND, -2 * CUTOFF, ALU.subtract, ALU.mult))
            then(nc.vector.tensor_tensor(turns[:], turns[:], cut[:], ALU.add))
            nc.vector.scalar_tensor_tensor(out=turns[:], in0=turns[:], scalar=-1.0, in1=turns[:],
                                           op0=ALU.mult, op1=ALU.max).then_inc(turned, 1)
            dve.wait_ge(base_back, 48)
            base_of = base_all[:].unsqueeze(2).to_broadcast([P, STEPS, TS])
            then(nc.vector.tensor_tensor(e["key_f"][:, :, 2].rearrange("p (s u) -> p s u", u=TS),
                                         dst_i[:].rearrange("p (s u) -> p s u", u=TS), base_of, ALU.subtract))
            nc.vector.tensor_copy(e["out_f"][:, :, 0], e["key_f"][:, :, 2])
            then(nc.vector.tensor_reduce(widest[:], span_row[:], mybir.AxisListType.X, ALU.max))
            then(nc.vector.tensor_scalar(e["fits"][:], widest[:], float(WIN), None, ALU.is_lt))
            dve.wait_ge(cosine, 1)
            nc.vector.tensor_scalar(e["out_f"][:, :, 1], turns[:], 0.5, 0.5, ALU.mult, ALU.add)

        @block.scalar
        def _(act):
            act.wait_ge(turned, 1)
            nc.scalar.activation(turns[:], turns[:], ACT.Sin, bias=c["half_pi"][:, 0:1], scale=-PI / CUTOFF).then_inc(cosine, 1)


def cut_scores(nc, c, uv, u_parts, v_d):
    with ExitStack() as ctx:
        rest = ctx.enter_context(nc.sbuf_tensor("cs_rest", [P, NODE_BLOCKS], FP32))
        v_rows = ctx.enter_context(nc.sbuf_tensor("cs_v_rows", [NODE_BLOCKS, P], FP32))
        ps_v = ctx.enter_context(nc.psum_tensor("cs_ps_v", [NODE_BLOCKS, P], FP32))
        v_done, v_ready, v_stored, done = (ctx.enter_context(nc.semaphore("cs_" + n))
                                           for n in ("v_done", "v_ready", "v_stored", "dve_done"))
        block = ctx.enter_context(nc.Block())

        @block.tensor
        def _(pe):
            nc.tensor.transpose(ps_v[:], uv[:, 1, :], c["ident"][:]).then_inc(v_done, 1)

        @block.vector
        def _(dve):
            nc.vector.tensor_copy(u_parts[:, 0, :], uv[:, 0, :]).then_inc(done, 1)
            dve.wait_ge(done, 1)
            nc.vector.tensor_tensor(rest[:], uv[:, 0, :], u_parts[:, 0, :], ALU.subtract).then_inc(done, 1)
            dve.wait_ge(done, 2)
            nc.vector.tensor_copy(u_parts[:, 1, :], rest[:]).then_inc(done, 1)
            dve.wait_ge(done, 3)
            nc.vector.tensor_tensor(rest[:], rest[:], u_parts[:, 1, :], ALU.subtract).then_inc(done, 1)
            dve.wait_ge(done, 4)
            nc.vector.tensor_copy(u_parts[:, 2, :], rest[:])
            dve.wait_ge(v_done, 1)
            nc.vector.tensor_copy(v_rows[:], ps_v[:]).then_inc(v_ready, 1)

        @block.sync
        def _(sp):
            sp.wait_ge(v_ready, 1)
            sp.dma_start(v_d[:].rearrange("(b p) -> b p", p=P), v_rows[:]).then_inc(v_stored, 16)
            sp.wait_ge(v_stored, 16)


def reached(engine, sem, value):
    if not (isinstance(value, int) and value < 1):
        engine.wait_ge(sem, value)


def attend(nc, c, e, u_parts, v_d, hv, tables, landed):
    with ExitStack() as ctx:
        one = lambda n, s, d=FP32: ctx.enter_context(nc.sbuf_tensor("at_" + n, s, d))
        two = lambda n, s, d=FP32: [one(f"{n}{q}", s, d) for q in range(2)]
        sem = lambda n: ctx.enter_context(nc.semaphore("at_" + n))
        psum = lambda n, s: ctx.enter_context(nc.psum_tensor("at_" + n, s, FP32))
        key_f, key_b = two("key_f", [P, TS, 3]), two("key_b", [P, TS, 2], BF16)
        h_win, v_win = two("h_win", [WIN, HW]), two("v_win", [P, WIN])
        place = one("place", [P, UNIT, P], BF16)
        equal, weights = two("equal", [P, UNIT, P]), two("weights", [P, UNIT, WIN])
        count, away, u, v, z, zl, zc, score = (two(n, [P, UNIT]) for n in
                                               ("count", "away", "u", "v", "z", "zl", "zc", "score"))
        spread = two("spread", [WIN, UNIT, P])
        masked_v, masked_u = one("masked_v", [P, UNIT, WIN], BF16), one("masked_u", [P, UNIT, NODE_BLOCKS], BF16)
        to_i = [one(f"to_i{j}", [P, UNIT], I32) for j in range(4)]
        sums = [one(f"sums{j}", [P, UNIT, HW]) for j in range(4)]
        ps_place, ps_src, ps_u, ps_spread = (psum(n, [P, 512]) for n in ("ps_place", "ps_src", "ps_u", "ps_spread"))
        ps_sum = psum("ps_sum", [P, 2, 512])
        keys_ready, numbers_done, place_ready, equal_ready, u_done, clipped, scored, weights_ready = (
            sem(n) for n in ("keys_ready", "numbers_done", "place_ready", "equal_ready", "u_done", "clipped", "scored",
                             "weights_ready"))
        spread_done, spread_ready, sums_done, sums_ready, to_ready = (
            sem(n) for n in ("spread_done", "spread_ready", "sums_done", "sums_ready", "to_ready"))
        win_in = [sem(f"win_in{q}") for q in range(2)]
        chain = sem("dve_chain")
        scattered = landed
        block = ctx.enter_context(nc.Block())
        TURNS = STEPS // 2
        UNITS = TURNS * 4

        @block.sync
        def _(sp):
            def windows(it):
                for q in range(2):
                    base = sp.value_load(e["base_row"][0:1, bass.ds(it * 2 + q, 1)], min_val=0, max_val=NODES_P - WIN)
                    reached(sp, sums_done, it * 4 + 2 * q - 2)
                    sp.dma_start(h_win[q][:], hv[bass.ds(base, WIN), :]).then_inc(win_in[q], 16)
                    sp.dma_start(v_win[q][:], v_d[bass.ds(base, WIN)].unsqueeze(0).to_broadcast([P, WIN])).then_inc(win_in[q], 16)
            windows(0)
            with sp.Fori(1, TURNS) as it:
                windows(it)

        @block.gpsimd
        def _(pool):
            with pool.Fori(0, TURNS) as it:
                for j in range(4):
                    gate(pool, c, to_ready, it * 4 + j + 1)
                    gate(pool, c, sums_ready, it * 4 + j + 1)
                    for t in range(UNIT):
                        gate(pool, c, scattered[t], it * 64 + 16 * (j + 1))
                        pool.indirect_dma_start(tables[t][:, :], bass.IndirectOffsetOnAxis(to_i[j][:, t:t + 1], 0),
                                                sums[j][:, t, :], None, compute_op=ALU.add).then_inc(scattered[t], 16)
            for t in range(UNIT):
                pool.wait_ge(scattered[t], 16 * (1 + UNITS))

        @block.vector
        def _(dve):
            own = Tally(chain, 4 * 5)

            def take_keys(step, q):
                nc.vector.tensor_copy(key_f[q][:], e["key_f"][:, bass.ds(step * TS, TS), :])
                nc.vector.tensor_copy(key_b[q][:], e["key_b"][:, bass.ds(step * TS, TS), :]).then_inc(keys_ready, 1)

            def late(n, j):
                q, r, t0 = j % 2, j // 2, (j % 2) * UNIT
                reached(dve, scored, n + 1)
                reached(dve, spread_done, n - 1)
                for t in range(UNIT):
                    last = nc.vector.tensor_scalar(weights[q][:, t, :], c["win_no"][:], key_f[r][:, t0 + t, 2:3],
                                                   score[q][:, t:t + 1], ALU.is_equal, ALU.mult)
                last.then_inc(weights_ready, 1)

            def turn(it, first, last_turn):
                own.start(it)
                for j in range(4):
                    n = it * 4 + j
                    q, r, t0 = j % 2, j // 2, (j % 2) * UNIT
                    reached(dve, numbers_done, n + 1)
                    if not (first and j == 0):
                        dve.wait_ge(u_done, n)
                    nc.vector.tensor_scalar(place[:], ps_place[:].rearrange("p (t x) -> p t x", t=UNIT),
                                            c["partition"][:, 0:1], None, ALU.is_equal).then_inc(place_ready, 1)
                    reached(dve, spread_done, n - 1)
                    for t in range(UNIT):
                        last = nc.vector.scalar_tensor_tensor(
                            out=equal[q][:, t, :], in0=ps_src[:, t * P:(t + 1) * P], scalar=key_f[r][:, t0 + t, 0:1],
                            in1=c["later"][:], op0=ALU.is_equal, op1=ALU.mult, accum_out=count[q][:, t:t + 1])
                    last.then_inc(equal_ready, 1)
                    nc.vector.tensor_scalar(away[q][:], key_f[r][:, t0:t0 + UNIT, 0], c["spare_row"][:, 0:1], None,
                                            ALU.subtract).then_inc(chain, 1)
                    own.n += 1
                    if not (first and j == 0):
                        late(n - 1, (j - 1) % 4)
                    own.wait(dve)
                    dve.wait_ge(equal_ready, n + 1)
                    own.inc(nc.vector.scalar_tensor_tensor(out=z[q][:], in0=count[q][:], scalar=1.0, in1=away[q][:],
                                                           op0=ALU.is_equal, op1=ALU.mult))
                    if j % 2 == 0:
                        dve.wait_ge(win_in[r], it * 32 + 32)
                    for t in range(UNIT):
                        last = nc.vector.scalar_tensor_tensor(
                            out=masked_v[:, t, :], in0=c["win_no"][:], scalar=key_f[r][:, t0 + t, 2:3], in1=v_win[r][:],
                            op0=ALU.is_equal, op1=ALU.mult, accum_out=v[q][:, t:t + 1])
                    own.wait(dve)
                    if not first:
                        for t in range(UNIT):
                            dve.wait_ge(scattered[t], it * 64 + 16 * (j + 1 - 4 + 1))
                    nc.vector.tensor_scalar(to_i[j][:], z[q][:], c["spare_row"][:, 0:1], None, ALU.add).then_inc(to_ready, 1)
                    if j % 2 == 0 and not (last_turn and j == 2):
                        take_keys(it * 2 + r + 1, 1 - r)
                    dve.wait_ge(u_done, n + 1)
                    for t in range(UNIT):
                        last = nc.vector.scalar_tensor_tensor(
                            out=masked_u[:, t, :], in0=c["block_no"][:], scalar=key_f[r][:, t0 + t, 1:2],
                            in1=ps_u[:, t * P:t * P + NODE_BLOCKS], op0=ALU.is_equal, op1=ALU.mult,
                            accum_out=u[q][:, t:t + 1])
                    own.inc(last)
                    own.wait(dve)
                    own.inc(nc.vector.tensor_tensor(z[q][:], u[q][:], v[q][:], ALU.add))
                    own.wait(dve)
                    own.inc(nc.vector.scalar_tensor_tensor(out=zl[q][:], in0=z[q][:], scalar=0.2, in1=z[q][:],
                                                           op0=ALU.mult, op1=ALU.max))
                    own.wait(dve)
                    nc.vector.tensor_scalar(zc[q][:], zl[q][:], 2.0, -2.0, ALU.min, ALU.max).then_inc(clipped, 1)
                own.end()

            take_keys(0, 0)
            turn(0, True, False)
            with dve.Fori(1, TURNS - 1) as it:
                turn(it, False, False)
            turn(TURNS - 1, False, True)
            late(UNITS - 1, 3)

        @block.tensor
        def _(pe):
            def numbers(n, j):
                r, t0 = j // 2, (j % 2) * UNIT
                for t in range(UNIT):
                    place_of, block_of = (key_b[r][:, t0 + t, k:k + 1].to_broadcast([P, P]) for k in (1, 0))
                    cols = slice(t * P, (t + 1) * P)
                    nc.tensor.matmul(ps_place[:, cols], place_of, c["ident_lo"][:], start=True, stop=True)
                    nc.tensor.matmul(ps_src[:, cols], block_of, c["ident_hi"][:], start=True, stop=False)
                    last = nc.tensor.matmul(ps_src[:, cols], place_of, c["ident_lo"][:], start=False, stop=True)
                last.then_inc(numbers_done, 1)

            def late(n, j):
                q, r = j % 2, j // 2
                pe.wait_ge(weights_ready, n + 1)
                pe.wait_ge(equal_ready, n + 1)
                reached(pe, spread_ready, n)
                for t in range(UNIT):
                    last = nc.tensor.matmul(ps_spread[0:WIN, t * P:(t + 1) * P], weights[q][:, t, :], equal[q][:, t, :],
                                            start=True, stop=True)
                last.then_inc(spread_done, 1)

            def last_part(it, n, j):
                q, r = j % 2, j // 2
                if j % 2 == 0:
                    pe.wait_ge(win_in[r], it * 32 + 32)
                pe.wait_ge(spread_ready, n + 1)
                reached(pe, sums_ready, n)
                for t in range(UNIT):
                    last = nc.tensor.matmul(ps_sum[:, t // 3, (t % 3) * HW:(t % 3 + 1) * HW], spread[q][:, t, :],
                                            h_win[r][:], start=True, stop=True)
                last.then_inc(sums_done, 1)

            def turn(it, first, last_turn):
                for j in range(4):
                    n = it * 4 + j
                    pe.wait_ge(place_ready, n + 1)
                    reached(pe, clipped, n)
                    for t in range(UNIT):
                        for k in range(3):
                            last = nc.tensor.matmul(ps_u[:, t * P:t * P + NODE_BLOCKS], place[:, t, :], u_parts[:, k, :],
                                                    start=k == 0, stop=k == 2)
                    last.then_inc(u_done, 1)
                    if not (first and j == 0):
                        late(n - 1, (j - 1) % 4)
                    if not (last_turn and j == 3):
                        pe.wait_ge(equal_ready, n + 1)
                        if j % 2 == 1:
                            pe.wait_ge(keys_ready, it * 2 + j // 2 + 2)
                        numbers(n + 1, (j + 1) % 4)
                    if not (first and j == 0):
                        last_part(it if j else it - 1, n - 1, (j - 1) % 4)

            pe.wait_ge(keys_ready, 1)
            numbers(0, 0)
            turn(0, True, False)
            with pe.Fori(1, TURNS - 1) as it:
                turn(it, False, False)
            turn(TURNS - 1, False, True)
            late(UNITS - 1, 3)
            last_part(TURNS - 1, UNITS - 1, 3)

        @block.scalar
        def _(act):
            def late(it, n, j, first):
                q = j % 2
                act.wait_ge(spread_done, n + 1)
                reached(act, sums_done, n - 1)
                nc.scalar.activation(spread[q][:], ps_spread[0:WIN, :].rearrange("p (t x) -> p t x", t=UNIT),
                                     ACT.Copy).then_inc(spread_ready, 1)
                act.wait_ge(sums_done, n + 1)
                if not first:
                    for t in range(UNIT):
                        act.wait_ge(scattered[t], it * 64 + 16 * (j + 1 - 4 + 1))
                nc.scalar.activation(sums[j][:, 0:3, :], ps_sum[:, 0, 0:3 * HW].rearrange("p (t x) -> p t x", t=3), ACT.Copy)
                nc.scalar.activation(sums[j][:, 3, :], ps_sum[:, 1, 0:HW], ACT.Copy).then_inc(sums_ready, 1)

            def turn(it, first):
                for j in range(4):
                    n = it * 4 + j
                    if not (first and j == 0):
                        late(it if j else it - 1, n - 1, (j - 1) % 4, first)
                    act.wait_ge(clipped, n + 1)
                    reached(act, weights_ready, n - 1)
                    nc.scalar.activation(score[j % 2][:], zc[j % 2][:], ACT.Exp).then_inc(scored, 1)

            turn(0, True)
            with act.Fori(1, TURNS) as it:
                turn(it, False)
            late(TURNS - 1, UNITS - 1, 3, False)


def convolve(nc, c, e, attr, w1, b1, w2, b2, h1, aggT):
    with ExitStack() as ctx:
        one = lambda n, s, d=FP32: ctx.enter_context(nc.sbuf_tensor("co_" + n, s, d))
        two = lambda n, s, d=FP32: [one(f"{n}{q}", s, d) for q in range(2)]
        sem = lambda n: ctx.enter_context(nc.semaphore("co_" + n))
        psum = lambda n: ctx.enter_context(nc.psum_tensor("co_" + n, [P, UNIT, P], FP32))
        w1_half = two("w1_half", [P, D])
        w2_sb, b1_sb = one("w2_sb", [P, D]), one("b1_sb", [P, 1])
        b2_row, rest, ones = one("b2_row", [1, D]), one("rest", [1, D]), one("ones", [P, P], BF16)
        b2_cut, b2_parts = one("b2_cut", [1, 3, D], BF16), one("b2_parts", [P, D], BF16)
        src_i, out_f = two("src_i", [P, TS], I32), two("out_f", [P, TS, 2])
        h_src, at = two("h_src", [P, TS, P]), two("at", [P, UNIT * P])
        hid, msg = two("hid", [P, UNIT, P]), two("msg", [P, UNIT, P])
        share = [one(f"share{j}", [P, UNIT, WIN]) for j in range(4)]
        ps_hid, ps_agg = [psum(f"ps_hid{q}") for q in range(2)], [psum(f"ps_agg{q}") for q in range(2)]
        ps_f = [psum(f"ps_f{j}") for j in range(4)]
        weights_in, w1_in, halves_set, b2_cut_ready, b2_moved, pre = (
            sem(n) for n in ("weights_in", "w1_in", "halves_set", "b2_cut_ready", "b2_moved", "dve_pre"))
        attr_in, gathered = [sem(f"attr_in{q}") for q in range(2)], [sem(f"gathered{j}") for j in range(4)]
        ids_ready, hid_done, hid_ready, filtered, share_ready, msg_ready, summed, added = (
            sem(n) for n in ("ids_ready", "hid_done", "hid_ready", "filtered", "share_ready", "msg_ready", "summed", "added"))
        block = ctx.enter_context(nc.Block())
        TURNS = STEPS // 2
        UNITS = TURNS * 4

        @block.sync
        def _(sp):
            for tile, array in ((b2_row[:], b2), (w2_sb[:], w2), (b1_sb[:], b1)):
                sp.dma_start(tile, array).then_inc(weights_in, 16)
            sp.wait_ge(halves_set, 1)
            for half in range(2):
                rows = slice(half * RBF_ROWS, half * RBF_ROWS + RBF_ROWS)
                sp.dma_start(w1_half[half][rows, :], w1[rows, :]).then_inc(w1_in, 16)

            def load(it, q):
                sp.dma_start(at[q][:], attr[bass.ds((it * 2 + q) * P, P), :]).then_inc(attr_in[q], 16)
            for q in range(2):
                load(0, q)
            sp.wait_ge(b2_cut_ready, 1)
            for k in range(3):
                sp.dma_start(b2_parts[k:k + 1, :], b2_cut[:, k, :]).then_inc(b2_moved, 16)
            with sp.Fori(1, TURNS) as it:
                for q in range(2):
                    sp.wait_ge(hid_done, it * 4 + 2 * q - 2)
                    load(it, q)

        @block.gpsimd
        def _(pool):
            def turn(it, first):
                for q in range(2):
                    gate(pool, c, ids_ready, it * 2 + q + 1)
                    if not first:
                        gate(pool, c, msg_ready, it * 4 + 2 * q - 2)
                    for t in range(TS):
                        pool.indirect_dma_start(h_src[q][:, t, :], None, h1[:, :],
                                                bass.IndirectOffsetOnAxis(src_i[q][:, t:t + 1], 0)
                                                ).then_inc(gathered[2 * q + t // UNIT], 16)
            turn(0, True)
            with pool.Fori(1, TURNS) as it:
                turn(it, False)

        @block.vector
        def _(dve):
            def take(step, q):
                nc.vector.tensor_copy(out_f[q][:], e["out_f"][:, bass.ds(step * TS, TS), :])
                nc.vector.tensor_copy(src_i[q][:], e["src_i"][:, bass.ds(step * TS, TS)]).then_inc(ids_ready, 1)

            def shares(n, j, new_step):
                reached(dve, summed, n - 3)
                if new_step is not None:
                    dve.wait_ge(ids_ready, new_step + 1)
                for t in range(UNIT):
                    of_edge = out_f[j // 2][:, (j % 2) * UNIT + t, :]
                    last = nc.vector.tensor_scalar(share[j][:, t, :], c["win_no"][:], of_edge[:, 0:1], of_edge[:, 1:2],
                                                   ALU.is_equal, ALU.mult)
                last.then_inc(share_ready, 1)

            def add(step, q):
                base = dve.value_load(e["base_row"][0:1, bass.ds(step, 1)], min_val=0, max_val=NODES_P - WIN)
                dve.wait_ge(summed, step * 2 + 2)
                dve.wait_ge(added, step + 1)
                nc.vector.tensor_tensor(aggT[:, bass.ds(base, WIN)], aggT[:, bass.ds(base, WIN)], ps_agg[q][:, 0, 0:WIN],
                                        ALU.add).then_inc(added, 1)

            nc.vector.memset(w1_half[0][:], 0.0)
            nc.vector.memset(w1_half[1][:], 0.0).then_inc(halves_set, 1)
            nc.vector.memset(ones[:], 1.0)
            nc.vector.memset(b2_parts[:], 0.0).then_inc(pre, 1)
            nc.vector.memset(aggT[:], 0.0).then_inc(added, 1)
            dve.wait_ge(weights_in, 48)
            nc.vector.tensor_copy(b2_cut[:, 0, :], b2_row[:]).then_inc(pre, 1)
            dve.wait_ge(pre, 2)
            nc.vector.tensor_tensor(rest[:], b2_row[:], b2_cut[:, 0, :], ALU.subtract).then_inc(pre, 1)
            dve.wait_ge(pre, 3)
            nc.vector.tensor_copy(b2_cut[:, 1, :], rest[:]).then_inc(pre, 1)
            dve.wait_ge(pre, 4)
            nc.vector.tensor_tensor(rest[:], rest[:], b2_cut[:, 1, :], ALU.subtract).then_inc(pre, 1)
            dve.wait_ge(pre, 5)
            nc.vector.tensor_copy(b2_cut[:, 2, :], rest[:]).then_inc(b2_cut_ready, 1)

            def turn(it, first, last_turn):
                for j in range(4):
                    n, r = it * 4 + j, j // 2
                    dve.wait_ge(filtered, n + 1)
                    dve.wait_ge(gathered[j], it * (16 * UNIT) + 16 * UNIT)
                    reached(dve, summed, n - 1)
                    nc.vector.tensor_tensor(msg[j % 2][:], ps_f[j][:], h_src[r][:, (j % 2) * UNIT:(j % 2 + 1) * UNIT],
                                            ALU.mult).then_inc(msg_ready, 1)
                    if not (last_turn and j == 3):
                        shares(n + 1, (j + 1) % 4, it * 2 + r + 1 if j % 2 else None)
                    if j % 2 == 0 and not (first and j == 0):
                        add(it * 2 + r - 1, 1 - r)
                    if j % 2 and not last_turn:
                        dve.wait_ge(share_ready, n + 1)
                        take(it * 2 + r + 2, r)

            take(0, 0)
            take(1, 1)
            shares(0, 0, 0)
            turn(0, True, False)
            with dve.Fori(1, TURNS - 1) as it:
                turn(it, False, False)
            turn(TURNS - 1, False, True)
            add(STEPS - 1, 1)

        @block.tensor
        def _(pe):
            def hidden(n, j, loads):
                if j % 2 == 0:
                    pe.wait_ge(attr_in[j // 2], loads * 16)
                reached(pe, hid_ready, n - 1)
                nc.tensor.matmul(ps_hid[j % 2][:].rearrange("p t x -> p (t x)"), w1_half[j % 2][:], at[j // 2][:],
                                 start=True, stop=True).then_inc(hid_done, 1)

            def filters(n, j):
                pe.wait_ge(hid_ready, n + 1)
                reached(pe, msg_ready, n - 3)
                for t in range(UNIT):
                    nc.tensor.matmul(ps_f[j][:, t, :], ones[:], b2_parts[:], start=True, stop=False)
                    last = nc.tensor.matmul(ps_f[j][:, t, :], hid[j % 2][:, t, :], w2_sb[:], start=False, stop=True)
                last.then_inc(filtered, 1)

            def turn(it, first, last_turn):
                for j in range(4):
                    n, r = it * 4 + j, j // 2
                    if not (last_turn and j >= 2):
                        hidden(n + 2, (j + 2) % 4, it + (1 if j < 2 else 2))
                    if not (last_turn and j == 3):
                        filters(n + 1, (j + 1) % 4)
                    pe.wait_ge(msg_ready, n + 1)
                    pe.wait_ge(share_ready, n + 1)
                    if j % 2 == 0 and not first:
                        pe.wait_ge(added, it * 2 + r)
                    for t in range(UNIT):
                        last = nc.tensor.matmul(ps_agg[r][:, 0, 0:WIN], msg[j % 2][:, t, :], share[j][:, t, :],
                                                start=j % 2 == 0 and t == 0, stop=j % 2 == 1 and t == UNIT - 1)
                    last.then_inc(summed, 1)

            pe.wait_ge(w1_in, 32)
            hidden(0, 0, 1)
            hidden(1, 1, 1)
            pe.wait_ge(b2_moved, 48)
            filters(0, 0)
            turn(0, True, False)
            with pe.Fori(1, TURNS - 1) as it:
                turn(it, False, False)
            turn(TURNS - 1, False, True)

        @block.scalar
        def _(act):
            act.wait_ge(weights_in, 48)

            def turn(it, first):
                for j in range(4):
                    n = it * 4 + j
                    act.wait_ge(hid_done, n + 1)
                    reached(act, filtered, n - 1)
                    nc.scalar.activation(hid[j % 2][:], ps_hid[j % 2][:], ACT.Tanh, bias=b1_sb[:, 0:1]).then_inc(hid_ready, 1)
            turn(0, True)
            with act.Fori(1, TURNS) as it:
                turn(it, False)


def collect_any(nc, c, tables, aggT):
    with ExitStack() as ctx:
        part = ctx.enter_context(nc.sbuf_tensor("ca_part", [P, COPIES, NB, D], FP32))
        ps_t = ctx.enter_context(nc.psum_tensor("ca_ps_t", [P, 8, P], FP32))
        loaded, halves, added, turned, taken = (ctx.enter_context(nc.semaphore("ca_" + n))
                                                for n in ("loaded", "halves", "added", "turned", "taken"))
        block = ctx.enter_context(nc.Block())

        @block.sync
        def _(sp):
            with sp.Fori(0, NODE_STEPS) as it:
                sp.wait_ge(turned, it)
                for k in range(COPIES):
                    sp.dma_start(part[:, k], node_rows(tables[k], it, D)).then_inc(loaded, 16)

        @block.vector
        def _(dve):
            with dve.Fori(0, NODE_STEPS) as it:
                dve.wait_ge(loaded, it * (16 * COPIES) + 16 * COPIES)
                nc.vector.tensor_tensor(part[:, 0], part[:, 0], part[:, 1], ALU.add)
                nc.vector.tensor_tensor(part[:, 2], part[:, 2], part[:, 3], ALU.add).then_inc(halves, 1)
                dve.wait_ge(halves, it + 1)
                nc.vector.tensor_tensor(part[:, 0], part[:, 0], part[:, 2], ALU.add).then_inc(added, 1)

        @block.tensor
        def _(pe):
            with pe.Fori(0, NODE_STEPS) as it:
                pe.wait_ge(added, it + 1)
                pe.wait_ge(taken, it)
                for b in range(NB):
                    last = nc.tensor.transpose(ps_t[:, b, :], part[:, 0, b], c["ident"][:])
                last.then_inc(turned, 1)

        @block.scalar
        def _(act):
            with act.Fori(0, NODE_STEPS) as it:
                act.wait_ge(turned, it + 1)
                for b0, b1 in ((0, 4), (4, NB)):
                    last = nc.scalar.activation(aggT[:, bass.ds(it * (NB * P) + b0 * P, (b1 - b0) * P)],
                                                ps_t[:, b0:b1].rearrange("p b x -> p (b x)"), ACT.Copy)
                last.then_inc(taken, 1)


def finish_nodes(nc, c, aggT, x1, w_out, b_out, w_lin, b_lin, out):
    with ExitStack() as ctx:
        sb = lambda n, s, d=FP32: [ctx.enter_context(nc.sbuf_tensor(f"n1_{n}{q}", s, d)) for q in range(2)]
        one = lambda n, s, d=FP32: ctx.enter_context(nc.sbuf_tensor("n1_" + n, s, d))
        sem = lambda n: ctx.enter_context(nc.semaphore("n1_" + n))
        sems = lambda n: [sem(f"{n}{q}") for q in range(2)]
        wo, wl, bo, bl = one("wo", [P, D]), one("wl", [P, D]), one("bo", [P, 1]), one("bl", [P, D])
        xs, y, outs, hidT = (sb(n, [P, NB, D]) for n in ("xs", "y", "outs", "hidT"))
        std, rstd = (sb(n, [P, NB]) for n in ("std", "rstd"))
        stats = sb("stats", [P, NB, 6])
        mv = sb("mv", [P, NB, 2])
        ps_h = ctx.enter_context(nc.psum_tensor("n1_ps_h", [P, 8, P], FP32))
        ps_o = ctx.enter_context(nc.psum_tensor("n1_ps_o", [P, 8, P], FP32))
        w_ready = sem("w_ready")
        loaded, stored = sems("loaded"), sems("stored")
        h_done, h_ready, o_done, var_ready, std_ready, out_ready, y_ready = (
            sems(n) for n in ("h_done", "h_ready", "o_done", "var_ready", "std_ready", "out_ready", "y_ready"))
        chain = sem("dve_chain")
        block = ctx.enter_context(nc.Block())
        HALF = NODE_STEPS // 2

        @block.sync
        def _(sp):
            for tile, array in ((wo[:], w_out), (wl[:], w_lin), (bo[:], b_out), (bl[:], b_lin.to_broadcast([P, D]))):
                sp.dma_start(tile, array).then_inc(w_ready, 16)
            with sp.Fori(0, HALF) as it:
                for q in range(2):
                    sp.wait_ge(y_ready[q], it)
                    sp.dma_start(xs[q][:], node_rows(x1, it * 2 + q, D)).then_inc(loaded[q], 16)

        @block.vector
        def _(dve):
            dve.wait_ge(w_ready, 64)
            own = Tally(chain, 2 * 3)
            with dve.Fori(0, HALF) as it:
                own.start(it)
                for q in range(2):
                    dve.wait_ge(loaded[q], it * 16 + 16)
                    own.inc(nc.vector.tensor_tensor(xs[q][:], xs[q][:], bl[:].unsqueeze(1).to_broadcast([P, NB, D]), ALU.add))
                    own.wait(dve)
                    dve.wait_ge(o_done[q], it + 1)
                    nc.vector.tensor_tensor(y[q][:, 0:4], ps_o[:, 0:4], xs[q][:, 0:4], ALU.add)
                    nc.vector.tensor_tensor(y[q][:, 4:NB], ps_o[:, 4:NB], xs[q][:, 4:NB], ALU.add).then_inc(y_ready[q], 1)
                    dve.wait_ge(y_ready[q], it + 1)
                    for b in range(NB):
                        last = nc.vector.bn_stats(stats[q][:, b], y[q][:, b])
                    own.inc(last)
                    own.wait(dve)
                    dve.sem_inc(c["gates_passed"], 1)
                    for b in range(NB):
                        last = nc.vector.bn_aggr(mv[q][:, b], stats[q][:, b])
                    last.then_inc(var_ready[q], 1)
                    dve.wait_ge(std_ready[q], it + 1)
                    own.inc(nc.vector.reciprocal(rstd[q][:], std[q][:]))
                    own.wait(dve)
                    dve.wait_ge(stored[q], it * 16)
                    for b in range(NB):
                        last = nc.vector.tensor_scalar(outs[q][:, b], y[q][:, b], mv[q][:, b, 0:1], rstd[q][:, b:b + 1],
                                                       ALU.subtract, ALU.mult)
                    last.then_inc(out_ready[q], 1)
                own.end()

        @block.tensor
        def _(pe):
            pe.wait_ge(w_ready, 64)
            with pe.Fori(0, HALF) as it:
                for q in range(2):
                    pe.wait_ge(h_ready[1 - q], it + q)
                    for b0, b1 in ((0, 4), (4, NB)):
                        last = nc.tensor.matmul(ps_h[:, b0:b1, :].rearrange("p b c -> p (b c)"), wo[:],
                                                aggT[:, bass.ds((it * 2 + q) * (NB * P) + b0 * P, (b1 - b0) * P)],
                                                start=True, stop=True)
                    last.then_inc(h_done[q], 1)
                    pe.wait_ge(h_ready[q], it + 1)
                    pe.wait_ge(y_ready[1 - q], it + q)
                    for b in range(NB):
                        last = nc.tensor.matmul(ps_o[:, b, :], hidT[q][:, b], wl[:], start=True, stop=True)
                    last.then_inc(o_done[q], 1)

        @block.scalar
        def _(act):
            act.wait_ge(w_ready, 64)
            with act.Fori(0, HALF) as it:
                for q in range(2):
                    act.wait_ge(h_done[q], it + 1)
                    nc.scalar.activation(hidT[q][:, 0:4], ps_h[:, 0:4], ACT.Tanh, bias=bo[:, 0:1])
                    nc.scalar.activation(hidT[q][:, 4:NB], ps_h[:, 4:NB], ACT.Tanh, bias=bo[:, 0:1]).then_inc(h_ready[q], 1)
                    act.wait_ge(var_ready[q], it + 1)
                    nc.scalar.activation(std[q][:], mv[q][:, :, 1], ACT.Sqrt, bias=c["eps"][:, 0:1]).then_inc(std_ready[q], 1)

        @block.gpsimd
        def _(pool):
            with pool.Fori(0, HALF) as it:
                for q in range(2):
                    gate(pool, c, out_ready[q], it + 1)
                    pool.dma_start(node_rows(out, it * 2 + q, D), outs[q][:]).then_inc(stored[q], 16)
            for q in range(2):
                pool.wait_ge(stored[q], 16 * HALF)


def network(nc, x, xT, src, dst, dst_steps, weight, attr, kernel, kernelT, att, w1, b1, w2, b2, w_in, w_out, b_out,
            w_lin, b_lin, out):
    dram = lambda n, rows, cols: nc.dram_tensor(n, [rows, cols], FP32, kind="Internal")
    hv = dram("hv", NODES_P, HW)
    x1, h1 = dram("x1", NODES_P, D), dram("h1", NODES_P, D)
    v_d = nc.dram_tensor("v_d", [NODES_P], FP32, kind="Internal")
    base_d = nc.dram_tensor("base_d", [STEPS], I32, kind="Internal")
    sums0 = [dram(f"sums0_{k}", ROWS, HW) for k in range(COPIES)]
    sums1 = [dram(f"sums1_{k}", ROWS, D) for k in range(COPIES)]
    with ExitStack() as ctx:
        tile = lambda within, n, s, d=FP32: within.enter_context(nc.sbuf_tensor(n, s, d))
        c = constants(nc, ctx)
        landed0 = [ctx.enter_context(nc.semaphore(f"landed0_{k}")) for k in range(COPIES)]
        e = {"src_i": tile(ctx, "src_i", [P, TILES], I32), "base_d": base_d,
             "out_f": tile(ctx, "out_f", [P, TILES, 2]),
             "base_row": tile(ctx, "base_row", [1, STEPS], I32), "fits": tile(ctx, "fits", [1, 1], I32)}
        with ExitStack() as first:
            e["key_f"] = tile(first, "key_f", [P, TILES, 3])
            e["key_b"] = tile(first, "key_b", [P, TILES, 2], BF16)
            uv = tile(first, "uv", [P, 2, NODE_BLOCKS])
            u_parts = tile(first, "u_parts", [P, 3, NODE_BLOCKS], BF16)
            number_edges(nc, c, src, dst, dst_steps, weight, e)
            project_nodes(nc, c, xT, kernel, kernelT, att, hv, uv)
            cut_scores(nc, c, uv, u_parts, v_d)
            zero_tables(nc, sums0, HW, landed0)
            fits = nc.values_load(e["fits"][0:1, 0:1], min_val=0, max_val=1)
            free = nc.snapshot_sems()
            with nc.If(fits == 1):
                attend(nc, c, e, u_parts, v_d, hv, sums0, landed0)
            nc.restore_sems(free)
            with nc.Else():
                attend_any(nc, c, src, dst, hv, sums0, landed0)
        update_nodes(nc, c, x, sums0, w_in, x1, h1)
        aggT = tile(ctx, "aggT", [P, NODES_P])
        fits = nc.values_load(e["fits"][0:1, 0:1], min_val=0, max_val=1)
        free = nc.snapshot_sems()
        with nc.If(fits == 1):
            convolve(nc, c, e, attr, w1, b1, w2, b2, h1, aggT)
        nc.restore_sems(free)
        with nc.Else():
            landed1 = [ctx.enter_context(nc.semaphore(f"landed1_{k}")) for k in range(COPIES)]
            zero_tables(nc, sums1, D, landed1)
            convolve_any(nc, c, e["src_i"], dst, weight, attr, w1, b1, w2, b2, h1, sums1, landed1)
            collect_any(nc, c, sums1, aggT)
        finish_nodes(nc, c, aggT, x1, w_out, b_out, w_lin, b_lin, out)


def kernel(x, src, dst, edge_attr_50, edge_weight, L0_gnn_kernel, L0_gnn_kernel_attention, L1_gnn_W_f1, L1_gnn_b_f1,
           L1_gnn_W_f2, L1_gnn_b_f2, L1_gnn_W_in, L1_gnn_W_out, L1_gnn_b_out, L1_gnn_W_lin, L1_gnn_b_lin):
    import numpy as np
    import concourse.bacc as bacc
    from concourse.bass_utils import run_bass_kernel_spmd as run

    def padded(a, n, value=0):
        a = np.asarray(a)
        return np.concatenate([a, np.full((n - a.shape[0],) + a.shape[1:], value, a.dtype)])

    def by_tile(a, value):
        return np.ascontiguousarray(padded(a, EDGES_P, value).reshape(TILES, P).T)

    xp = padded(x, NODES_P)
    attr = padded(edge_attr_50, EDGES_P).reshape(STEPS, 2, TS * P // 2, RBF).transpose(0, 1, 3, 2)
    attr = np.concatenate([attr, np.zeros((STEPS, 2, RBF_ROWS - RBF, TS * P // 2), attr.dtype)], axis=2)
    w1 = padded(L1_gnn_W_f1, RBF_ROWS)
    arrays = {
        "x": xp, "xT": xp.T,
        "src": by_tile(src, N_NODES), "dst": by_tile(dst, N_NODES), "weight": by_tile(edge_weight, 0),
        "dst_steps": padded(dst, EDGES_P, N_NODES).reshape(STEPS // 4, 4, TS * P),
        "attr": attr.reshape(STEPS * P, TS * P // 2),
        "kernel": L0_gnn_kernel, "kernelT": np.asarray(L0_gnn_kernel).T,
        "att": np.asarray(L0_gnn_kernel_attention).reshape(2, D).T,
        "w1": np.concatenate([w1, w1]), "b1": np.asarray(L1_gnn_b_f1).reshape(D, 1),
        "w2": L1_gnn_W_f2, "b2": np.asarray(L1_gnn_b_f2).reshape(1, D), "w_in": L1_gnn_W_in,
        "w_out": L1_gnn_W_out, "b_out": np.asarray(L1_gnn_b_out).reshape(D, 1),
        "w_lin": L1_gnn_W_lin, "b_lin": np.asarray(L1_gnn_b_lin).reshape(1, D),
    }
    arrays = {k: np.ascontiguousarray(v) for k, v in arrays.items()}
    nc = bacc.Bacc("TRN2", target_bir_lowering=False, num_devices=1)
    aps = {k: nc.dram_tensor(f"in_{k}", v.shape, mybir.dt.from_np(v.dtype), kind="ExternalInput").ap() for k, v in arrays.items()}
    out = nc.dram_tensor("out", (NODES_P, D), FP32, kind="ExternalOutput").ap()
    network(nc, out=out, **aps)
    return run(nc, [{f"in_{k}": v for k, v in arrays.items()}], core_ids=[0]).results[0]["out"][:N_NODES]
```

```python
import concourse.bass as bass
from concourse import mybir
from contextlib import ExitStack

FP32 = mybir.dt.float32
BF16 = mybir.dt.bfloat16
I32 = mybir.dt.int32
ALU = mybir.AluOpType
ACT = mybir.ActivationFunctionType

P = 128
D = 128
N_NODES = 12500
N_EDGES = 412500
RBF = 50
RBF_ROWS = 64
TS = 8
NODE_BLOCKS = -(-N_NODES // P)
NB = 7
NODE_STEPS = NODE_BLOCKS // NB
NODES_P = NODE_BLOCKS * P
STEPS = -(-N_EDGES // (P * TS))
STEPS += STEPS % 2
TILES = STEPS * TS
EDGES_P = TILES * P
SW = D + 1
HW = D + 3
ONE_COL, U_COL, V_COL = D, D + 1, D + 2
PW = D + 2
HALF_P = P // 2
HALF_BLOCKS = 2 * NODE_BLOCKS
WIN = 64
UNIT = 4
COPIES = 4
ROWS = NODES_P + P
EPS = 1e-5
CUTOFF = 10.0
PI = 3.141592653589793
ROUND = 12582912.0


class Tally:

    def __init__(self, sem, per):
        self.sem, self.per, self.n, self.it = sem, per, 0, 0

    def start(self, it):
        self.it, self.n = it, 0

    def inc(self, instruction):
        self.n += 1
        instruction.then_inc(self.sem, 1)

    def wait(self, engine):
        engine.wait_ge(self.sem, self.it * self.per + self.n)

    def end(self):
        assert self.n == self.per, (self.n, self.per)


def gate(pool, c, sem, value):
    pool.wait_ge(sem, value)
    pool.sem_inc(c["gates_passed"], 1)


def constants(nc, ctx):
    c = {"gates_passed": ctx.enter_context(nc.semaphore("gates_passed"))}
    for name, shape, dt in (("ident", [P, P], FP32), ("ident_lo", [P, P], BF16), ("ident_hi", [P, P], BF16), ("ident_half", [P, P], BF16),
                            ("later", [P, P], FP32), ("spare_row", [P, 1], FP32), ("eps", [P, 1], FP32), ("one", [P, 1], FP32),
                            ("half_pi", [P, 1], FP32), ("minus_place", [P, 1], FP32), ("block_no", [P, HALF_BLOCKS], FP32),
                            ("win_no", [P, WIN], FP32), ("zeros", [P, SW], FP32)):
        c[name] = ctx.enter_context(nc.sbuf_tensor(name, shape, dt))
    with nc.semaphore("const_filled") as filled, nc.Block() as block:
        @block.gpsimd
        def _(pool):
            pool.memset(c["ident"][:], 0.0)
            pool.memset(c["ident_lo"][:], 0.0)
            pool.memset(c["ident_hi"][:], 0.0)
            pool.memset(c["ident_half"][:], 0.0)
            pool.memset(c["later"][:], 1.0)
            pool.memset(c["eps"][:], EPS)
            pool.memset(c["one"][:], 1.0)
            pool.memset(c["zeros"][:], 0.0)
            pool.memset(c["half_pi"][:], PI / 2)
            pool.iota(c["minus_place"][:], [[0, 1]], base=0, channel_multiplier=-1, allow_small_or_imprecise_dtypes=True)
            pool.iota(c["block_no"][:], [[1, HALF_BLOCKS]], base=0, channel_multiplier=0,
                      allow_small_or_imprecise_dtypes=True)
            pool.iota(c["win_no"][:], [[1, WIN]], base=0, channel_multiplier=0, allow_small_or_imprecise_dtypes=True)
            pool.iota(c["spare_row"][:], [[0, 1]], base=NODES_P, channel_multiplier=1,
                      allow_small_or_imprecise_dtypes=True).then_inc(filled, 1)
            pool.wait_ge(filled, 1)
            pool.iota(c["minus_place"][HALF_P:P, :], [[0, 1]], base=0, channel_multiplier=-1,
                      allow_small_or_imprecise_dtypes=True).then_inc(filled, 1)
            pool.wait_ge(filled, 2)
            for name, one in (("ident", 1.0), ("ident_lo", 1.0), ("ident_hi", 128.0), ("ident_half", 64.0)):
                pool.affine_select(out=c[name][:], in_=c[name][:], pattern=[[-1, P]],
                                   compare_op=ALU.not_equal, fill=one, base=0, channel_multiplier=1)
            pool.affine_select(out=c["later"][:], in_=c["later"][:], pattern=[[1, P]],
                               compare_op=ALU.is_ge, fill=0.0, base=0, channel_multiplier=-1).then_inc(filled, 1)
    return c


def fill(pool, tables, zeros, landed):
    for k, table in enumerate(tables):
        pool.dma_start(table[:, :].rearrange("(p r) c -> p r c", p=P),
                       zeros[:].unsqueeze(1).to_broadcast([P, ROWS // P, zeros.shape[1]])).then_inc(landed[k], 16)


def zero_tables(nc, tables, width, landed):
    with nc.sbuf_tensor(f"zeros{width}", [P, width], FP32) as zeros, nc.semaphore(f"zeros{width}_set") as zeros_set, \
            nc.Block() as block:
        @block.vector
        def _(dve):
            nc.vector.memset(zeros[:], 0.0).then_inc(zeros_set, 1)

        @block.gpsimd
        def _(pool):
            pool.wait_ge(zeros_set, 1)
            fill(pool, tables, zeros, landed)
            for k in range(len(tables)):
                pool.wait_ge(landed[k], 16)


def node_rows(table, step, width):
    return table[bass.ds(step * (NB * P), NB * P), :].rearrange("(b p) c -> p b c", p=P)


def project_nodes(nc, c, xT, kernel, kernelT, att, hv):
    with ExitStack() as ctx:
        sb = lambda n, s, d=FP32: ctx.enter_context(nc.sbuf_tensor("pr_" + n, s, d))
        sem = lambda n: ctx.enter_context(nc.semaphore("pr_" + n))
        kw = sb("kw", [P, D + 2])
        kT = sb("kT", [P, D])
        att_sb = sb("att_sb", [P, 2])
        xt = [sb(f"xt{q}", [P, NB * P]) for q in range(2)]
        rows = [sb(f"hv_rows{q}", [P, NB, HW]) for q in range(2)]
        ps_a = ctx.enter_context(nc.psum_tensor("pr_ps_a", [P, 512], FP32))
        ps = [ctx.enter_context(nc.psum_tensor(f"pr_ps_h{q}", [P, 3, 512], FP32)) for q in range(2)]
        weights_in, ka_ready, kw_ready = sem("weights_in"), sem("ka_ready"), sem("kw_ready")
        xt_in = [sem(f"xt_in{q}") for q in range(2)]
        h_ready = [sem(f"h_ready{q}") for q in range(2)]
        rows_ready = [sem(f"rows_ready{q}") for q in range(2)]
        stored = [sem(f"hv_stored{q}") for q in range(2)]
        block = ctx.enter_context(nc.Block())

        @block.sync
        def _(sp):
            sp.dma_start(kw[:, 0:D], kernel).then_inc(weights_in, 16)
            sp.dma_start(kT[:], kernelT).then_inc(weights_in, 16)
            sp.dma_start(att_sb[:], att).then_inc(weights_in, 16)
            with sp.Fori(0, NODE_STEPS // 2) as it:
                for q in range(2):
                    sp.wait_ge(h_ready[q], it)
                    sp.dma_start(xt[q][:], xT[:, bass.ds((it * 2 + q) * (NB * P), NB * P)]).then_inc(xt_in[q], 16)

        @block.tensor
        def _(pe):
            pe.wait_ge(weights_in, 48)
            nc.tensor.matmul(ps_a[:, 0:2], kT[:], att_sb[:], start=True, stop=True).then_inc(ka_ready, 1)
            pe.wait_ge(kw_ready, 1)
            with pe.Fori(0, NODE_STEPS // 2) as it:
                for q in range(2):
                    pe.wait_ge(xt_in[q], it * 16 + 16)
                    pe.wait_ge(rows_ready[q], it)
                    for b in range(NB):
                        last = nc.tensor.matmul(ps[q][:, b // 3, (b % 3) * (D + 2):(b % 3 + 1) * (D + 2)],
                                                xt[q][:, b * P:(b + 1) * P], kw[:], start=True, stop=True)
                    last.then_inc(h_ready[q], 1)

        @block.vector
        def _(dve):
            nc.vector.memset(rows[0][:], 1.0)
            nc.vector.memset(rows[1][:], 1.0)
            dve.wait_ge(ka_ready, 1)
            nc.vector.tensor_copy(kw[:, D:D + 2], ps_a[:, 0:2]).then_inc(kw_ready, 1)
            dve.wait_ge(kw_ready, 1)
            with dve.Fori(0, NODE_STEPS // 2) as it:
                for q in range(2):
                    dve.wait_ge(h_ready[q], it + 1)
                    dve.wait_ge(stored[q], it * 16)
                    for k in range(3):
                        b0, b1 = 3 * k, min(3 * k + 3, NB)
                        n = b1 - b0
                        taken = ps[q][:, k, 0:n * (D + 2)].rearrange("p (b c) -> p b c", b=n)
                        nc.vector.tensor_copy(rows[q][:, b0:b1, 0:D], taken[:, :, 0:D])
                        last = nc.vector.tensor_copy(rows[q][:, b0:b1, U_COL:V_COL + 1], taken[:, :, D:D + 2])
                    last.then_inc(rows_ready[q], 1)

        @block.scalar
        def _(act):
            with act.Fori(0, NODE_STEPS // 2) as it:
                for q in range(2):
                    act.wait_ge(rows_ready[q], it + 1)
                    act.dma_start(node_rows(hv, it * 2 + q, HW), rows[q][:]).then_inc(stored[q], 16)
            for q in range(2):
                act.wait_ge(stored[q], 16 * (NODE_STEPS // 2))


def attend_any(nc, c, src, dst, hv, tables, landed):
    with ExitStack() as ctx:
        sb = lambda n, s, d=FP32: [ctx.enter_context(nc.sbuf_tensor(f"l0_{n}{q}", s, d)) for q in range(2)]
        sem = lambda n: ctx.enter_context(nc.semaphore("l0_" + n))
        sems = lambda n: [sem(f"{n}{q}") for q in range(2)]
        src_all = ctx.enter_context(nc.sbuf_tensor("l0_src_all", [P, TILES], I32))
        dst_all = ctx.enter_context(nc.sbuf_tensor("l0_dst_all", [P, TILES], I32))
        src_i, dst_i, hi_i, lo_i, to_i = (sb(n, [P, TS], I32) for n in ("src_i", "dst_i", "hi_i", "lo_i", "to_i"))
        src_f, cnt, away, z, zl, zc, w = (sb(n, [P, TS]) for n in ("src_f", "cnt", "away", "z", "zl", "zc", "w"))
        hl = sb("hl", [P, 2, TS], BF16)
        equal = sb("equal", [P, TS, P])
        h_dst, h_src = (sb(n, [P, TS, HW]) for n in ("h_dst", "h_src"))
        hw, sums = (sb(n, [P, TS, SW]) for n in ("hw", "sums"))
        ps_key = ctx.enter_context(nc.psum_tensor("l0_ps_key", [P, TS, P], FP32))
        ps_sum = ctx.enter_context(nc.psum_tensor("l0_ps_sum", [P, 3, 512], FP32))
        ids_in = sem("ids_in")
        ids_ready, halves_ready, keys_ready, equal_ready = (sems(n) for n in ("ids_ready", "halves_ready", "keys_ready", "equal_ready"))
        gathered, clipped, scored, weighted, summed, sums_ready = (
            sems(n) for n in ("gathered", "clipped", "scored", "weighted", "summed", "sums_ready"))
        chain = sem("dve_chain")
        scattered = landed
        block = ctx.enter_context(nc.Block())
        HALF = STEPS // 2
        PER_COPY = 2 * TS // COPIES

        @block.sync
        def _(sp):
            sp.dma_start(src_all[:], src).then_inc(ids_in, 16)
            sp.dma_start(dst_all[:], dst).then_inc(ids_in, 16)
            sp.wait_ge(ids_in, 32)

        @block.gpsimd
        def _(pool):
            with pool.Fori(0, HALF) as it:
                for q in range(2):
                    gate(pool, c, ids_ready[q], it + 1)
                    gate(pool, c, weighted[q], it)
                    for u in range(TS):
                        pool.indirect_dma_start(h_dst[q][:, u, :], None, hv[:, :],
                                                bass.IndirectOffsetOnAxis(dst_i[q][:, u:u + 1], 0)).then_inc(gathered[q], 16)
                        pool.indirect_dma_start(h_src[q][:, u, :], None, hv[:, :],
                                                bass.IndirectOffsetOnAxis(src_i[q][:, u:u + 1], 0)).then_inc(gathered[q], 16)
                for q in range(2):
                    gate(pool, c, sums_ready[q], it + 1)
                    for u in range(TS):
                        k = u % COPIES
                        gate(pool, c, scattered[k], it * (16 * PER_COPY) + 16 * (1 + q * (TS // COPIES) + u // COPIES))
                        pool.indirect_dma_start(tables[k][:, :], bass.IndirectOffsetOnAxis(to_i[q][:, u:u + 1], 0),
                                                sums[q][:, u, :], None, compute_op=ALU.add).then_inc(scattered[k], 16)
            for k in range(COPIES):
                pool.wait_ge(scattered[k], 16 * (1 + HALF * PER_COPY))

        @block.vector
        def _(dve):
            dve.wait_ge(ids_in, 32)
            own = Tally(chain, 2 * 6)
            with dve.Fori(0, HALF) as it:
                own.start(it)
                for q in range(2):
                    cols = bass.ds((it * 2 + q) * TS, TS)
                    dve.wait_ge(gathered[q], it * (32 * TS))
                    nc.vector.tensor_copy(dst_i[q][:], dst_all[:, cols])
                    nc.vector.tensor_copy(src_i[q][:], src_all[:, cols]).then_inc(ids_ready[q], 1)
                    nc.vector.tensor_copy(src_f[q][:], src_all[:, cols])
                    nc.vector.tensor_single_scalar(hi_i[q][:], src_all[:, cols], 7, ALU.arith_shift_right)
                    own.inc(nc.vector.tensor_single_scalar(lo_i[q][:], src_all[:, cols], 127, ALU.bitwise_and))
                    own.wait(dve)
                    nc.vector.tensor_copy(hl[q][:, 0, :], hi_i[q][:])
                    nc.vector.tensor_copy(hl[q][:, 1, :], lo_i[q][:]).then_inc(halves_ready[q], 1)
                for q in range(2):
                    dve.wait_ge(keys_ready[q], it + 1)
                    dve.wait_ge(summed[q], it)
                    for u in range(TS):
                        last = nc.vector.scalar_tensor_tensor(
                            out=equal[q][:, u, :], in0=ps_key[:, u, :], scalar=src_f[q][:, u:u + 1], in1=c["later"][:],
                            op0=ALU.is_equal, op1=ALU.mult, accum_out=cnt[q][:, u:u + 1])
                    last.then_inc(equal_ready[q], 1)
                    own.inc(nc.vector.tensor_scalar(away[q][:], src_f[q][:], c["spare_row"][:, 0:1], None, ALU.subtract))
                    own.wait(dve)
                    dve.wait_ge(equal_ready[q], it + 1)
                    own.inc(nc.vector.scalar_tensor_tensor(out=z[q][:], in0=cnt[q][:], scalar=1.0, in1=away[q][:],
                                                           op0=ALU.is_equal, op1=ALU.mult))
                    own.wait(dve)
                    for k in range(COPIES):
                        dve.wait_ge(scattered[k], it * (16 * PER_COPY) + 16)
                    own.inc(nc.vector.tensor_scalar(to_i[q][:], z[q][:], c["spare_row"][:, 0:1], None, ALU.add))
                    own.wait(dve)
                    dve.wait_ge(gathered[q], it * (32 * TS) + 32 * TS)
                    own.inc(nc.vector.tensor_tensor(z[q][:], h_src[q][:, :, U_COL], h_dst[q][:, :, V_COL], ALU.add))
                    own.wait(dve)
                    own.inc(nc.vector.scalar_tensor_tensor(out=zl[q][:], in0=z[q][:], scalar=0.2, in1=z[q][:],
                                                           op0=ALU.mult, op1=ALU.max))
                    own.wait(dve)
                    nc.vector.tensor_scalar(zc[q][:], zl[q][:], 2.0, -2.0, ALU.min, ALU.max).then_inc(clipped[q], 1)
                own.end()

        @block.tensor
        def _(pe):
            with pe.Fori(0, HALF) as it:
                for q in range(2):
                    pe.wait_ge(halves_ready[q], it + 1)
                    pe.wait_ge(equal_ready[1 - q], it + q)
                    for u in range(TS):
                        nc.tensor.matmul(ps_key[:, u, :], hl[q][:, 0, u:u + 1].to_broadcast([P, P]), c["ident_hi"][:],
                                         start=True, stop=False)
                        last = nc.tensor.matmul(ps_key[:, u, :], hl[q][:, 1, u:u + 1].to_broadcast([P, P]), c["ident_lo"][:],
                                                start=False, stop=True)
                    last.then_inc(keys_ready[q], 1)
                    pe.wait_ge(equal_ready[q], it + 1)
                    pe.wait_ge(weighted[q], it + 1)
                    pe.wait_ge(sums_ready[1 - q], it + q)
                    for u in range(TS):
                        last = nc.tensor.matmul(ps_sum[:, u // 3, (u % 3) * SW:(u % 3 + 1) * SW], equal[q][:, u, :],
                                                hw[q][:, u, :], start=True, stop=True)
                    last.then_inc(summed[q], 1)

        @block.scalar
        def _(act):
            with act.Fori(0, HALF) as it:
                for q in range(2):
                    act.wait_ge(clipped[q], it + 1)
                    nc.scalar.activation(w[q][:], zc[q][:], ACT.Exp).then_inc(scored[q], 1)
                    act.wait_ge(scored[q], it + 1)
                    act.wait_ge(summed[q], it)
                    for u in range(TS):
                        last = nc.scalar.activation(hw[q][:, u, :], h_dst[q][:, u, 0:SW], ACT.Copy, scale=w[q][:, u:u + 1])
                    last.then_inc(weighted[q], 1)
                    act.wait_ge(summed[q], it + 1)
                    for k in range(COPIES):
                        act.wait_ge(scattered[k], it * (16 * PER_COPY) + 16)
                    for k in range(3):
                        u0, u1 = 3 * k, min(3 * k + 3, TS)
                        last = nc.scalar.activation(sums[q][:, u0:u1, :],
                                                    ps_sum[:, k, 0:(u1 - u0) * SW].rearrange("p (u c) -> p u c", u=u1 - u0),
                                                    ACT.Copy)
                    last.then_inc(sums_ready[q], 1)


def update_nodes(nc, c, x, tables, w_in, x1, h1):
    with ExitStack() as ctx:
        sb = lambda n, s, d=FP32: [ctx.enter_context(nc.sbuf_tensor(f"n0_{n}{q}", s, d)) for q in range(2)]
        sem = lambda n: ctx.enter_context(nc.semaphore("n0_" + n))
        sems = lambda n: [sem(f"{n}{q}") for q in range(2)]
        w_sb = ctx.enter_context(nc.sbuf_tensor("n0_w_in_sb", [P, D], FP32))
        part = sb("part", [P, COPIES, NB, SW])
        xs, y, x1s, xT, h1s = (sb(n, [P, NB, D]) for n in ("xs", "y", "x1s", "xT", "h1s"))
        den, rden, std, rstd, shift = (sb(n, [P, NB]) for n in ("den", "rden", "std", "rstd", "shift"))
        stats = sb("stats", [P, NB, 6])
        mv = sb("mv", [P, NB, 2])
        ps_t = ctx.enter_context(nc.psum_tensor("n0_ps_t", [P, 8, P], FP32))
        ps_h = ctx.enter_context(nc.psum_tensor("n0_ps_h", [P, 8, P], FP32))
        w_ready = sem("w_ready")
        loaded, first_added, shift_ready, stored = sems("loaded"), sems("first_added"), sems("shift_ready"), sems("stored")
        var_ready, std_ready, x1_ready, xT_done, xT_ready, h1_done, h1_ready = (
            sems(n) for n in ("var_ready", "std_ready", "x1_ready", "xT_done", "xT_ready", "h1_done", "h1_ready"))
        chain = sem("dve_chain")
        block = ctx.enter_context(nc.Block())
        HALF = NODE_STEPS // 2

        @block.sync
        def _(sp):
            sp.dma_start(w_sb[:], w_in).then_inc(w_ready, 16)
            with sp.Fori(0, HALF) as it:
                for q in range(2):
                    sp.wait_ge(x1_ready[q], it)
                    for k in range(COPIES):
                        sp.dma_start(part[q][:, k], node_rows(tables[k], it * 2 + q, SW)).then_inc(loaded[q], 16)
                    sp.dma_start(xs[q][:], node_rows(x, it * 2 + q, D)).then_inc(loaded[q], 16)

        @block.vector
        def _(dve):
            own = Tally(chain, 2 * 7)
            with dve.Fori(0, HALF) as it:
                own.start(it)
                for q in range(2):
                    dve.wait_ge(loaded[q], it * (16 * (COPIES + 1)) + 16 * (COPIES + 1))
                    own.inc(nc.vector.tensor_tensor(part[q][:, 2], part[q][:, 2], part[q][:, 3], ALU.add))
                    own.wait(dve)
                    dve.wait_ge(first_added[q], it + 1)
                    own.inc(nc.vector.tensor_tensor(part[q][:, 0], part[q][:, 0], part[q][:, 2], ALU.add))
                    own.wait(dve)
                    own.inc(nc.vector.tensor_scalar(den[q][:], part[q][:, 0, :, ONE_COL], 1e-30, None, ALU.max))
                    own.wait(dve)
                    own.inc(nc.vector.reciprocal(rden[q][:], den[q][:]))
                    own.wait(dve)
                    for b in range(NB):
                        last = nc.vector.scalar_tensor_tensor(out=y[q][:, b], in0=part[q][:, 0, b, 0:D],
                                                              scalar=rden[q][:, b:b + 1], in1=xs[q][:, b],
                                                              op0=ALU.mult, op1=ALU.add)
                    own.inc(last)
                    own.wait(dve)
                    for b in range(NB):
                        last = nc.vector.bn_stats(stats[q][:, b], y[q][:, b])
                    own.inc(last)
                    own.wait(dve)
                    dve.sem_inc(c["gates_passed"], 1)
                    for b in range(NB):
                        last = nc.vector.bn_aggr(mv[q][:, b], stats[q][:, b])
                    last.then_inc(var_ready[q], 1)
                    dve.wait_ge(std_ready[q], it + 1)
                    own.inc(nc.vector.reciprocal(rstd[q][:], std[q][:]))
                    own.wait(dve)
                    nc.vector.scalar_tensor_tensor(out=shift[q][:], in0=mv[q][:, :, 0], scalar=-1.0, in1=rstd[q][:],
                                                   op0=ALU.mult, op1=ALU.mult).then_inc(shift_ready[q], 1)
                own.end()

        @block.tensor
        def _(pe):
            pe.wait_ge(w_ready, 16)
            with pe.Fori(0, HALF) as it:
                for q in range(2):
                    pe.wait_ge(x1_ready[q], it + 1)
                    pe.wait_ge(xT_ready[1 - q], it + q)
                    for b in range(NB):
                        last = nc.tensor.transpose(ps_t[:, b, :], x1s[q][:, b], c["ident"][:])
                    last.then_inc(xT_done[q], 1)
                    pe.wait_ge(xT_ready[q], it + 1)
                    pe.wait_ge(h1_ready[1 - q], it + q)
                    for b in range(NB):
                        last = nc.tensor.matmul(ps_h[:, b, :], xT[q][:, b], w_sb[:], start=True, stop=True)
                    last.then_inc(h1_done[q], 1)

        @block.scalar
        def _(act):
            def finish(q, done):
                act.wait_ge(h1_done[q], done)
                for b in (slice(0, 4), slice(4, NB)):
                    last = nc.scalar.activation(h1s[q][:, b], ps_h[:, b], ACT.Copy)
                last.then_inc(h1_ready[q], 1)

            def store(n, q, done):
                act.wait_ge(x1_ready[q], done)
                act.dma_start(node_rows(x1, n, D), x1s[q][:]).then_inc(stored[q], 16)
                act.wait_ge(h1_ready[q], done)
                act.dma_start(node_rows(h1, n, D), h1s[q][:]).then_inc(stored[q], 16)

            def turn(it, first):
                for q in range(2):
                    act.wait_ge(var_ready[q], it + 1)
                    nc.scalar.activation(std[q][:], mv[q][:, :, 1], ACT.Sqrt, bias=c["eps"][:, 0:1]).then_inc(std_ready[q], 1)
                    act.wait_ge(shift_ready[q], it + 1)
                    if not first:
                        act.wait_ge(stored[q], it * 32)
                    for b in range(NB):
                        last = nc.scalar.activation(x1s[q][:, b], y[q][:, b], ACT.Identity, bias=shift[q][:, b:b + 1],
                                                    scale=rstd[q][:, b:b + 1])
                    last.then_inc(x1_ready[q], 1)
                    if not (first and q == 0):
                        done = it + q
                        finish(1 - q, done)
                        store(it * 2 + q - 1, 1 - q, done)
                    act.wait_ge(xT_done[q], it + 1)
                    for b in (slice(0, 4), slice(4, NB)):
                        last = nc.scalar.activation(xT[q][:, b], ps_t[:, b], ACT.Copy)
                    last.then_inc(xT_ready[q], 1)
            turn(0, True)
            with act.Fori(1, HALF) as it:
                turn(it, False)
            finish(1, HALF)
            store(NODE_STEPS - 1, 1, HALF)
            for q in range(2):
                act.wait_ge(stored[q], 32 * HALF)

        @block.gpsimd
        def _(pool):
            with pool.Fori(0, HALF) as it:
                for q in range(2):
                    pool.wait_ge(loaded[q], it * (16 * (COPIES + 1)) + 16 * (COPIES + 1))
                    pool.tensor_tensor(part[q][:, 0], part[q][:, 0], part[q][:, 1], ALU.add).then_inc(first_added[q], 1)


def convolve_any(nc, c, src_all, dst, weight, attr, w1, b1, w2, b2, h1, tables, landed):
    with ExitStack() as ctx:
        sb = lambda n, s, d=FP32: [ctx.enter_context(nc.sbuf_tensor(f"l1_{n}{q}", s, d)) for q in range(2)]
        one = lambda n, s, d=FP32: ctx.enter_context(nc.sbuf_tensor("l1_" + n, s, d))
        sem = lambda n: ctx.enter_context(nc.semaphore("l1_" + n))
        sems = lambda n: [sem(f"{n}{q}") for q in range(2)]
        dst_all = one("dst_all", [P, TILES], I32)
        cut = one("cut", [P, TILES])
        turns = one("turns", [P, TILES])
        w1_sb, w2_sb, b1_sb = one("w1_sb", [P, D]), one("w2_sb", [P, D]), one("b1_sb", [P, 1])
        b2_row, ones = one("b2_row", [1, D]), one("ones", [1, P])
        src_i, dst_i, hi_i, lo_i, to_i = (sb(n, [P, TS], I32) for n in ("src_i", "dst_i", "hi_i", "lo_i", "to_i"))
        dst_f, cnt, away, z, cut_s = (sb(n, [P, TS]) for n in ("dst_f", "cnt", "away", "z", "cut_s"))
        hl = sb("hl", [P, 2, TS], BF16)
        equal, h_src, msg, sums = (sb(n, [P, TS, P]) for n in ("equal", "h_src", "msg", "sums"))
        at, hid = sb("at", [P, TS * P // 2]), sb("hid", [P, TS, P])
        ps_key = ctx.enter_context(nc.psum_tensor("l1_ps_key", [P, TS, P], FP32))
        ps_hid = ctx.enter_context(nc.psum_tensor("l1_ps_hid", [P, TS, P], FP32))
        ps_f = ctx.enter_context(nc.psum_tensor("l1_ps_f", [P, TS, P], FP32))
        ps_sum = ctx.enter_context(nc.psum_tensor("l1_ps_sum", [P, TS, P], FP32))
        ids_in, weights_in, cut_ready, ones_ready = sem("ids_in"), sem("weights_in"), sem("cut_ready"), sem("ones_ready")
        ids_ready, halves_ready, keys_ready, equal_ready, attr_in = (
            sems(n) for n in ("ids_ready", "halves_ready", "keys_ready", "equal_ready", "attr_in"))
        gathered, hid_done, hid_ready, filtered, msg_ready, summed, sums_ready = (
            sems(n) for n in ("gathered", "hid_done", "hid_ready", "filtered", "msg_ready", "summed", "sums_ready"))
        pre, chain = sem("dve_pre"), sem("dve_chain")
        scattered = landed
        block = ctx.enter_context(nc.Block())
        HALF = STEPS // 2
        PER_COPY = 2 * TS // COPIES

        @block.sync
        def _(sp):
            sp.dma_start(dst_all[:], dst).then_inc(ids_in, 16)
            sp.dma_start(cut[:], weight).then_inc(ids_in, 16)
            for tile, array in ((w1_sb[:], w1), (w2_sb[:], w2), (b1_sb[:], b1), (b2_row[:], b2)):
                sp.dma_start(tile, array).then_inc(weights_in, 16)
            sp.wait_ge(weights_in, 64)
            with sp.Fori(0, HALF) as it:
                for q in range(2):
                    sp.wait_ge(hid_done[q], it)
                    sp.dma_start(at[q][:], attr[bass.ds((it * 2 + q) * P, P), :]).then_inc(attr_in[q], 16)

        @block.gpsimd
        def _(pool):
            with pool.Fori(0, HALF) as it:
                for q in range(2):
                    gate(pool, c, ids_ready[q], it + 1)
                    gate(pool, c, msg_ready[q], it)
                    for u in range(TS):
                        pool.indirect_dma_start(h_src[q][:, u, :], None, h1[:, :],
                                                bass.IndirectOffsetOnAxis(src_i[q][:, u:u + 1], 0)).then_inc(gathered[q], 16)
                for q in range(2):
                    gate(pool, c, sums_ready[q], it + 1)
                    for u in range(TS):
                        k = u % COPIES
                        gate(pool, c, scattered[k], it * (16 * PER_COPY) + 16 * (1 + q * (TS // COPIES) + u // COPIES))
                        pool.indirect_dma_start(tables[k][:, :], bass.IndirectOffsetOnAxis(to_i[q][:, u:u + 1], 0),
                                                sums[q][:, u, :], None, compute_op=ALU.add).then_inc(scattered[k], 16)
            for k in range(COPIES):
                pool.wait_ge(scattered[k], 16 * (1 + HALF * PER_COPY))

        @block.vector
        def _(dve):
            dve.wait_ge(ids_in, 32)
            nc.vector.tensor_scalar(turns[:], cut[:], 1 / (2 * CUTOFF), ROUND, ALU.mult, ALU.add).then_inc(pre, 1)
            dve.wait_ge(pre, 1)
            nc.vector.tensor_scalar(turns[:], turns[:], ROUND, -2 * CUTOFF, ALU.subtract, ALU.mult).then_inc(pre, 1)
            dve.wait_ge(pre, 2)
            nc.vector.tensor_tensor(turns[:], turns[:], cut[:], ALU.add).then_inc(pre, 1)
            dve.wait_ge(pre, 3)
            nc.vector.scalar_tensor_tensor(out=turns[:], in0=turns[:], scalar=-1.0, in1=turns[:],
                                           op0=ALU.mult, op1=ALU.max).then_inc(pre, 1)
            dve.wait_ge(cut_ready, 1)
            nc.vector.tensor_scalar(cut[:], turns[:], 0.5, 0.5, ALU.mult, ALU.add).then_inc(pre, 1)
            nc.vector.memset(ones[:], 1.0).then_inc(ones_ready, 1)
            dve.wait_ge(pre, 5)
            own = Tally(chain, 2 * 4)
            with dve.Fori(0, HALF) as it:
                own.start(it)
                for q in range(2):
                    cols = bass.ds((it * 2 + q) * TS, TS)
                    dve.wait_ge(gathered[q], it * (16 * TS))
                    nc.vector.tensor_copy(src_i[q][:], src_all[:, cols]).then_inc(ids_ready[q], 1)
                    nc.vector.tensor_copy(dst_f[q][:], dst_all[:, cols])
                    nc.vector.tensor_copy(cut_s[q][:], cut[:, cols])
                    nc.vector.tensor_single_scalar(hi_i[q][:], dst_all[:, cols], 7, ALU.arith_shift_right)
                    own.inc(nc.vector.tensor_single_scalar(lo_i[q][:], dst_all[:, cols], 127, ALU.bitwise_and))
                    own.wait(dve)
                    nc.vector.tensor_copy(hl[q][:, 0, :], hi_i[q][:])
                    nc.vector.tensor_copy(hl[q][:, 1, :], lo_i[q][:]).then_inc(halves_ready[q], 1)
                for q in range(2):
                    dve.wait_ge(keys_ready[q], it + 1)
                    dve.wait_ge(summed[q], it)
                    for u in range(TS):
                        last = nc.vector.scalar_tensor_tensor(
                            out=equal[q][:, u, :], in0=ps_key[:, u, :], scalar=dst_f[q][:, u:u + 1], in1=c["later"][:],
                            op0=ALU.is_equal, op1=ALU.mult, accum_out=cnt[q][:, u:u + 1])
                    last.then_inc(equal_ready[q], 1)
                    own.inc(nc.vector.tensor_scalar(away[q][:], dst_f[q][:], c["spare_row"][:, 0:1], None, ALU.subtract))
                    own.wait(dve)
                    dve.wait_ge(equal_ready[q], it + 1)
                    own.inc(nc.vector.scalar_tensor_tensor(out=z[q][:], in0=cnt[q][:], scalar=1.0, in1=away[q][:],
                                                           op0=ALU.is_equal, op1=ALU.mult))
                    own.wait(dve)
                    for k in range(COPIES):
                        dve.wait_ge(scattered[k], it * (16 * PER_COPY) + 16)
                    own.inc(nc.vector.tensor_scalar(to_i[q][:], z[q][:], c["spare_row"][:, 0:1], None, ALU.add))
                    own.wait(dve)
                    dve.wait_ge(gathered[q], it * (16 * TS) + 16 * TS)
                    dve.wait_ge(filtered[q], it + 1)
                    for u in range(TS):
                        last = nc.vector.scalar_tensor_tensor(out=msg[q][:, u], in0=ps_f[:, u], scalar=cut_s[q][:, u:u + 1],
                                                              in1=h_src[q][:, u], op0=ALU.mult, op1=ALU.mult)
                    last.then_inc(msg_ready[q], 1)
                own.end()

        @block.tensor
        def _(pe):
            pe.wait_ge(weights_in, 64)
            pe.wait_ge(ones_ready, 1)
            with pe.Fori(0, HALF) as it:
                for q in range(2):
                    pe.wait_ge(halves_ready[q], it + 1)
                    pe.wait_ge(equal_ready[1 - q], it + q)
                    for u in range(TS):
                        nc.tensor.matmul(ps_key[:, u, :], hl[q][:, 0, u:u + 1].to_broadcast([P, P]), c["ident_hi"][:],
                                         start=True, stop=False)
                        last = nc.tensor.matmul(ps_key[:, u, :], hl[q][:, 1, u:u + 1].to_broadcast([P, P]), c["ident_lo"][:],
                                                start=False, stop=True)
                    last.then_inc(keys_ready[q], 1)
                    pe.wait_ge(attr_in[q], it * 16 + 16)
                    pe.wait_ge(hid_ready[1 - q], it + q)
                    for half in range(2):
                        rows = slice(half * RBF_ROWS, half * RBF_ROWS + RBF_ROWS)
                        last = nc.tensor.matmul(ps_hid[:, half * 4:half * 4 + 4, :].rearrange("p u c -> p (u c)"),
                                                w1_sb[rows, :], at[q][rows, :], start=True, stop=True)
                    last.then_inc(hid_done[q], 1)
                    pe.wait_ge(hid_ready[q], it + 1)
                    pe.wait_ge(msg_ready[1 - q], it + q)
                    for u in range(TS):
                        nc.tensor.matmul(ps_f[:, u, :], ones[:], b2_row[:], start=True, stop=False)
                        last = nc.tensor.matmul(ps_f[:, u, :], hid[q][:, u, :], w2_sb[:], start=False, stop=True)
                    last.then_inc(filtered[q], 1)
                    pe.wait_ge(equal_ready[q], it + 1)
                    pe.wait_ge(msg_ready[q], it + 1)
                    pe.wait_ge(sums_ready[1 - q], it + q)
                    for u in range(TS):
                        last = nc.tensor.matmul(ps_sum[:, u, :], equal[q][:, u, :], msg[q][:, u, :], start=True, stop=True)
                    last.then_inc(summed[q], 1)

        @block.scalar
        def _(act):
            act.wait_ge(weights_in, 64)
            act.wait_ge(pre, 4)
            nc.scalar.activation(turns[:], turns[:], ACT.Sin, bias=c["half_pi"][:, 0:1], scale=-PI / CUTOFF).then_inc(cut_ready, 1)
            with act.Fori(0, HALF) as it:
                for q in range(2):
                    act.wait_ge(hid_done[q], it + 1)
                    act.wait_ge(filtered[q], it)
                    for half in range(2):
                        last = nc.scalar.activation(hid[q][:, half * 4:half * 4 + 4], ps_hid[:, half * 4:half * 4 + 4],
                                                    ACT.Tanh, bias=b1_sb[:, 0:1])
                    last.then_inc(hid_ready[q], 1)
                    act.wait_ge(summed[q], it + 1)
                    for k in range(COPIES):
                        act.wait_ge(scattered[k], it * (16 * PER_COPY) + 16)
                    for half in range(2):
                        last = nc.scalar.activation(sums[q][:, half * 4:half * 4 + 4], ps_sum[:, half * 4:half * 4 + 4],
                                                    ACT.Copy)
                    last.then_inc(sums_ready[q], 1)


def number_edges(nc, c, src, dst, dst_steps, weight, e):
    SP_ = STEPS // 4
    with ExitStack() as ctx:
        one = lambda n, s, d=FP32: ctx.enter_context(nc.sbuf_tensor("ne_" + n, s, d))
        sem = lambda n: ctx.enter_context(nc.semaphore("ne_" + n))
        dst_i, half_i = one("dst_i", [P, TILES], I32), one("half_i", [P, TILES], I32)
        steps_i = one("steps_i", [SP_, 4, TS * P], I32)
        low, high, span = one("low", [SP_, 4]), one("high", [SP_, 4]), one("span", [SP_, 4])
        base_i = one("base_i", [SP_, 4], I32)
        base_all = one("base_all", [P, STEPS], I32)
        span_row, widest = one("span_row", [1, STEPS]), one("widest", [1, 1])
        turns, cut = one("turns", [P, TILES]), one("cut", [P, TILES])
        span_d = nc.dram_tensor("span_d", [STEPS], FP32, kind="Internal")
        ids_in, steps_in, weight_in = sem("ids_in"), sem("steps_in"), sem("weight_in")
        based, base_stored, base_back = sem("based"), sem("base_stored"), sem("base_back")
        turned, cosine, done = sem("turned"), sem("cosine"), sem("dve_done")
        block = ctx.enter_context(nc.Block())

        @block.sync
        def _(sp):
            sp.dma_start(steps_i[:], dst_steps).then_inc(steps_in, 16)
            sp.dma_start(e["src_i"][:], src).then_inc(ids_in, 16)
            sp.dma_start(dst_i[:], dst).then_inc(ids_in, 16)
            sp.dma_start(cut[:], weight).then_inc(weight_in, 16)
            sp.wait_ge(based, 1)
            sp.dma_start(e["base_d"][:].rearrange("(p c) -> p c", c=4), base_i[:]).then_inc(base_stored, 16)
            sp.dma_start(span_d[:].rearrange("(p c) -> p c", c=4), span[:]).then_inc(base_stored, 16)
            sp.wait_ge(base_stored, 32)
            sp.dma_start(e["base_row"][:], e["base_d"][:].unsqueeze(0)).then_inc(base_back, 16)
            sp.dma_start(base_all[:], e["base_d"][:].unsqueeze(0).to_broadcast([P, STEPS])).then_inc(base_back, 16)
            sp.dma_start(span_row[:], span_d[:].unsqueeze(0)).then_inc(base_back, 16)

        @block.vector
        def _(dve):
            n = 0

            def then(instruction, wait=True):
                nonlocal n
                n += 1
                instruction.then_inc(done, 1)
                if wait:
                    dve.wait_ge(done, n)

            dve.wait_ge(steps_in, 16)
            then(nc.vector.tensor_reduce(low[:], steps_i[:], mybir.AxisListType.X, ALU.min), False)
            then(nc.vector.tensor_reduce(high[:], steps_i[:], mybir.AxisListType.X, ALU.max))
            then(nc.vector.tensor_scalar(low[:], low[:], float(NODES_P - WIN), None, ALU.min))
            then(nc.vector.tensor_tensor(span[:], high[:], low[:], ALU.subtract), False)
            nc.vector.tensor_copy(base_i[:], low[:]).then_inc(based, 1)
            dve.wait_ge(ids_in, 32)
            nc.vector.tensor_copy(e["key_f"][:, :, 0], e["src_i"][:])
            nc.vector.tensor_scalar(e["key_f"][:, :, 2], e["src_i"][:], c["spare_row"][:, 0:1], None, ALU.subtract)
            then(nc.vector.tensor_single_scalar(half_i[:], e["src_i"][:], 6, ALU.arith_shift_right))
            nc.vector.tensor_copy(e["key_f"][:, :, 1], half_i[:])
            then(nc.vector.tensor_copy(e["key_b"][:, :, 2], half_i[:]))
            then(nc.vector.tensor_single_scalar(half_i[:], e["src_i"][:], HALF_P - 1, ALU.bitwise_and))
            then(nc.vector.tensor_copy(e["key_b"][:, :, 1], half_i[:]))
            dve.wait_ge(weight_in, 16)
            then(nc.vector.tensor_scalar(turns[:], cut[:], 1 / (2 * CUTOFF), ROUND, ALU.mult, ALU.add))
            then(nc.vector.tensor_scalar(turns[:], turns[:], ROUND, -2 * CUTOFF, ALU.subtract, ALU.mult))
            then(nc.vector.tensor_tensor(turns[:], turns[:], cut[:], ALU.add))
            nc.vector.scalar_tensor_tensor(out=turns[:], in0=turns[:], scalar=-1.0, in1=turns[:],
                                           op0=ALU.mult, op1=ALU.max).then_inc(turned, 1)
            dve.wait_ge(base_back, 48)
            base_of = base_all[:].unsqueeze(2).to_broadcast([P, STEPS, TS])
            then(nc.vector.tensor_tensor(e["out_f"][:, :, 0].rearrange("p (s u) -> p s u", u=TS),
                                         dst_i[:].rearrange("p (s u) -> p s u", u=TS), base_of, ALU.subtract))
            nc.vector.tensor_copy(e["key_b"][:, :, 0], e["out_f"][:, :, 0])
            then(nc.vector.tensor_reduce(widest[:], span_row[:], mybir.AxisListType.X, ALU.max))
            then(nc.vector.tensor_scalar(e["fits"][:], widest[:], float(WIN), None, ALU.is_lt))
            dve.wait_ge(cosine, 1)
            nc.vector.tensor_scalar(e["out_f"][:, :, 1], turns[:], 0.5, 0.5, ALU.mult, ALU.add)

        @block.scalar
        def _(act):
            act.wait_ge(turned, 1)
            nc.scalar.activation(turns[:], turns[:], ACT.Sin, bias=c["half_pi"][:, 0:1], scale=-PI / CUTOFF).then_inc(cosine, 1)


def project_parts(nc, c, xT, kernel, kernelT, att, parts_d, u_parts, tables, landed):
    with ExitStack() as ctx:
        sb = lambda n, s, d=FP32: ctx.enter_context(nc.sbuf_tensor("pp_" + n, s, d))
        sem = lambda n: ctx.enter_context(nc.semaphore("pp_" + n))
        kw, kT, att_sb = sb("kw", [P, D + 2]), sb("kT", [P, D]), sb("att_sb", [P, 2])
        xt = [sb(f"xt{q}", [P, NB * P]) for q in range(2)]
        rows = [sb(f"rows{q}", [P, NB, 3, PW], BF16) for q in range(2)]
        rest, rest2 = ([sb(f"{n}{q}", [P, NB, D + 2]) for q in range(2)] for n in ("rest", "rest2"))
        u_all = sb("u_all", [P, 3, NODE_BLOCKS], BF16)
        u_low = sb("u_low", [P, 3, NODE_BLOCKS], BF16)
        one_hot = sb("one_hot", [P, NB, 3], BF16)
        ps_a = ctx.enter_context(nc.psum_tensor("pp_ps_a", [P, 512], FP32))
        ps = [ctx.enter_context(nc.psum_tensor(f"pp_ps_h{q}", [P, 3, 512], FP32)) for q in range(2)]
        weights_in, ka_ready, kw_ready = sem("weights_in"), sem("ka_ready"), sem("kw_ready")
        xt_in, stored = ([sem(f"{n}{q}") for q in range(2)] for n in ("xt_in", "stored"))
        h_ready, outer_ready, rest_ready, rest2_ready, rows_ready, u_taken = (
            sem(n) for n in ("h_ready", "outer_ready", "rest_ready", "rest2_ready", "rows_ready", "u_taken"))
        second_ready, moved = sem("second_ready"), sem("moved")
        block = ctx.enter_context(nc.Block())
        TURNS = NODE_STEPS // 2
        BANKS = [(0, 3), (3, 6), (6, 7)]

        @block.sync
        def _(sp):
            sp.dma_start(kw[:, 0:D], kernel).then_inc(weights_in, 16)
            sp.dma_start(kT[:], kernelT).then_inc(weights_in, 16)
            sp.dma_start(att_sb[:], att).then_inc(weights_in, 16)

            def load(n, q):
                sp.dma_start(xt[q][:], xT[:, bass.ds(n * (NB * P), NB * P)]).then_inc(xt_in[q], 16)

            def store(n, q):
                sp.wait_ge(rows_ready, n + 1)
                sp.dma_start(parts_d[bass.ds(n * (NB * P), NB * P), :].rearrange("(b p) x -> p b x", p=P),
                             rows[q][:].rearrange("p b k x -> p b (k x)")).then_inc(stored[q], 16)
            for q in range(2):
                load(q, q)
            with sp.Fori(0, TURNS - 1) as it:
                for q in range(2):
                    store(it * 2 + q, q)
                    load(it * 2 + q + 2, q)
            for q in range(2):
                store(NODE_STEPS - 2 + q, q)
            for q in range(2):
                sp.wait_ge(stored[q], 16 * TURNS)
            sp.wait_ge(u_taken, NODE_STEPS + 1)
            sp.dma_start(u_low[HALF_P:P], u_all[0:HALF_P]).then_inc(moved, 16)
            sp.wait_ge(moved, 16)

        @block.tensor
        def _(pe):
            pe.wait_ge(weights_in, 48)
            nc.tensor.matmul(ps_a[:, 0:2], kT[:], att_sb[:], start=True, stop=True).then_inc(ka_ready, 1)
            pe.wait_ge(kw_ready, 1)
            with pe.Fori(0, TURNS) as it:
                for q in range(2):
                    n = it * 2 + q
                    pe.wait_ge(xt_in[q], it * 16 + 16)
                    if q == 0:
                        pe.wait_ge(rest_ready, n)
                    else:
                        pe.wait_ge(rest_ready, n - 1)
                    for b in range(NB):
                        last = nc.tensor.matmul(ps[q][:, b // 3, (b % 3) * (D + 2):(b % 3 + 1) * (D + 2)],
                                                xt[q][:, b * P:(b + 1) * P], kw[:], start=True, stop=True)
                    last.then_inc(h_ready, 1)

        def product(q, k):
            b0, b1 = BANKS[k]
            return ps[q][:, k, 0:(b1 - b0) * (D + 2)].rearrange("p (b x) -> p b x", b=b1 - b0)

        @block.scalar
        def _(act):
            with act.Fori(0, TURNS) as it:
                for q in range(2):
                    n = it * 2 + q
                    act.wait_ge(h_ready, n + 1)
                    act.wait_ge(stored[q], it * 16)
                    for k, (b0, b1) in enumerate(BANKS):
                        last = nc.scalar.activation(rows[q][:, b0:b1, 0, :], product(q, k), ACT.Copy)
                    last.then_inc(outer_ready, 1)
                    act.wait_ge(rest2_ready, n + 1)
                    nc.scalar.activation(rows[q][:, :, 2, :], rest2[q][:], ACT.Copy).then_inc(outer_ready, 1)

        @block.vector
        def _(dve):
            nc.vector.memset(one_hot[:], 0.0).then_inc(second_ready, 1)
            dve.wait_ge(second_ready, 1)
            nc.vector.memset(one_hot[:, :, 0], 1.0).then_inc(u_taken, 1)
            dve.wait_ge(ka_ready, 1)
            nc.vector.tensor_copy(kw[:, D:D + 2], ps_a[:, 0:2]).then_inc(kw_ready, 1)
            with dve.Fori(0, TURNS) as it:
                for q in range(2):
                    n = it * 2 + q
                    dve.wait_ge(outer_ready, n * 2 + 1)
                    for k, (b0, b1) in enumerate(BANKS):
                        last = nc.vector.tensor_tensor(rest[q][:, b0:b1], product(q, k), rows[q][:, b0:b1, 0, :], ALU.subtract)
                    last.then_inc(rest_ready, 1)
                    dve.wait_ge(rest_ready, n + 1)
                    nc.vector.tensor_copy(rows[q][:, :, 1, :], rest[q][:]).then_inc(second_ready, 1)
                    dve.wait_ge(second_ready, n + 2)
                    nc.vector.tensor_tensor(rest2[q][:], rest[q][:], rows[q][:, :, 1, :], ALU.subtract).then_inc(rest2_ready, 1)
                    dve.wait_ge(outer_ready, n * 2 + 2)
                    nc.vector.tensor_copy(u_all[:, :, bass.ds(n * NB, NB)],
                                          rows[q][:, :, :, D].rearrange("p b k -> p k b")).then_inc(u_taken, 1)
                    dve.wait_ge(u_taken, n + 2)
                    nc.vector.tensor_copy(rows[q][:, :, :, D], one_hot[:]).then_inc(rows_ready, 1)
            upper = slice(HALF_P, P)
            for k in range(3):
                by_half = u_parts[upper, k, :].rearrange("p (b h) -> p b h", h=2)
                nc.vector.tensor_copy(by_half[:, :, 1], u_all[upper, k, :])
            dve.wait_ge(moved, 16)
            for k in range(3):
                by_half = u_parts[upper, k, :].rearrange("p (b h) -> p b h", h=2)
                nc.vector.tensor_copy(by_half[:, :, 0], u_low[upper, k, :])

        @block.gpsimd
        def _(pool):
            pool.memset(u_parts[0:HALF_P], 0.0)
            for k in range(COPIES):
                pool.wait_ge(rows_ready, k * (NODE_STEPS // COPIES) + 1)
                fill(pool, tables[k:k + 1], c["zeros"], landed[k:k + 1])


def reached(engine, sem, value):
    if not (isinstance(value, int) and value < 1):
        engine.wait_ge(sem, value)


def attend(nc, c, e, u_parts, parts_d, tables, landed):
    with ExitStack() as ctx:
        one = lambda n, s, d=FP32: ctx.enter_context(nc.sbuf_tensor("at_" + n, s, d))
        two = lambda n, s, d=FP32: [one(f"{n}{q}", s, d) for q in range(2)]
        four = lambda n, s, d=FP32: [one(f"{n}{j}", s, d) for j in range(4)]
        sem = lambda n: ctx.enter_context(nc.semaphore("at_" + n))
        psum = lambda n, s: ctx.enter_context(nc.psum_tensor("at_" + n, s, FP32))
        key_f, key_b = two("key_f", [P, TS, 3]), two("key_b", [P, TS, 3], BF16)
        window = two("window", [P, 3, PW], BF16)
        distance = one("distance", [P, UNIT * P])
        place = two("place", [P, UNIT * P], BF16)
        equal = four("equal", [P, UNIT, P])
        masked = one("masked", [P, UNIT, HALF_BLOCKS], BF16)
        count, u, z, zl, zc, score, away = (two(n, [P, UNIT]) for n in ("count", "u", "z", "zl", "zc", "score", "away"))
        scored_rows = two("scored_rows", [P, UNIT, SW])
        to_i, sums = four("to_i", [P, UNIT], I32), four("sums", [P, UNIT, SW])
        ps_place, ps_src = psum("ps_place", [P, 512]), psum("ps_src", [P, 512])
        ps_u, ps_rows, ps_sum = psum("ps_u", [P, 2, 512]), psum("ps_rows", [P, 2, 512]), psum("ps_sum", [P, 2, 512])
        keys_ready, places_done, srcs_done, distance_ready, place_ready, equal_ready, u_done, rows_done = (
            sem(n) for n in ("keys_ready", "places_done", "srcs_done", "distance_ready", "place_ready", "equal_ready",
                             "u_done", "rows_done"))
        u_taken, clipped, scored, rows_scored, sums_done, sums_ready, to_ready = (
            sem(n) for n in ("u_taken", "clipped", "scored", "rows_scored", "sums_done", "sums_ready", "to_ready"))
        window_in = [sem(f"window_in{q}") for q in range(2)]
        chain = sem("dve_chain")
        scattered = landed
        block = ctx.enter_context(nc.Block())
        TURNS = STEPS // 2
        UNITS = TURNS * 4

        def tile_at(ps, t, width, per_bank):
            return ps[:, t // per_bank, (t % per_bank) * width:(t % per_bank + 1) * width]

        def is_unit(n):
            return not isinstance(n, int) or 0 <= n < UNITS

        def over_turns(engine, turn):
            for n in range(8):
                turn(n // 4, n, n % 4)
            with engine.Fori(2, TURNS - 1) as it:
                for j in range(4):
                    turn(it, it * 4 + j, j)
            for n in range(UNITS - 4, UNITS + 3):
                turn(n // 4, n, n % 4)

        def unit_scattered(engine, n):
            if is_unit(n):
                for t in range(UNIT):
                    engine.wait_ge(scattered[t], n * 16 + 32)

        @block.sync
        def _(sp):
            def load(step, q):
                base = sp.value_load(e["base_row"][0:1, bass.ds(step, 1)], min_val=0, max_val=NODES_P - WIN)
                reached(sp, rows_done, step * 2 - 2)
                sp.dma_start(window[q][0:WIN].rearrange("p k x -> p (k x)"), parts_d[bass.ds(base, WIN), :]).then_inc(window_in[q], 16)
            sp.wait_ge(chain, 1)
            for q in range(2):
                load(q, q)
            with sp.Fori(1, TURNS) as it:
                for q in range(2):
                    load(it * 2 + q, q)

        @block.gpsimd
        def _(pool):
            with pool.Fori(0, TURNS) as it:
                for j in range(4):
                    gate(pool, c, to_ready, it * 4 + j + 1)
                    gate(pool, c, sums_ready, it * 4 + j + 1)
                    for t in range(UNIT):
                        gate(pool, c, scattered[t], it * 64 + 16 * (j + 1))
                        pool.indirect_dma_start(tables[t][:, :], bass.IndirectOffsetOnAxis(to_i[j][:, t:t + 1], 0),
                                                sums[j][:, t, :], None, compute_op=ALU.add).then_inc(scattered[t], 16)
            for t in range(UNIT):
                pool.wait_ge(scattered[t], 16 * (1 + UNITS))

        @block.vector
        def _(dve):
            def take_keys(step, q):
                nc.vector.tensor_copy(key_f[q][:], e["key_f"][:, bass.ds(step * TS, TS), :])
                nc.vector.tensor_copy(key_b[q][:], e["key_b"][:, bass.ds(step * TS, TS), :]).then_inc(keys_ready, 1)

            def equals(n, j, tiles):
                for t in tiles:
                    last = nc.vector.scalar_tensor_tensor(
                        out=equal[j][:, t, :], in0=ps_src[:, t * P:(t + 1) * P],
                        scalar=key_f[j // 2][:, (j % 2) * UNIT + t, 0:1], in1=c["later"][:],
                        op0=ALU.is_equal, op1=ALU.mult, accum_out=count[j % 2][:, t:t + 1])
                return last

            def turn(it, n, j):
                q, r, t0 = j % 2, j // 2, (j % 2) * UNIT
                m, i, o = n - 1, (j - 1) % 4, 1 - q
                if is_unit(n):
                    dve.wait_ge(srcs_done, n + 1)
                    reached(dve, sums_done, n - 3)
                    equals(n, j, (0, 1))
                if is_unit(m):
                    dve.wait_ge(u_taken, m + 1)
                    dve.wait_ge(rows_done, m + 1)
                    for bank, tiles in enumerate((slice(0, 3), slice(3, 4))):
                        v = ps_rows[:, bank, 0:(tiles.stop - tiles.start) * PW].rearrange("p (t x) -> p t x", x=PW)[:, :, D + 1]
                        last = nc.vector.tensor_tensor(z[o][:, tiles], v, u[o][:, tiles], ALU.add)
                    last.then_inc(chain, 1)
                if is_unit(n):
                    equals(n, j, (2, 3)).then_inc(equal_ready, 1)
                if is_unit(m):
                    dve.wait_ge(chain, m * 3 + 2)
                    nc.vector.scalar_tensor_tensor(out=zl[o][:], in0=z[o][:], scalar=0.2, in1=z[o][:],
                                                   op0=ALU.mult, op1=ALU.max).then_inc(chain, 1)
                    dve.wait_ge(equal_ready, m + 1)
                    nc.vector.scalar_tensor_tensor(
                        out=away[o][:], in0=count[o][:], scalar=1.0,
                        in1=key_f[i // 2][:, (i % 2) * UNIT:(i % 2 + 1) * UNIT, 2],
                        op0=ALU.is_equal, op1=ALU.mult).then_inc(chain, 1)
                    dve.wait_ge(chain, m * 3 + 3)
                    nc.vector.tensor_scalar(zc[o][:], zl[o][:], 2.0, -2.0, ALU.min, ALU.max).then_inc(clipped, 1)
                    dve.wait_ge(chain, m * 3 + 4)
                if is_unit(n):
                    if j % 2 == 0 and is_unit(n + 2):
                        take_keys(it * 2 + r + 1, 1 - r)
                    dve.wait_ge(u_done, n + 1)
                    for t in range(UNIT):
                        last = nc.vector.scalar_tensor_tensor(
                            out=masked[:, t, :], in0=c["block_no"][:], scalar=key_f[r][:, t0 + t, 1:2],
                            in1=tile_at(ps_u, t, HALF_BLOCKS, 2), op0=ALU.is_equal, op1=ALU.mult,
                            accum_out=u[q][:, t:t + 1])
                    last.then_inc(u_taken, 1)
                if is_unit(m):
                    unit_scattered(dve, n - 5)
                    nc.vector.tensor_scalar(to_i[i][:], away[o][:], c["spare_row"][:, 0:1], None, ALU.add).then_inc(to_ready, 1)

            nc.vector.memset(window[0][WIN:P], 0.0)
            nc.vector.memset(window[1][WIN:P], 0.0).then_inc(chain, 1)
            take_keys(0, 0)
            over_turns(dve, turn)

        @block.tensor
        def _(pe):
            def key_of(r, t, k, partitions):
                return key_b[r][:, t, k:k + 1].to_broadcast([P, partitions])

            def places(n, j):
                reached(pe, distance_ready, n)
                for t in range(UNIT):
                    for k in range(2):
                        last = nc.tensor.matmul(ps_place[k * HALF_P:(k + 1) * HALF_P, t * P:(t + 1) * P],
                                                key_of(j // 2, (j % 2) * UNIT + t, k, HALF_P), c["ident_lo"][:],
                                                start=True, stop=True)
                last.then_inc(places_done, 1)

            def srcs(n, j):
                reached(pe, equal_ready, n)
                for t in range(UNIT):
                    cols, tile = slice(t * P, (t + 1) * P), (j % 2) * UNIT + t
                    nc.tensor.matmul(ps_src[:, cols], key_of(j // 2, tile, 2, P), c["ident_half"][:], start=True, stop=False)
                    last = nc.tensor.matmul(ps_src[:, cols], key_of(j // 2, tile, 1, P), c["ident_lo"][:], start=False, stop=True)
                last.then_inc(srcs_done, 1)

            def turn(it, n, j):
                q, r = j % 2, j // 2
                if is_unit(n + 1):
                    if j % 2:
                        pe.wait_ge(keys_ready, it * 2 + r + 2)
                    places(n + 1, (j + 1) % 4)
                if is_unit(n):
                    pe.wait_ge(place_ready, n + 1)
                    reached(pe, u_taken, n)
                    for t in range(UNIT):
                        for k in range(3):
                            last = nc.tensor.matmul(tile_at(ps_u, t, HALF_BLOCKS, 2), place[q][:, t * P:(t + 1) * P],
                                                    u_parts[:, k, :], start=k == 0, stop=k == 2)
                    last.then_inc(u_done, 1)
                if is_unit(n - 2):
                    pe.wait_ge(rows_scored, n - 1)
                    reached(pe, sums_ready, n - 2)
                    for t in range(UNIT):
                        last = nc.tensor.matmul(tile_at(ps_sum, t, SW, 3), equal[(j + 2) % 4][:, t, :],
                                                scored_rows[q][:, t, :], start=True, stop=True)
                    last.then_inc(sums_done, 1)
                if is_unit(n + 1):
                    srcs(n + 1, (j + 1) % 4)
                if is_unit(n):
                    if j % 2 == 0:
                        pe.wait_ge(window_in[r], it * 16 + 16)
                    reached(pe, rows_scored, n)
                    for t in range(UNIT):
                        for k in range(3):
                            last = nc.tensor.matmul(tile_at(ps_rows, t, PW, 3), place[q][:, t * P:(t + 1) * P],
                                                    window[r][:, k, :], start=k == 0, stop=k == 2)
                    last.then_inc(rows_done, 1)

            pe.wait_ge(chain, 1)
            pe.wait_ge(keys_ready, 1)
            places(0, 0)
            srcs(0, 0)
            over_turns(pe, turn)

        @block.scalar
        def _(act):
            def measure(n):
                act.wait_ge(places_done, n + 1)
                reached(act, place_ready, n)
                nc.scalar.activation(distance[:], ps_place[:], ACT.Abs, bias=c["minus_place"][:, 0:1]).then_inc(distance_ready, 1)

            def make_place(n, q):
                act.wait_ge(distance_ready, n + 1)
                reached(act, u_done, n - 1)
                reached(act, rows_done, n - 1)
                nc.scalar.activation(place[q][:], distance[:], ACT.Relu, bias=c["one"][:, 0:1], scale=-1.0).then_inc(place_ready, 1)

            def turn(it, n, j):
                o = 1 - j % 2
                if is_unit(n - 3):
                    act.wait_ge(sums_done, n - 2)
                    unit_scattered(act, n - 7)
                    k = (j + 1) % 4
                    nc.scalar.activation(sums[k][:, 0:3, :], ps_sum[:, 0, 0:3 * SW].rearrange("p (t x) -> p t x", t=3), ACT.Copy)
                    nc.scalar.activation(sums[k][:, 3, :], ps_sum[:, 1, 0:SW], ACT.Copy).then_inc(sums_ready, 1)
                if is_unit(n + 1):
                    measure(n + 1)
                if is_unit(n - 1):
                    act.wait_ge(clipped, n)
                    reached(act, rows_scored, n - 2)
                    nc.scalar.activation(score[o][:], zc[o][:], ACT.Exp).then_inc(scored, 1)
                    act.wait_ge(scored, n)
                    reached(act, sums_done, n - 2)
                    for t in range(UNIT):
                        last = nc.scalar.activation(scored_rows[o][:, t, :], tile_at(ps_rows, t, PW, 3)[:, 0:SW], ACT.Copy,
                                                    scale=score[o][:, t:t + 1])
                    last.then_inc(rows_scored, 1)
                if is_unit(n + 1):
                    make_place(n + 1, o)

            measure(0)
            make_place(0, 0)
            over_turns(act, turn)


def convolve(nc, c, e, attr, w1, b1, w2, b2, h1, aggT):
    with ExitStack() as ctx:
        one = lambda n, s, d=FP32: ctx.enter_context(nc.sbuf_tensor("co_" + n, s, d))
        two = lambda n, s, d=FP32: [one(f"{n}{q}", s, d) for q in range(2)]
        sem = lambda n: ctx.enter_context(nc.semaphore("co_" + n))
        psum = lambda n: ctx.enter_context(nc.psum_tensor("co_" + n, [P, UNIT, P], FP32))
        w1_half = two("w1_half", [P, D])
        w2_sb, b1_sb = one("w2_sb", [P, D]), one("b1_sb", [P, 1])
        b2_row, rest, ones = one("b2_row", [1, D]), one("rest", [1, D]), one("ones", [P, P], BF16)
        b2_cut, b2_parts = one("b2_cut", [1, 3, D], BF16), one("b2_parts", [P, D], BF16)
        src_i, out_f = two("src_i", [P, TS], I32), two("out_f", [P, TS, 2])
        h_src, at = two("h_src", [P, TS, P]), two("at", [P, UNIT * P])
        hid, msg = two("hid", [P, UNIT, P]), two("msg", [P, UNIT, P])
        share = [one(f"share{j}", [P, UNIT, WIN]) for j in range(4)]
        ps_hid, ps_agg = [psum(f"ps_hid{q}") for q in range(2)], [psum(f"ps_agg{q}") for q in range(2)]
        ps_f = [psum(f"ps_f{j}") for j in range(4)]
        weights_in, w1_in, halves_set, b2_cut_ready, b2_moved, pre = (
            sem(n) for n in ("weights_in", "w1_in", "halves_set", "b2_cut_ready", "b2_moved", "dve_pre"))
        attr_in, gathered = [sem(f"attr_in{q}") for q in range(2)], [sem(f"gathered{j}") for j in range(4)]
        ids_ready, hid_done, hid_ready, filtered, share_ready, msg_ready, summed, added = (
            sem(n) for n in ("ids_ready", "hid_done", "hid_ready", "filtered", "share_ready", "msg_ready", "summed", "added"))
        block = ctx.enter_context(nc.Block())
        TURNS = STEPS // 2
        UNITS = TURNS * 4

        @block.sync
        def _(sp):
            for tile, array in ((b2_row[:], b2), (w2_sb[:], w2), (b1_sb[:], b1)):
                sp.dma_start(tile, array).then_inc(weights_in, 16)
            sp.wait_ge(halves_set, 1)
            for half in range(2):
                rows = slice(half * RBF_ROWS, half * RBF_ROWS + RBF_ROWS)
                sp.dma_start(w1_half[half][rows, :], w1[rows, :]).then_inc(w1_in, 16)

            def load(it, q):
                sp.dma_start(at[q][:], attr[bass.ds((it * 2 + q) * P, P), :]).then_inc(attr_in[q], 16)
            for q in range(2):
                load(0, q)
            sp.wait_ge(b2_cut_ready, 1)
            for k in range(3):
                sp.dma_start(b2_parts[k:k + 1, :], b2_cut[:, k, :]).then_inc(b2_moved, 16)
            with sp.Fori(1, TURNS) as it:
                for q in range(2):
                    sp.wait_ge(hid_done, it * 4 + 2 * q - 2)
                    load(it, q)

        @block.gpsimd
        def _(pool):
            def turn(it, first):
                for q in range(2):
                    gate(pool, c, ids_ready, it * 2 + q + 1)
                    if not first:
                        gate(pool, c, msg_ready, it * 4 + 2 * q - 2)
                    for t in range(TS):
                        pool.indirect_dma_start(h_src[q][:, t, :], None, h1[:, :],
                                                bass.IndirectOffsetOnAxis(src_i[q][:, t:t + 1], 0)
                                                ).then_inc(gathered[2 * q + t // UNIT], 16)
            turn(0, True)
            with pool.Fori(1, TURNS) as it:
                turn(it, False)

        @block.vector
        def _(dve):
            def take(step, q):
                nc.vector.tensor_copy(out_f[q][:], e["out_f"][:, bass.ds(step * TS, TS), :])
                nc.vector.tensor_copy(src_i[q][:], e["src_i"][:, bass.ds(step * TS, TS)]).then_inc(ids_ready, 1)

            def shares(n, j, new_step):
                reached(dve, summed, n - 3)
                if new_step is not None:
                    dve.wait_ge(ids_ready, new_step + 1)
                for t in range(UNIT):
                    of_edge = out_f[j // 2][:, (j % 2) * UNIT + t, :]
                    last = nc.vector.tensor_scalar(share[j][:, t, :], c["win_no"][:], of_edge[:, 0:1], of_edge[:, 1:2],
                                                   ALU.is_equal, ALU.mult)
                last.then_inc(share_ready, 1)

            def add(step, q):
                base = dve.value_load(e["base_row"][0:1, bass.ds(step, 1)], min_val=0, max_val=NODES_P - WIN)
                dve.wait_ge(summed, step * 2 + 2)
                dve.wait_ge(added, step + 1)
                nc.vector.tensor_tensor(aggT[:, bass.ds(base, WIN)], aggT[:, bass.ds(base, WIN)], ps_agg[q][:, 0, 0:WIN],
                                        ALU.add).then_inc(added, 1)

            nc.vector.memset(w1_half[0][:], 0.0)
            nc.vector.memset(w1_half[1][:], 0.0).then_inc(halves_set, 1)
            nc.vector.memset(ones[:], 1.0)
            nc.vector.memset(b2_parts[:], 0.0).then_inc(pre, 1)
            nc.vector.memset(aggT[:], 0.0).then_inc(added, 1)
            dve.wait_ge(weights_in, 48)
            nc.vector.tensor_copy(b2_cut[:, 0, :], b2_row[:]).then_inc(pre, 1)
            dve.wait_ge(pre, 2)
            nc.vector.tensor_tensor(rest[:], b2_row[:], b2_cut[:, 0, :], ALU.subtract).then_inc(pre, 1)
            dve.wait_ge(pre, 3)
            nc.vector.tensor_copy(b2_cut[:, 1, :], rest[:]).then_inc(pre, 1)
            dve.wait_ge(pre, 4)
            nc.vector.tensor_tensor(rest[:], rest[:], b2_cut[:, 1, :], ALU.subtract).then_inc(pre, 1)
            dve.wait_ge(pre, 5)
            nc.vector.tensor_copy(b2_cut[:, 2, :], rest[:]).then_inc(b2_cut_ready, 1)

            def turn(it, first, last_turn):
                for j in range(4):
                    n, r = it * 4 + j, j // 2
                    dve.wait_ge(filtered, n + 1)
                    dve.wait_ge(gathered[j], it * (16 * UNIT) + 16 * UNIT)
                    reached(dve, summed, n - 1)
                    nc.vector.tensor_tensor(msg[j % 2][:], ps_f[j][:], h_src[r][:, (j % 2) * UNIT:(j % 2 + 1) * UNIT],
                                            ALU.mult).then_inc(msg_ready, 1)
                    if not (last_turn and j == 3):
                        shares(n + 1, (j + 1) % 4, it * 2 + r + 1 if j % 2 else None)
                    if j % 2 == 0 and not (first and j == 0):
                        add(it * 2 + r - 1, 1 - r)
                    if j % 2 and not last_turn:
                        dve.wait_ge(share_ready, n + 1)
                        take(it * 2 + r + 2, r)

            take(0, 0)
            take(1, 1)
            shares(0, 0, 0)
            turn(0, True, False)
            with dve.Fori(1, TURNS - 1) as it:
                turn(it, False, False)
            turn(TURNS - 1, False, True)
            add(STEPS - 1, 1)

        @block.tensor
        def _(pe):
            def hidden(n, j, loads):
                if j % 2 == 0:
                    pe.wait_ge(attr_in[j // 2], loads * 16)
                reached(pe, hid_ready, n - 1)
                nc.tensor.matmul(ps_hid[j % 2][:].rearrange("p t x -> p (t x)"), w1_half[j % 2][:], at[j // 2][:],
                                 start=True, stop=True).then_inc(hid_done, 1)

            def filters(n, j):
                pe.wait_ge(hid_ready, n + 1)
                reached(pe, msg_ready, n - 3)
                for t in range(UNIT):
                    nc.tensor.matmul(ps_f[j][:, t, :], ones[:], b2_parts[:], start=True, stop=False)
                    last = nc.tensor.matmul(ps_f[j][:, t, :], hid[j % 2][:, t, :], w2_sb[:], start=False, stop=True)
                last.then_inc(filtered, 1)

            def turn(it, first, last_turn):
                for j in range(4):
                    n, r = it * 4 + j, j // 2
                    if not (last_turn and j >= 2):
                        hidden(n + 2, (j + 2) % 4, it + (1 if j < 2 else 2))
                    if not (last_turn and j == 3):
                        filters(n + 1, (j + 1) % 4)
                    pe.wait_ge(msg_ready, n + 1)
                    pe.wait_ge(share_ready, n + 1)
                    if j % 2 == 0 and not first:
                        pe.wait_ge(added, it * 2 + r)
                    for t in range(UNIT):
                        last = nc.tensor.matmul(ps_agg[r][:, 0, 0:WIN], msg[j % 2][:, t, :], share[j][:, t, :],
                                                start=j % 2 == 0 and t == 0, stop=j % 2 == 1 and t == UNIT - 1)
                    last.then_inc(summed, 1)

            pe.wait_ge(w1_in, 32)
            hidden(0, 0, 1)
            hidden(1, 1, 1)
            pe.wait_ge(b2_moved, 48)
            filters(0, 0)
            turn(0, True, False)
            with pe.Fori(1, TURNS - 1) as it:
                turn(it, False, False)
            turn(TURNS - 1, False, True)

        @block.scalar
        def _(act):
            act.wait_ge(weights_in, 48)

            def turn(it, first):
                for j in range(4):
                    n = it * 4 + j
                    act.wait_ge(hid_done, n + 1)
                    reached(act, filtered, n - 1)
                    nc.scalar.activation(hid[j % 2][:], ps_hid[j % 2][:], ACT.Tanh, bias=b1_sb[:, 0:1]).then_inc(hid_ready, 1)
            turn(0, True)
            with act.Fori(1, TURNS) as it:
                turn(it, False)


def collect_any(nc, c, tables, aggT):
    with ExitStack() as ctx:
        part = ctx.enter_context(nc.sbuf_tensor("ca_part", [P, COPIES, NB, D], FP32))
        ps_t = ctx.enter_context(nc.psum_tensor("ca_ps_t", [P, 8, P], FP32))
        loaded, halves, added, turned, taken = (ctx.enter_context(nc.semaphore("ca_" + n))
                                                for n in ("loaded", "halves", "added", "turned", "taken"))
        block = ctx.enter_context(nc.Block())

        @block.sync
        def _(sp):
            with sp.Fori(0, NODE_STEPS) as it:
                sp.wait_ge(turned, it)
                for k in range(COPIES):
                    sp.dma_start(part[:, k], node_rows(tables[k], it, D)).then_inc(loaded, 16)

        @block.vector
        def _(dve):
            with dve.Fori(0, NODE_STEPS) as it:
                dve.wait_ge(loaded, it * (16 * COPIES) + 16 * COPIES)
                nc.vector.tensor_tensor(part[:, 0], part[:, 0], part[:, 1], ALU.add)
                nc.vector.tensor_tensor(part[:, 2], part[:, 2], part[:, 3], ALU.add).then_inc(halves, 1)
                dve.wait_ge(halves, it + 1)
                nc.vector.tensor_tensor(part[:, 0], part[:, 0], part[:, 2], ALU.add).then_inc(added, 1)

        @block.tensor
        def _(pe):
            with pe.Fori(0, NODE_STEPS) as it:
                pe.wait_ge(added, it + 1)
                pe.wait_ge(taken, it)
                for b in range(NB):
                    last = nc.tensor.transpose(ps_t[:, b, :], part[:, 0, b], c["ident"][:])
                last.then_inc(turned, 1)

        @block.scalar
        def _(act):
            with act.Fori(0, NODE_STEPS) as it:
                act.wait_ge(turned, it + 1)
                for b0, b1 in ((0, 4), (4, NB)):
                    last = nc.scalar.activation(aggT[:, bass.ds(it * (NB * P) + b0 * P, (b1 - b0) * P)],
                                                ps_t[:, b0:b1].rearrange("p b x -> p (b x)"), ACT.Copy)
                last.then_inc(taken, 1)


def finish_nodes(nc, c, aggT, x1, w_out, b_out, w_lin, b_lin, out):
    with ExitStack() as ctx:
        one = lambda n, s, d=FP32: ctx.enter_context(nc.sbuf_tensor("n1_" + n, s, d))
        two = lambda n, s, d=FP32: [one(f"{n}{q}", s, d) for q in range(2)]
        sem = lambda n: ctx.enter_context(nc.semaphore("n1_" + n))
        wo, wl, bo, bl = one("wo", [P, D]), one("wl", [P, D]), one("bo", [P, 1]), one("bl", [P, D])
        xs, hidT = two("xs", [P, NB, D]), two("hidT", [P, NB, D])
        y_step, y = two("y_step", [P, NB, D]), one("y", [P, NODE_BLOCKS, D])
        stats = two("stats", [P, NB, 6])
        mv_step = two("mv_step", [P, NB, 2])
        mv = one("mv", [P, NODE_BLOCKS, 2])
        std, rstd, shift = (one(n, [P, NODE_BLOCKS]) for n in ("std", "rstd", "shift"))
        ps_h = ctx.enter_context(nc.psum_tensor("n1_ps_h", [P, 8, P], FP32))
        ps_o = ctx.enter_context(nc.psum_tensor("n1_ps_o", [P, 8, P], FP32))
        loaded = [sem(f"loaded{q}") for q in range(2)]
        w_in, shifted, h_done, h_ready, o_done, y_ready, y_kept, stats_ready, mv_ready, mv_kept = (
            sem(n) for n in ("w_in", "shifted", "h_done", "h_ready", "o_done", "y_ready", "y_kept", "stats_ready", "mv_ready",
                             "mv_kept"))
        std_ready, scales_ready, dve_out, act_out, stored = (
            sem(n) for n in ("std_ready", "scales_ready", "dve_out", "act_out", "stored"))
        block = ctx.enter_context(nc.Block())
        HALF = NODE_STEPS // 2
        OF_DVE = 4
        BANKS = (slice(0, 4), slice(4, NB))

        @block.sync
        def _(sp):
            for tile, array in ((wo[:], w_out), (wl[:], w_lin), (bo[:], b_out), (bl[:], b_lin.to_broadcast([P, D]))):
                sp.dma_start(tile, array).then_inc(w_in, 16)

            def load(n, q):
                sp.dma_start(xs[q][:], node_rows(x1, n, D)).then_inc(loaded[q], 16)
            for q in range(2):
                load(q, q)
            with sp.Fori(1, HALF) as it:
                for q in range(2):
                    sp.wait_ge(y_ready, it * 2 + q - 1)
                    load(it * 2 + q, q)
            for n in range(NODE_STEPS):
                sp.wait_ge(dve_out, n + 1)
                sp.wait_ge(act_out, n + 1)
                sp.dma_start(node_rows(out, n, D), y[:, n * NB:(n + 1) * NB]).then_inc(stored, 16)
            sp.wait_ge(stored, 16 * NODE_STEPS)

        @block.gpsimd
        def _(pool):
            pool.wait_ge(w_in, 64)
            with pool.Fori(0, HALF) as it:
                for q in range(2):
                    pool.wait_ge(loaded[q], it * 16 + 16)
                    pool.tensor_tensor(xs[q][:], xs[q][:], bl[:].unsqueeze(1).to_broadcast([P, NB, D]), ALU.add
                                       ).then_inc(shifted, 1)

        @block.vector
        def _(dve):
            def rows(it):
                for q in range(2):
                    n = it * 2 + q
                    dve.wait_ge(shifted, n + 1)
                    dve.wait_ge(o_done, n + 1)
                    reached(dve, y_kept, n - 1)
                    for b in BANKS:
                        last = nc.vector.tensor_tensor(y_step[q][:, b], ps_o[:, b], xs[q][:, b], ALU.add)
                    last.then_inc(y_ready, 1)
                    dve.wait_ge(y_ready, n + 1)
                    for b in range(NB):
                        last = nc.vector.bn_stats(stats[q][:, b], y_step[q][:, b])
                    last.then_inc(stats_ready, 1)
                    dve.wait_ge(stats_ready, n + 1)
                    dve.sem_inc(c["gates_passed"], 1)
                    for b in range(NB):
                        last = nc.vector.bn_aggr(mv_step[q][:, b], stats[q][:, b])
                    last.then_inc(mv_ready, 1)
                    dve.wait_ge(mv_ready, n + 1)
                    nc.vector.tensor_copy(mv[:, bass.ds(n * NB, NB), :], mv_step[q][:]).then_inc(mv_kept, 1)

            rows(0)
            with dve.Fori(1, HALF) as it:
                rows(it)
            dve.wait_ge(y_kept, NODE_STEPS)
            dve.wait_ge(std_ready, 1)
            nc.vector.reciprocal(rstd[:], std[:]).then_inc(scales_ready, 1)
            dve.wait_ge(scales_ready, 1)
            nc.vector.scalar_tensor_tensor(out=shift[:], in0=mv[:, :, 0], scalar=-1.0, in1=rstd[:], op0=ALU.mult,
                                           op1=ALU.mult).then_inc(scales_ready, 1)
            for n in range(NODE_STEPS):
                for b in range(n * NB, n * NB + OF_DVE):
                    last = nc.vector.tensor_scalar(y[:, b], y[:, b], mv[:, b, 0:1], rstd[:, b:b + 1],
                                                   ALU.subtract, ALU.mult)
                last.then_inc(dve_out, 1)

        @block.tensor
        def _(pe):
            pe.wait_ge(w_in, 64)

            def hidden(n):
                for b in BANKS:
                    last = nc.tensor.matmul(ps_h[:, b, :].rearrange("p b c -> p (b c)"), wo[:],
                                            aggT[:, bass.ds(n * (NB * P) + b.start * P, (b.stop - b.start) * P)],
                                            start=True, stop=True)
                last.then_inc(h_done, 1)

            def outputs(n, q):
                pe.wait_ge(h_ready, n + 1)
                reached(pe, y_ready, n)
                for b in range(NB):
                    last = nc.tensor.matmul(ps_o[:, b, :], hidT[q][:, b], wl[:], start=True, stop=True)
                last.then_inc(o_done, 1)

            hidden(0)
            outputs(0, 0)
            pe.wait_ge(h_ready, 1)
            hidden(1)
            outputs(1, 1)
            with pe.Fori(1, HALF) as it:
                for q in range(2):
                    pe.wait_ge(h_ready, it * 2 + q)
                    hidden(it * 2 + q)
                    outputs(it * 2 + q, q)

        @block.scalar
        def _(act):
            act.wait_ge(w_in, 64)

            def tanh(n, q):
                act.wait_ge(h_done, n + 1)
                reached(act, o_done, n - 1)
                for b in BANKS:
                    last = nc.scalar.activation(hidT[q][:, b], ps_h[:, b], ACT.Tanh, bias=bo[:, 0:1])
                last.then_inc(h_ready, 1)

            def keep(n, q):
                act.wait_ge(y_ready, n + 1)
                nc.scalar.activation(y[:, bass.ds(n * NB, NB), :], y_step[q][:], ACT.Copy).then_inc(y_kept, 1)
            tanh(0, 0)
            tanh(1, 1)
            keep(0, 0)
            with act.Fori(1, HALF) as it:
                for q in range(2):
                    tanh(it * 2 + q, q)
                    keep(it * 2 + q - 1, 1 - q)
            keep(NODE_STEPS - 1, 1)
            act.wait_ge(y_kept, NODE_STEPS)
            act.wait_ge(mv_kept, NODE_STEPS)
            nc.scalar.activation(std[:], mv[:, :, 1], ACT.Sqrt, bias=c["eps"][:, 0:1]).then_inc(std_ready, 1)
            act.wait_ge(scales_ready, 2)
            for n in range(NODE_STEPS):
                for b in range(n * NB + OF_DVE, (n + 1) * NB):
                    last = nc.scalar.activation(y[:, b], y[:, b], ACT.Identity, bias=shift[:, b:b + 1], scale=rstd[:, b:b + 1])
                last.then_inc(act_out, 1)


def network(nc, x, xT, src, dst, dst_steps, weight, attr, kernel, kernelT, att, w1, b1, w2, b2, w_in, w_out, b_out,
            w_lin, b_lin, out):
    dram = lambda n, rows, cols: nc.dram_tensor(n, [rows, cols], FP32, kind="Internal")
    hv = dram("hv", NODES_P, HW)
    x1, h1 = dram("x1", NODES_P, D), dram("h1", NODES_P, D)
    parts_d = nc.dram_tensor("parts_d", [NODES_P, 3 * PW], BF16, kind="Internal")
    base_d = nc.dram_tensor("base_d", [STEPS], I32, kind="Internal")
    sums0 = [dram(f"sums0_{k}", ROWS, SW) for k in range(COPIES)]
    sums1 = [dram(f"sums1_{k}", ROWS, D) for k in range(COPIES)]
    with ExitStack() as ctx:
        tile = lambda within, n, s, d=FP32: within.enter_context(nc.sbuf_tensor(n, s, d))
        c = constants(nc, ctx)
        landed0 = [ctx.enter_context(nc.semaphore(f"landed0_{k}")) for k in range(COPIES)]
        e = {"src_i": tile(ctx, "src_i", [P, TILES], I32), "base_d": base_d,
             "out_f": tile(ctx, "out_f", [P, TILES, 2]),
             "base_row": tile(ctx, "base_row", [1, STEPS], I32), "fits": tile(ctx, "fits", [1, 1], I32)}
        with ExitStack() as first:
            e["key_f"] = tile(first, "key_f", [P, TILES, 3])
            e["key_b"] = tile(first, "key_b", [P, TILES, 3], BF16)
            number_edges(nc, c, src, dst, dst_steps, weight, e)
            fits = nc.values_load(e["fits"][0:1, 0:1], min_val=0, max_val=1)
            free = nc.snapshot_sems()
            with nc.If(fits == 1):
                with nc.sbuf_tensor("u_parts", [P, 3, HALF_BLOCKS], BF16) as u_parts:
                    project_parts(nc, c, xT, kernel, kernelT, att, parts_d, u_parts, sums0, landed0)
                    attend(nc, c, e, u_parts, parts_d, sums0, landed0)
            nc.restore_sems(free)
            with nc.Else():
                zero_tables(nc, sums0, SW, landed0)
                project_nodes(nc, c, xT, kernel, kernelT, att, hv)
                attend_any(nc, c, src, dst, hv, sums0, landed0)
        update_nodes(nc, c, x, sums0, w_in, x1, h1)
        aggT = tile(ctx, "aggT", [P, NODES_P])
        fits = nc.values_load(e["fits"][0:1, 0:1], min_val=0, max_val=1)
        free = nc.snapshot_sems()
        with nc.If(fits == 1):
            convolve(nc, c, e, attr, w1, b1, w2, b2, h1, aggT)
        nc.restore_sems(free)
        with nc.Else():
            landed1 = [ctx.enter_context(nc.semaphore(f"landed1_{k}")) for k in range(COPIES)]
            zero_tables(nc, sums1, D, landed1)
            convolve_any(nc, c, e["src_i"], dst, weight, attr, w1, b1, w2, b2, h1, sums1, landed1)
            collect_any(nc, c, sums1, aggT)
        finish_nodes(nc, c, aggT, x1, w_out, b_out, w_lin, b_lin, out)


def kernel(x, src, dst, edge_attr_50, edge_weight, L0_gnn_kernel, L0_gnn_kernel_attention, L1_gnn_W_f1, L1_gnn_b_f1,
           L1_gnn_W_f2, L1_gnn_b_f2, L1_gnn_W_in, L1_gnn_W_out, L1_gnn_b_out, L1_gnn_W_lin, L1_gnn_b_lin):
    import numpy as np
    import concourse.bacc as bacc
    from concourse.bass_utils import run_bass_kernel_spmd as run

    def padded(a, n, value=0):
        a = np.asarray(a)
        return np.concatenate([a, np.full((n - a.shape[0],) + a.shape[1:], value, a.dtype)])

    def by_tile(a, value):
        return np.ascontiguousarray(padded(a, EDGES_P, value).reshape(TILES, P).T)

    xp = padded(x, NODES_P)
    attr = padded(edge_attr_50, EDGES_P).reshape(STEPS, 2, TS * P // 2, RBF).transpose(0, 1, 3, 2)
    attr = np.concatenate([attr, np.zeros((STEPS, 2, RBF_ROWS - RBF, TS * P // 2), attr.dtype)], axis=2)
    w1 = padded(L1_gnn_W_f1, RBF_ROWS)
    arrays = {
        "x": xp, "xT": xp.T,
        "src": by_tile(src, N_NODES), "dst": by_tile(dst, N_NODES), "weight": by_tile(edge_weight, 0),
        "dst_steps": padded(dst, EDGES_P, N_NODES).reshape(STEPS // 4, 4, TS * P),
        "attr": attr.reshape(STEPS * P, TS * P // 2),
        "kernel": L0_gnn_kernel, "kernelT": np.asarray(L0_gnn_kernel).T,
        "att": np.asarray(L0_gnn_kernel_attention).reshape(2, D).T,
        "w1": np.concatenate([w1, w1]), "b1": np.asarray(L1_gnn_b_f1).reshape(D, 1),
        "w2": L1_gnn_W_f2, "b2": np.asarray(L1_gnn_b_f2).reshape(1, D), "w_in": L1_gnn_W_in,
        "w_out": L1_gnn_W_out, "b_out": np.asarray(L1_gnn_b_out).reshape(D, 1),
        "w_lin": L1_gnn_W_lin, "b_lin": np.asarray(L1_gnn_b_lin).reshape(1, D),
    }
    arrays = {k: np.ascontiguousarray(v) for k, v in arrays.items()}
    nc = bacc.Bacc("TRN2", target_bir_lowering=False, num_devices=1)
    aps = {k: nc.dram_tensor(f"in_{k}", v.shape, mybir.dt.from_np(v.dtype), kind="ExternalInput").ap() for k, v in arrays.items()}
    out = nc.dram_tensor("out", (NODES_P, D), FP32, kind="ExternalOutput").ap()
    network(nc, out=out, **aps)
    return run(nc, [{f"in_{k}": v for k, v in arrays.items()}], core_ids=[0]).results[0]["out"][:N_NODES]
```
